# Optimizing a Trainium2 kernel written in Bass

```python
import numpy as np
import jax
import jax.numpy as jnp

def _softmax(x, axis=-1):
    return jax.nn.softmax(x, axis=axis)

def _gelu(x):
    return jax.nn.gelu(x, approximate=True)

def _silu(x):
    return jax.nn.silu(x)

def _sigmoid(x):
    return jax.nn.sigmoid(x)

def _layernorm(x, axis=-1, eps=1e-05):
    m = jnp.mean(x, axis=axis, keepdims=True)
    v = jnp.var(x, axis=axis, keepdims=True)
    return (x - m) / jnp.sqrt(v + eps)

def _scatter_add(tgt, idx, src, axis=0):
    return tgt.at[idx].add(src)

def _segment_sum(src, seg, n):
    return jax.ops.segment_sum(src, seg, n)
kernel_name = 'mk_gnn_preln_d2_gnn_r32_7ccac9'

def setup_inputs(seed: int=0):
    np.random.seed(seed)
    _w = jnp.asarray

    def _rec_inputs():
        import jax
        import jax.numpy as jnp
        _gk = jax.random.key(seed)
        x = -8.776e-05 + 1 * jax.random.normal(jax.random.fold_in(_gk, 1), (3125, 256), jnp.float32)
        src = jax.random.randint(jax.random.fold_in(_gk, 2), (50000,), 0, 3125, jnp.int32)
        dst = jax.random.randint(jax.random.fold_in(_gk, 3), (50000,), 0, 3125, jnp.int32)
        _o = jnp.argsort(dst, stable=True)
        src = src[_o]
        dst = dst[_o]
        edge_attr_64 = 0.000279952 + 1.00013 * jax.random.normal(jax.random.fold_in(_gk, 11), (50000, 64), jnp.float32)
        edge_type_3 = jax.random.randint(jax.random.fold_in(_gk, 14), (50000,), 0, 3, jnp.int32)
        return (x, src, dst, edge_attr_64, edge_type_3)
    x, src, dst, edge_attr_64, edge_type_3 = _rec_inputs()

    def _L0_gnn_setup():
        import jax, jax.numpy as jnp
        import numpy as np
        N, E, H, ED = (625, 10000, 256, 64)
        key = jax.random.key(seed)
        ks = jax.random.split(key, 12)

        def init_w(k, shape, fan_in):
            return (jax.random.normal(k, shape, jnp.float32) / np.sqrt(fan_in)).astype(jnp.float32)
        h = jax.random.normal(ks[0], (N, H), jnp.float32)
        edge_indices = jax.random.randint(ks[1], (2, E), 0, N, jnp.int32)
        edge_attr = jax.random.normal(ks[2], (E, ED), jnp.float32)
        din = 2 * H + ED
        W1 = init_w(ks[3], (H, din), din)
        b1 = jnp.zeros((H,), jnp.float32)
        W2 = init_w(ks[4], (H, H), H)
        b2 = jnp.zeros((H,), jnp.float32)
        W_ih = init_w(ks[5], (3 * H, H), H)
        b_ih = jnp.zeros((3 * H,), jnp.float32)
        W_hh = init_w(ks[6], (3 * H, H), H)
        b_hh = jnp.zeros((3 * H,), jnp.float32)
        return {'h': h, 'edge_indices': edge_indices, 'edge_attr': edge_attr, 'W1': W1, 'b1': b1, 'W2': W2, 'b2': b2, 'W_ih': W_ih, 'b_ih': b_ih, 'W_hh': W_hh, 'b_hh': b_hh}
    _L0_gnn_all = _L0_gnn_setup()
    _L0_gnn_in = {k: v for k, v in _L0_gnn_all.items() if k in ('W1', 'b1', 'W2', 'b2', 'W_ih', 'b_ih', 'W_hh', 'b_hh')}
    del _L0_gnn_all

    def _L1_gnn_setup():
        import jax, jax.numpy as jnp
        import numpy as np
        H = 4
        DH = 64
        HID = 256
        EPS = 1e-05
        N_NODES = 625
        N_EDGES = 10000
        N_LAYERS = 3

        def _layer_norm(x, g, b):
            mu = jnp.mean(x, axis=-1, keepdims=True)
            var = jnp.mean((x - mu) ** 2, axis=-1, keepdims=True)
            return (x - mu) * jax.lax.rsqrt(var + EPS) * g + b

        def _message_passing(h, src, tgt, et, Wq, bq, Wk, bk, Wv, bv, Ee, Wo, bo, n_nodes):
            Q = (h @ Wq.T + bq).reshape(-1, H, DH)
            K = (h @ Wk.T + bk).reshape(-1, H, DH)
            V = (h @ Wv.T + bv).reshape(-1, H, DH)
            scores = jnp.einsum('ehd,egd->ehg', Q[src], K[tgt]) / jnp.sqrt(jnp.float32(DH))
            attn = jax.nn.softmax(scores, axis=-1)
            msg = jnp.einsum('ehg,egd->ehd', attn, V[tgt]).reshape(-1, HID)
            msg = msg + Ee[et]
            proj = msg @ Wo.T + bo
            return jax.ops.segment_sum(proj, src, num_segments=n_nodes)
        key = jax.random.key(seed)
        ks = jax.random.split(key, 16)

        def w(k, shape, s=0.05):
            return jax.random.normal(k, shape, jnp.float32) * s
        return {'x': jax.random.normal(ks[0], (N_NODES, HID), jnp.float32), 'edges': jax.random.randint(ks[1], (N_EDGES, 2), 0, N_NODES), 'edge_types': jax.random.randint(ks[2], (N_EDGES,), 0, 3), 'Win': w(ks[3], (HID, HID)), 'b_in': jnp.zeros((HID,), jnp.float32), 'Wq': w(ks[4], (N_LAYERS, HID, HID)), 'bq': jnp.zeros((N_LAYERS, HID), jnp.float32), 'Wk': w(ks[5], (N_LAYERS, HID, HID)), 'bk': jnp.zeros((N_LAYERS, HID), jnp.float32), 'Wv': w(ks[6], (N_LAYERS, HID, HID)), 'bv': jnp.zeros((N_LAYERS, HID), jnp.float32), 'Eemb': w(ks[7], (N_LAYERS, 3, HID)), 'Wo': w(ks[8], (N_LAYERS, HID, HID)), 'bo': jnp.zeros((N_LAYERS, HID), jnp.float32), 'ln_g': jnp.ones((N_LAYERS, HID), jnp.float32), 'ln_b': jnp.zeros((N_LAYERS, HID), jnp.float32), 'W1': w(ks[9], (HID, HID)), 'b1': jnp.zeros((HID,), jnp.float32), 'W2': w(ks[10], (HID, HID)), 'b2': jnp.zeros((HID,), jnp.float32)}
    _L1_gnn_all = _L1_gnn_setup()
    _L1_gnn_in = {k: v for k, v in _L1_gnn_all.items() if k in ('Win', 'b_in', 'Wq', 'bq', 'Wk', 'bk', 'Wv', 'bv', 'Eemb', 'Wo', 'bo', 'ln_g', 'ln_b', 'W1', 'b1', 'W2', 'b2')}
    del _L1_gnn_all
    return {'x': x, 'src': src, 'dst': dst, 'edge_attr_64': edge_attr_64, 'edge_type_3': edge_type_3, 'L0_gnn_W1': _L0_gnn_in['W1'], 'L0_gnn_b1': _L0_gnn_in['b1'], 'L0_gnn_W2': _L0_gnn_in['W2'], 'L0_gnn_b2': _L0_gnn_in['b2'], 'L0_gnn_W_ih': _L0_gnn_in['W_ih'], 'L0_gnn_b_ih': _L0_gnn_in['b_ih'], 'L0_gnn_W_hh': _L0_gnn_in['W_hh'], 'L0_gnn_b_hh': _L0_gnn_in['b_hh'], 'L1_gnn_Win': _L1_gnn_in['Win'], 'L1_gnn_b_in': _L1_gnn_in['b_in'], 'L1_gnn_Wq': _L1_gnn_in['Wq'], 'L1_gnn_bq': _L1_gnn_in['bq'], 'L1_gnn_Wk': _L1_gnn_in['Wk'], 'L1_gnn_bk': _L1_gnn_in['bk'], 'L1_gnn_Wv': _L1_gnn_in['Wv'], 'L1_gnn_bv': _L1_gnn_in['bv'], 'L1_gnn_Eemb': _L1_gnn_in['Eemb'], 'L1_gnn_Wo': _L1_gnn_in['Wo'], 'L1_gnn_bo': _L1_gnn_in['bo'], 'L1_gnn_ln_g': _L1_gnn_in['ln_g'], 'L1_gnn_ln_b': _L1_gnn_in['ln_b'], 'L1_gnn_W1': _L1_gnn_in['W1'], 'L1_gnn_b1': _L1_gnn_in['b1'], 'L1_gnn_W2': _L1_gnn_in['W2'], 'L1_gnn_b2': _L1_gnn_in['b2']}

def reference(x, src, dst, edge_attr_64, edge_type_3, L0_gnn_W1, L0_gnn_b1, L0_gnn_W2, L0_gnn_b2, L0_gnn_W_ih, L0_gnn_b_ih, L0_gnn_W_hh, L0_gnn_b_hh, L1_gnn_Win, L1_gnn_b_in, L1_gnn_Wq, L1_gnn_bq, L1_gnn_Wk, L1_gnn_bk, L1_gnn_Wv, L1_gnn_bv, L1_gnn_Eemb, L1_gnn_Wo, L1_gnn_bo, L1_gnn_ln_g, L1_gnn_ln_b, L1_gnn_W1, L1_gnn_b1, L1_gnn_W2, L1_gnn_b2):
    import jax
    import jax.numpy as jnp

    def _L0_gnn_ref(h, edge_indices, edge_attr, W1, b1, W2, b2, W_ih, b_ih, W_hh, b_hh):
        import jax, jax.numpy as jnp
        import numpy as np
        N, E, H, ED = (625, 10000, 256, 64)
        row, col = (edge_indices[0], edge_indices[1])
        edge_in = jnp.concatenate([h[row], h[col], edge_attr], axis=-1)
        msg = jax.nn.relu(edge_in @ W1.T + b1) @ W2.T + b2
        agg = jax.ops.segment_sum(msg, row, num_segments=h.shape[0])
        gx = agg @ W_ih.T + b_ih
        gh = h @ W_hh.T + b_hh
        xr, xz, xn = jnp.split(gx, 3, axis=-1)
        hr, hz, hn = jnp.split(gh, 3, axis=-1)
        r = jax.nn.sigmoid(xr + hr)
        z = jax.nn.sigmoid(xz + hz)
        n = jnp.tanh(xn + r * hn)
        h_new = (1.0 - z) * n + z * h
        return h_new

    def _L1_gnn_ref(x, edges, edge_types, Win, b_in, Wq, bq, Wk, bk, Wv, bv, Eemb, Wo, bo, ln_g, ln_b, W1, b1, W2, b2):
        import jax, jax.numpy as jnp
        import numpy as np
        H = 4
        DH = 64
        HID = 256
        EPS = 1e-05
        N_NODES = 625
        N_EDGES = 10000
        N_LAYERS = 3

        def _layer_norm(x, g, b):
            mu = jnp.mean(x, axis=-1, keepdims=True)
            var = jnp.mean((x - mu) ** 2, axis=-1, keepdims=True)
            return (x - mu) * jax.lax.rsqrt(var + EPS) * g + b

        def _message_passing(h, src, tgt, et, Wq, bq, Wk, bk, Wv, bv, Ee, Wo, bo, n_nodes):
            Q = (h @ Wq.T + bq).reshape(-1, H, DH)
            K = (h @ Wk.T + bk).reshape(-1, H, DH)
            V = (h @ Wv.T + bv).reshape(-1, H, DH)
            scores = jnp.einsum('ehd,egd->ehg', Q[src], K[tgt]) / jnp.sqrt(jnp.float32(DH))
            attn = jax.nn.softmax(scores, axis=-1)
            msg = jnp.einsum('ehg,egd->ehd', attn, V[tgt]).reshape(-1, HID)
            msg = msg + Ee[et]
            proj = msg @ Wo.T + bo
            return jax.ops.segment_sum(proj, src, num_segments=n_nodes)
        n_nodes = x.shape[0]
        src, tgt = (edges[:, 0], edges[:, 1])
        hidden = x @ Win.T + b_in
        for l in range(N_LAYERS):
            m = _message_passing(hidden, src, tgt, edge_types, Wq[l], bq[l], Wk[l], bk[l], Wv[l], bv[l], Eemb[l], Wo[l], bo[l], n_nodes)
            hidden = jax.nn.relu(_layer_norm(hidden + m, ln_g[l], ln_b[l]))
        adjustment = jax.nn.relu(hidden @ W1.T + b1) @ W2.T + b2
        return x + adjustment
    edge_index = jnp.stack([src, dst])
    edge_index_t = jnp.stack([src, dst], axis=1)
    h = jnp.maximum(_layernorm(x, axis=-1), 0.0)
    x = x + _L0_gnn_ref(h, edge_index, edge_attr_64, L0_gnn_W1, L0_gnn_b1, L0_gnn_W2, L0_gnn_b2, L0_gnn_W_ih, L0_gnn_b_ih, L0_gnn_W_hh, L0_gnn_b_hh)
    h = jnp.maximum(_layernorm(x, axis=-1), 0.0)
    x = x + _L1_gnn_ref(h, edge_index_t, edge_type_3, L1_gnn_Win, L1_gnn_b_in, L1_gnn_Wq, L1_gnn_bq, L1_gnn_Wk, L1_gnn_bk, L1_gnn_Wv, L1_gnn_bv, L1_gnn_Eemb, L1_gnn_Wo, L1_gnn_bo, L1_gnn_ln_g, L1_gnn_ln_b, L1_gnn_W1, L1_gnn_b1, L1_gnn_W2, L1_gnn_b2)
    return x

_drawn_inputs = setup_inputs


def setup_inputs(seed=0):
    import zlib

    import numpy as np

    out = dict(_drawn_inputs(seed))
    spreads = {'L0_gnn_b1': (0.0, 0.1),
     'L0_gnn_b2': (0.0, 0.1),
     'L0_gnn_b_ih': (0.0, 0.575),
     'L0_gnn_b_hh': (0.0, 0.683),
     'L1_gnn_b_in': (0.0, 0.597),
     'L1_gnn_bq': (0.0, 0.8),
     'L1_gnn_bk': (0.0, 0.749),
     'L1_gnn_bv': (0.0, 0.1),
     'L1_gnn_bo': (0.0, 0.1),
     'L1_gnn_ln_g': (1.0, 0.2),
     'L1_gnn_ln_b': (0.0, 0.296),
     'L1_gnn_b1': (0.0, 0.332),
     'L1_gnn_b2': (0.0, 0.1)}
    factors = {}
    for name, (base, spread) in spreads.items():
        noise = np.random.default_rng([zlib.crc32(name.encode()), seed]).standard_normal(out[name].shape)
        drawn = base * np.exp(spread * noise) if base else spread * noise
        out[name] = jnp.asarray(drawn.astype(out[name].dtype))
    for name, factor in factors.items():
        out[name] = (out[name] * factor).astype(out[name].dtype)
    return out
```

```python
from contextlib import ExitStack

import concourse.bass as bass
from concourse import mybir

F32 = mybir.dt.float32
BF16 = mybir.dt.bfloat16
I32 = mybir.dt.int32
ALU = mybir.AluOpType
ACT = mybir.ActivationFunctionType
AX = mybir.AxisListType

P = 128
NODES, HID, EDGES, ATTR = 3125, 256, 50000, 64
HEADS, DH, LAYERS, TYPES = 4, 64, 3, 3
WIN = 32
BLOCKS = 26
NPAD = BLOCKS * P
NWIN = NPAD // WIN
WPB = P // WIN
RWIN = -(-NODES // WIN)
GT = 4
RING = 3
BODY = GT * RING
NEED = (EDGES + RWIN * (P - 1)) // P
ITERS = -(-NEED // BODY)
TILES = ITERS * BODY
GROUPS = TILES // GT
ROWS = TILES * P
COLS = 392
EPAD = P * COLS
CH = 7
CHUNKS = COLS // CH
QC = 56
NQ = COLS // QC
PARTS = QC // CH
WPP = NWIN // PARTS
REC = 128
R_OH, R_CNT, R_DST, R_END = 64, 96, 100, 101
PK = R_END - R_OH
FAR = 1 << 22
NEGB = -(2.0 ** 100)
B_PREP, B_E0, B_N1, B_N2, PER_LAYER = 1, 2, 3, 4, 4
EPS = 1e-5


def gnn(nc, a, out):
    ctx = ExitStack()
    with ctx:
        def sb(name, shape, dt=F32):
            return ctx.enter_context(nc.sbuf_tensor(name, shape, dt))

        def sem(name):
            return ctx.enter_context(nc.semaphore(name))

        def sems(name, n):
            return [sem(f"{name}{i}") for i in range(n)]

        def dram(name, shape, dt=F32):
            return nc.dram_tensor(name, shape, dt).ap()

        rect = dram("edge_records", (ROWS, REC))
        packd = dram("edge_packs", (GROUPS, P, GT * PK))
        maskd = dram("edge_masks", (GROUPS, WIN, GT * P), BF16)
        qrows = dram("dst_rows", (NPAD, HID))
        kvrows = dram("kv_rows", (NPAD, 2 * HID))
        h0d = dram("h0", (NPAD, HID))
        h0Td = dram("h0T", (NPAD, HID))
        x1d = dram("x1", (NPAD, HID))
        based = dram("base", (NPAD, HID))
        hidd = dram("hidden", (NPAD, HID))
        yd = dram("y", (NPAD, HID))
        cntd = dram("counts", (4, NPAD))

        big = sb("big", [P, NWIN, HID])
        accr = sb("accr", [P, NWIN * 96])
        ring = sb("ring", [P, BODY * 2 * HID])
        node = sb("node", [P, 6144])
        ident = sb("ident", [P, P])
        ones = sb("ones", [P, P])
        before = sb("before", [P, P])
        neg = sb("neg", [P, 4 * HEADS * WIN], BF16)
        wtab = sb("wtab", [P, TILES], I32)
        bst = sb("bst", [P, BLOCKS, 6])
        st4 = sb("st4", [P, 8, BLOCKS])
        rstd, nmr = st4[:, 0, :], st4[:, 1, :]
        banks = [ctx.enter_context(nc.psum_tensor(f"bank{i}", [P, 512], F32)) for i in range(8)]

        def at(region, off, *shape, parts=P):
            n = 1
            for d in shape:
                n *= d
            v = region[0:parts, off:off + n]
            if len(shape) == 2:
                v = v.rearrange("p (a b) -> p a b", a=shape[0])
            elif len(shape) == 3:
                v = v.rearrange("p (a b c) -> p a b c", a=shape[0], b=shape[1])
            return v

        phase_end, entered = sem("phase_end"), sem("entered")

        def events(phase, words):
            return {w: sem(f"{phase}_{w}") for w in words.split()}

        block = ctx.enter_context(nc.Block())

        def need(eng, s, i, base, count, peeled=0):
            if isinstance(i, int) and i == 0 and peeled + count <= 0:
                return
            eng.wait_ge(s, base + count)

        def hold(eng):
            eng.sem_inc(entered, 1)

        def barrier(eng, n):
            hold(eng)
            eng.drain().then_inc(phase_end, 1)
            eng.wait_ge(phase_end, n * 5)
            hold(eng)

        def layer_barrier(eng, l, k):
            barrier(eng, l * PER_LAYER + (B_N2 + k))

        def pairs(eng, body):
            body(0)
            with eng.Fori(1, BLOCKS // 2) as i:
                body(i)

        def bodies(eng, body):
            body(0)
            with eng.Fori(1, ITERS) as it:
                body(it)

        class Steps:

            def __init__(self, eng, s, n=0, per=0, base=0):
                self.eng, self.s, self.start, self.per, self.c = eng, s, n * per + base, per, 0

            def __call__(self, ins):
                ins.then_inc(self.s, 1)
                self.c += 1
                self.eng.wait_ge(self.s, self.start + self.c)

            def end(self):
                assert self.per in (0, self.c), (self.c, self.per)
                return self.c

        def rows(t, b, n=P):
            return t[bass.ds(b * P, n), :]

        def row_of(v):
            return v.rearrange("(a n) -> a n", a=1).broadcast_to([P, v.shape[0]])

        win = accr[:, 0:392]
        loc = accr[:, 392:784]
        typ = accr[:, 784:1176]
        pen = accr[:, 1176:1568]
        dsti = accr[:, 1568:1960].bitcast(I32)
        srci = accr[:, 1960:2352].bitcast(I32)
        typi = accr[:, 2352:2744].bitcast(I32)
        pos = accr[:, 2744:3136]
        off = accr[:, 3136:3240]
        cnt = accr[:, 3240:3344]
        ntl = accr[:, 3344:3448]
        tbi = accr[:, 3448:3552]
        zrow = accr[:, 3552:3656]
        tcol = accr[0:NWIN, 3656:3657]
        toti = accr[:, 3660:3764].bitcast(I32)
        PE1 = QC + 1
        hot = at(accr, 3800, WPP, PE1)
        hotf = accr[:, 3800:3800 + WPP * PE1]
        run = at(accr, 4541, WPP, PE1)
        runf = accr[:, 4541:4541 + WPP * PE1]
        prod = at(accr, 5282, WPP, QC)
        psum_pos = accr[:, 6010:6066]
        keep = at(accr, 6066, WPP, PE1)
        keepf = accr[:, 6066:6066 + WPP * PE1]
        recc = [at(accr, 6807 + s * CH * REC, CH, REC) for s in range(2)]
        slot = [accr[:, 8599 + 8 * s:8599 + 8 * s + CH].bitcast(I32) for s in range(2)]
        ni, na, nb = (accr[:, 8616 + 8 * i:8616 + 8 * i + CH].bitcast(I32) for i in range(3))
        iwin = accr[:, 8650:8754]
        iloc = accr[:, 8760:8792]
        ityp = accr[:, 8792:8795]
        itile = accr[:, 8800:9292]
        lemat = accr[:, 9292:9784]
        blank = at(ring, 0, BODY, REC)
        wgate = at(ring, 3072, 4, 768)
        w2l0 = at(node, 5376, 2, HID)
        b2x = node[:, 5888:6144]
        wpq = at(node, 0, 2, 512)
        b1row = node[0:1, 1024:1536]
        xb = [node[:, 1536 + 256 * s:1792 + 256 * s] for s in range(2)]
        hb = [node[:, 2048 + 256 * s:2304 + 256 * s] for s in range(2)]
        hT = [at(node, 2560 + 256 * s, 2, P) for s in range(2)]
        hTf = [node[:, 2560 + 256 * s:2816 + 256 * s] for s in range(2)]
        qst = [node[:, 3072 + 256 * s:3328 + 256 * s] for s in range(2)]
        xs = [node[:, 3584 + 256 * s:3840 + 256 * s] for s in range(2)]
        rec = [at(node, 512 * g, GT, REC) for g in range(RING)]
        lh = [node[0:96, 1536 + P * s:1536 + P * (s + 1)] for s in range(2)]
        pre = [node[:, 1792 + 256 * k:2048 + 256 * k] for k in range(GT)]
        act = [node[:, 2816 + 256 * k:3072 + 256 * k] for k in range(GT)]
        mk0 = [node[64:96, 3840 + 256 * g:4096 + 256 * g].bitcast(BF16) for g in range(RING)]
        qg = [ring[:, HID * t:HID * (t + 1)] for t in range(BODY)]
        acc0 = at(accr, 0, NWIN, 96)
        A = node[:, 0:2048].rearrange("p (k c n) -> p k c n", k=GT, c=16)
        pk = [at(node, 2048 + GT * PK * g, GT, PK) for g in range(RING)]
        pkf = [node[:, 2048 + GT * PK * g:2048 + GT * PK * (g + 1)] for g in range(RING)]
        mk = [node[:, 2496 + 256 * g:2752 + 256 * g].bitcast(BF16) for g in range(RING)]
        mkall = node[:, 2496:3264]
        kT = [node[:, 3264 + 256 * s:3520 + 256 * s] for s in range(2)]
        sc = at(node, 3776, GT, 16)
        scf = node[:, 3776:3840]
        mx = at(node, 3840, GT, HEADS)
        ex = at(node, 3856, GT, 16)
        exf = node[:, 3856:3920]
        sm = at(node, 3920, GT, HEADS)
        smf = node[:, 3920:3936]
        att = at(node, 3936, GT, 16)
        kv = [ring[:, 2 * HID * t:2 * HID * (t + 1)] for t in range(BODY)]
        acc1 = at(accr, 0, NWIN, DH)
        acc1f = accr[:, 0:NWIN * DH]

        ghT = [at(node, 256 * s, 2, P) for s in range(2)]
        ghTf = [node[:, 256 * s:256 * s + 256] for s in range(2)]
        gh = [node[:, 512 + 256 * s:768 + 256 * s] for s in range(2)]
        gx = [node[:, 1024 + 256 * s:1280 + 256 * s] for s in range(2)]
        aggT = [at(node, 1536 + 256 * s, 2, P) for s in range(2)]
        aggTf = [node[:, 1536 + 256 * s:1792 + 256 * s] for s in range(2)]
        rz = [node[:, 2048 + 512 * s:2560 + 512 * s] for s in range(2)]
        cand = [node[:, 3072 + 256 * s:3328 + 256 * s] for s in range(2)]
        newx = [node[:, 3584 + 256 * s:3840 + 256 * s] for s in range(2)]
        gt = node[:, 4096:4352]
        brz, brzh = ring[:, 0:512], ring[:, 512:1024]
        bxn, bhn = ring[:, 1024:1280], ring[:, 1280:1536]
        iw = at(node, 0, 2, HID)
        ib = node[:, 512:768]
        ix = [node[:, 768 + 256 * s:1024 + 256 * s] for s in range(2)]
        ih = [node[:, 1280 + 256 * s:1536 + 256 * s] for s in range(2)]
        ihT = [at(node, 1792 + 256 * s, 2, P) for s in range(2)]
        ihTf = [node[:, 1792 + 256 * s:2048 + 256 * s] for s in range(2)]
        ibase = [node[:, 2304 + 256 * s:2560 + 256 * s] for s in range(2)]
        ihid = [node[:, 2816 + 256 * s:3072 + 256 * s] for s in range(2)]
        wq = node[:, 0:1024].rearrange("p (k h m) -> p k h m", k=2, h=HEADS)
        wkv = at(node, 1024, 2, 512)
        bq = node[:, 2048:2052]
        bkv = node[:, 2052:2564]
        ah = [node[:, 2564 + 256 * s:2820 + 256 * s] for s in range(2)]
        ahT = [at(node, 3076 + 256 * s, 2, P) for s in range(2)]
        ahTf = [node[:, 3076 + 256 * s:3332 + 256 * s] for s in range(2)]
        akv = [node[:, 3588 + 512 * s:4100 + 512 * s] for s in range(2)]
        QT = big[:, :, :].rearrange("p w (g h n) -> p w g h n", g=2, h=HEADS)
        wo = at(node, 0, HEADS, HID, parts=DH)
        eeT = at(node, 1024, HEADS, 4, parts=DH)
        borow = node[0:1, 1040:1296]
        eb = node[0:4, 1296:1552]
        cst = [at(node, 1552 + 256 * s, WPB, DH) for s in range(2)]
        cT = [at(node, 2064 + 512 * s, HEADS, P, parts=DH) for s in range(2)]
        cc = [node[0:4, 3088 + P * s:3088 + P * (s + 1)] for s in range(2)]
        ch = [node[:, 3344 + 256 * s:3600 + 256 * s] for s in range(2)]
        cy = [node[:, 3856 + 256 * s:4112 + 256 * s] for s in range(2)]
        lng, lnb = node[:, 0:256], node[:, 256:512]
        dy = [node[:, 512 + 256 * s:768 + 256 * s] for s in range(2)]
        dt = [node[:, 1024 + 256 * s:1280 + 256 * s] for s in range(2)]
        du = [node[:, 1536 + 256 * s:1792 + 256 * s] for s in range(2)]
        fw1, fw2 = at(node, 0, 2, HID), at(node, 512, 2, HID)
        fb1, fb2 = node[:, 1024:1026], node[:, 1026:1282]
        fh = [node[:, 1282 + 256 * s:1538 + 256 * s] for s in range(2)]
        fhT = [at(node, 1794 + 256 * s, 2, P) for s in range(2)]
        fhTf = [node[:, 1794 + 256 * s:2050 + 256 * s] for s in range(2)]
        fuT = [at(node, 2306 + 256 * s, 2, P) for s in range(2)]
        fbase = [node[:, 2818 + 256 * s:3074 + 256 * s] for s in range(2)]
        fo = [node[:, 3330 + 256 * s:3586 + 256 * s] for s in range(2)]

        pr = events("pr", "consts idx weights x_read var root norm cnt pre_psum tile_base base_psum below win_psum "
                          "blank cleared rec pool vstep rstep")
        pr_x, pr_attr, pr_scat = (sems(f"pr_{w}", 2) for w in ("x", "attr", "scat"))
        n0 = events("n0", "h hT_psum hT pq_psum pq")
        n0_x, n0_h, n0_hT, n0_q = (sems(f"n0_{w}", 2) for w in ("x", "hst", "hTst", "qst"))
        e0 = events("e0", "T_psum T pre_psum pre act seg_psum added mask vstep ")
        e0_rec, e0_pack, e0_mask = (sems(f"e0_{w}", RING) for w in ("rec", "pack", "mask"))
        e0_q = sems("e0_q", RING)
        n1 = events("n1", "loads agg_psum aggT gate_psum rz_pre rz n_pre n x1 vstep")
        n1_in, n1_out = sems("n1_in", 2), sems("n1_out", 2)
        n2 = events("n2", "loads h hT_psum hT hid_psum base hid")
        n2_x, n2_b, n2_h = (sems(f"n2_{w}", 2) for w in ("x", "bst", "hst"))
        pa = events("pa", "loads hT_psum hT q_psum kv_psum q kv")
        pa_in, pa_out = sems("pa_in", 2), sems("pa_out", 2)
        e1 = events("e1", "mask_rows T_psum T s_psum s_read shifted exp a o_psum added vstep vgroup")
        e1_pk, e1_mk = sems("e1_pk", RING), sems("e1_mk", RING)
        e1_kv = sems("e1_kv", RING)
        pb = events("pb", "loads eb_psum eb staged T_psum aT m_psum y vstep vstat var root")
        pb_in, pb_out = sems("pb_in", 2), sems("pb_out", 2)
        pc = events("pc", "loads t u o vstep")
        pc_in, pc_out = sems("pc_in", 2), sems("pc_out", 2)
        pf = events("pf", "loads hT_psum hT u_psum u o_psum o vstep")
        pf_in, pf_out = sems("pf_in", 2), sems("pf_out", 2)

        WINT = (0, NWIN - 1)
        HALF = BLOCKS // 2

        def windows(engine, t):
            return nc.values_load_multi_w_load_instructions(
                wtab[0:1, bass.ds(t, GT)], engines=(engine,), min_val=0, max_val=NWIN - 1)[1]

        def sum_bank(k):
            return banks[6 + k // 2]

        STAT_STEPS = 14

        def stats_v(step, var, root, n):
            v = nc.vector
            mean, var_, t0, t1, root_ = (st4[:, j, :] for j in range(2, 7))
            me, m2e, mo, m2o = bst[:, :, 1], bst[:, :, 2], bst[:, :, 4], bst[:, :, 5]
            step(v.tensor_tensor(t0, me, mo, ALU.subtract))
            step(v.tensor_tensor(mean, me, mo, ALU.add))
            step(v.tensor_scalar(mean, mean, 0.5, None, ALU.mult))
            step(v.tensor_scalar(t0, t0, 0.5, None, ALU.mult))
            step(v.tensor_tensor(t0, t0, t0, ALU.mult))
            step(v.tensor_tensor(t1, m2e, m2o, ALU.add))
            step(v.tensor_scalar(t1, t1, 1.0 / HID, EPS, ALU.mult, ALU.add))
            v.tensor_tensor(var_, t0, t1, ALU.add).then_inc(var, 1)
            v.wait_ge(root, n)
            step(v.reciprocal(rstd, root_))
            step(v.tensor_tensor(t0, rstd, rstd, ALU.mult))
            step(v.tensor_tensor(t0, t0, var_, ALU.mult))
            step(v.tensor_scalar(t0, t0, -0.5, 1.5, ALU.mult, ALU.add))
            step(v.tensor_tensor(rstd, rstd, t0, ALU.mult))
            step(v.tensor_tensor(t1, mean, rstd, ALU.mult))
            step(v.tensor_scalar(nmr, t1, -1.0, None, ALU.mult))

        def stats_a(var, root, n):
            nc.scalar.wait_ge(var, n)
            hold(nc.scalar)
            nc.scalar.activation(st4[:, 6, :], st4[:, 3, :], ACT.Sqrt).then_inc(root, 1)

        @block.sync
        def _(sp):
            def after(s, count):
                sp.wait_ge(s, count)
                hold(sp)

            def need_sp(s, i, base, count):
                if not (isinstance(i, int) and count <= 0):
                    after(s, base + count)

            for v, w in ((srci, "src"), (dsti, "dst"), (typi, "typ")):
                sp.dma_start(v, a[w]).then_inc(pr["idx"], 16)

            def load_x(i):
                for s in range(2):
                    need_sp(pr["x_read"], i, i * 2, s - 1)
                    sp.dma_start(xs[s], rows(a["x"], i * 2 + s)).then_inc(pr_x[s], 16)
            pairs(sp, load_x)
            for v, w in ((wpq, "w_pq"), (b1row, "b1_row"), (w2l0, "w2_l0"), (b2x, "b2_rows")):
                sp.dma_start(v, a[w]).then_inc(pr["weights"], 16)
            for half in range(4):
                sp.dma_start(wgate[:, half, :], a["w_gate"][:, half, :]).then_inc(pr["weights"], 16)
            sp.dma_start(big[0:ATTR, :, :], a["w1_attr"].unsqueeze(1).broadcast_to([ATTR, NWIN, HID])
                         ).then_inc(pr["weights"], 16)

            def load_x_again(i):
                for s in range(2):
                    need_sp(n0["h"], i, i * 2, s - 1)
                    sp.dma_start(xb[s], rows(a["x"], i * 2 + s)).then_inc(n0_x[s], 16)
            pairs(sp, load_x_again)

            def load_attr(i):
                for s in range(2):
                    if isinstance(i, int):
                        after(pr["cleared"], 1)
                    else:
                        after(pr_scat[s], i * (16 * CH))
                    sp.dma_start(recc[s][:, :, 0:ATTR], a["attr"].rearrange("(p c) f -> p c f", p=P)[
                        :, bass.ds(i * (2 * CH) + s * CH, CH), :]).then_inc(pr_attr[s], 16)
            load_attr(0)
            with sp.Fori(1, CHUNKS // 2) as i:
                load_attr(i)
            after(pr["weights"], 144)
            barrier(sp, B_PREP)

            def e0_load(it, g):
                need_sp(e0["seg_psum"], it, it * BODY, (g - 2) * GT)
                if not isinstance(it, int):
                    after(e0_pack[g], it * 16)
                sp.dma_start(rec[g], rect[bass.ds((it * RING + g) * (GT * P), GT * P), :]
                             .rearrange("(p k) f -> p k f", k=GT)).then_inc(e0_rec[g], 16)

            def e0_store(it, g):
                after(e0_rec[g], it * 16 + 16)
                sp.dma_start(packd[bass.ds(it * RING + g, 1), :, :].rearrange("a p (k f) -> (a p) k f", k=GT),
                             rec[g][:, :, R_OH:R_END]).then_inc(e0_pack[g], 16)
                after(e0["mask"], it * BODY + (g + 1) * GT)
                sp.dma_start(maskd[bass.ds(it * RING + g, 1), :, :].rearrange("a p f -> (a p) f"),
                             mk0[g]).then_inc(e0_mask[g], 16)

            for g in range(RING):
                e0_load(0, g)
            with sp.Fori(1, ITERS) as it:
                for g in range(RING):
                    e0_store(it - 1, g)
                    after(e0["seg_psum"], it * BODY + (g - 2) * GT)
                    after(e0_pack[g], it * 16)
                    sp.dma_start(rec[g], rect[bass.ds((it * RING + g) * (GT * P), GT * P), :]
                                 .rearrange("(p k) f -> p k f", k=GT)).then_inc(e0_rec[g], 16)
            for g in range(RING):
                e0_store(ITERS - 1, g)
            for g in range(RING):
                after(e0_pack[g], 16 * ITERS)
                after(e0_mask[g], 16 * ITERS)
            barrier(sp, B_E0)

            sp.dma_start(cntd.rearrange("c (w n) -> c w n", n=WIN), acc0[96:100, :, 64:96]).then_inc(n1["loads"], 16)
            for v, w in ((brz, a["b_ih"][0:512]), (brzh, a["b_hh"][0:512]), (bxn, a["b_ih"][512:768]),
                         (bhn, a["b_hh"][512:768])):
                sp.dma_start(v, row_of(w)).then_inc(n1["loads"], 16)

            def load_gate(i):
                for s in range(2):
                    b = i * 2 + s
                    need_sp(n1["x1"], i, i * 2, s - 1)
                    for v, t in ((ghTf[s], h0Td), (gh[s], h0d), (gx[s], a["x"])):
                        sp.dma_start(v, rows(t, b)).then_inc(n1_in[s], 16)
            pairs(sp, load_gate)
            after(n1["loads"], 80)
            barrier(sp, B_N1)

            sp.dma_start(iw, a["w_in"]).then_inc(n2["loads"], 16)
            sp.dma_start(ib, row_of(a["b_in"])).then_inc(n2["loads"], 16)

            def load_entry(i):
                for s in range(2):
                    need_sp(n2["base"], i, i * 2, s - 1)
                    sp.dma_start(ix[s], rows(x1d, i * 2 + s)).then_inc(n2_x[s], 16)
            pairs(sp, load_entry)
            barrier(sp, B_N2)

            with sp.Fori(0, LAYERS) as l:
                def lay(w):
                    return a[w][bass.ds(l * (a[w].shape[0] // LAYERS), a[w].shape[0] // LAYERS)]
                sp.dma_start(node[:, 0:1024], lay("w_q")).then_inc(pa["loads"], 16)
                sp.dma_start(node[:, 1024:2048], lay("w_kv")).then_inc(pa["loads"], 16)
                sp.dma_start(bq, lay("b_q")).then_inc(pa["loads"], 16)
                sp.dma_start(bkv, lay("b_kv").broadcast_to([P, 512])).then_inc(pa["loads"], 16)

                def load_hidden(i):
                    for s in range(2):
                        need_sp(pa["hT_psum"], i, l * BLOCKS + i * 2, s - 1)
                        sp.dma_start(ah[s], rows(hidd, i * 2 + s)).then_inc(pa_in[s], 16)
                pairs(sp, load_hidden)
                layer_barrier(sp, l, 1)

                def load_pack(it):
                    for g in range(RING):
                        if not isinstance(it, int):
                            after(e1["a"], l * TILES + it * BODY + (g - 2) * GT)
                            after(e1["s_psum"], l * TILES + it * BODY + (g - 2) * GT)
                        n = it * RING + g
                        sp.dma_start(pkf[g], packd[bass.ds(n, 1), :, :].rearrange("a p f -> (a p) f")
                                     ).then_inc(e1_pk[g], 16)
                        sp.dma_start(mk[g][64:96, :], maskd[bass.ds(n, 1), :, :].rearrange("a p f -> (a p) f")
                                     ).then_inc(e1_mk[g], 16)
                after(e1["mask_rows"], l + 1)
                bodies(sp, load_pack)
                layer_barrier(sp, l, 2)

                sp.dma_start(node[0:DH, 0:1024], lay("w_o")).then_inc(pb["loads"], 16)
                sp.dma_start(node[0:DH, 1024:1040], lay("e_T")).then_inc(pb["loads"], 16)
                sp.dma_start(borow, lay("b_o")).then_inc(pb["loads"], 16)

                def load_residual(i):
                    for s in range(2):
                        b = i * 2 + s
                        need_sp(pb["y"], i, l * BLOCKS + i * 2, s - 1)
                        sp.dma_start(ch[s], rows(hidd, b)).then_inc(pb_in[s], 16)
                        sp.dma_start(cc[s], cntd[:, bass.ds(b * P, P)]).then_inc(pb_in[s], 16)
                pairs(sp, load_residual)
                layer_barrier(sp, l, 3)

                sp.dma_start(lng, lay("ln_g").broadcast_to([P, HID])).then_inc(pc["loads"], 16)
                sp.dma_start(lnb, lay("ln_b").broadcast_to([P, HID])).then_inc(pc["loads"], 16)

                def load_sum(i):
                    for s in range(2):
                        need_sp(pc["t"], i, l * BLOCKS + i * 2, s - 1)
                        sp.dma_start(dy[s], rows(yd, i * 2 + s)).then_inc(pc_in[s], 16)
                pairs(sp, load_sum)
                layer_barrier(sp, l, 4)

            for v, w in ((fw1, "w_f1"), (fw2, "w_f2"), (fb1, "b_f1")):
                sp.dma_start(v, a[w]).then_inc(pf["loads"], 16)
            sp.dma_start(fb2, row_of(a["b_f2"])).then_inc(pf["loads"], 16)

            def load_last(i):
                for s in range(2):
                    b = i * 2 + s
                    need_sp(pf["o"], i, i * 2, s - 1)
                    sp.dma_start(fh[s], rows(hidd, b)).then_inc(pf_in[s], 16)
                    sp.dma_start(fbase[s], rows(based, b)).then_inc(pf_in[s], 16)
            pairs(sp, load_last)

        @block.gpsimd
        def _(pool):
            steps = Steps(pool, pr["pool"])
            for m in (ident, before, ones):
                last = pool.memset(m[:, :], 1.0 if m is ones else 0.0)
                steps(last)
            steps(pool.affine_select(out=ident[:, :], in_=ident[:, :], compare_op=ALU.not_equal, fill=1.0, base=0,
                                     pattern=[[-1, P]], channel_multiplier=1))
            steps(pool.affine_select(out=before[:, :], in_=before[:, :], compare_op=ALU.is_ge, fill=1.0, base=0,
                                     pattern=[[-1, P]], channel_multiplier=1))
            steps(pool.memset(neg[:, :], 0.0))
            steps(pool.affine_select(out=neg[:, :].rearrange("p (c n) -> p c n", n=WIN),
                                     in_=neg[:, :].rearrange("p (c n) -> p c n", n=WIN),
                                     compare_op=ALU.not_equal, fill=NEGB, base=-64, pattern=[[0, 16], [-1, WIN]],
                                     channel_multiplier=1))
            for v, n in ((iwin, NWIN), (iloc, WIN), (ityp, TYPES), (itile, TILES)):
                steps(pool.iota(v, pattern=[[1, n]], base=0, channel_multiplier=0,
                                allow_small_or_imprecise_dtypes=True))
            for v, val in ((keepf, 1.0), (zrow, 0.0), (pos, 0.0)):
                steps(pool.memset(v, val))
            steps(pool.memset(keep[:, :, 0:1], 0.0))
            pool.sem_inc(pr["consts"], 1)
            steps(pool.memset(blank[:, :, :], 0.0))
            steps(pool.memset(blank[:, :, R_DST:R_DST + 1].bitcast(I32), FAR))
            for s in range(2):
                steps(pool.memset(recc[s], 0.0))
                steps(pool.memset(recc[s][:, :, R_CNT:R_CNT + 1], 1.0))
            pool.sem_inc(pr["cleared"], 1)
            all_rows = pool.to_reg(ROWS - 1)
            all_nodes = pool.to_reg(NPAD - 1)
            with pool.Fori(0, ITERS) as i:
                pool.dma_start(rect[bass.ds(i * (BODY * P), BODY * P), :].rearrange("(p k) f -> p k f", k=BODY),
                               blank).then_inc(pr["blank"], 16)
            pool.wait_ge(pr["blank"], 16 * ITERS)

            def scatter(i):
                for s in range(2):
                    pool.wait_ge(pr["rec"], i * 2 + (s + 1))
                    pool.wait_ge(pr_attr[s], i * 16 + 16)
                    hold(pool)
                    for j in range(CH):
                        pool.indirect_dma_start(rect, bass.IndirectOffsetOnAxis(ap=slot[s][:, j:j + 1], axis=0),
                                                recc[s][:, j, :], None, bounds_check=all_rows, oob_is_err=False
                                                ).then_inc(pr_scat[s], 16)
            scatter(0)
            with pool.Fori(1, CHUNKS // 2) as i:
                scatter(i)
            for s in range(2):
                pool.wait_ge(pr_scat[s], 16 * CH * (CHUNKS // 2))
            barrier(pool, B_PREP)

            steps(pool.memset(ring[:, 0:BODY * HID], 0.0))

            def gather_rows(it):
                for g in range(RING):
                    pool.wait_ge(e0_rec[g], it * 16 + 16)
                    hold(pool)
                    for k in range(GT):
                        t = GT * g + k
                        if not isinstance(it, int):
                            pool.wait_ge(e0["pre"], it * BODY + (t + 1 - BODY))
                            hold(pool)
                        pool.indirect_dma_start(qg[t], None, qrows, bass.IndirectOffsetOnAxis(
                            ap=rec[g][:, k, R_DST:R_DST + 1].bitcast(I32), axis=0), bounds_check=all_nodes,
                            oob_is_err=False).then_inc(e0_q[g], 16)
            bodies(pool, gather_rows)
            barrier(pool, B_E0)

            def store_x1(i):
                for s in range(2):
                    pool.wait_ge(n1["x1"], i * 2 + (s + 1))
                    hold(pool)
                    pool.dma_start(rows(x1d, i * 2 + s), newx[s]).then_inc(n1_out[s], 16)
            pairs(pool, store_x1)
            for s in range(2):
                pool.wait_ge(n1_out[s], 16 * HALF)
            barrier(pool, B_N1)

            pool.memset(QT[0:64, :, 1, :, :].rearrange("p w h n -> p w (h n)"), 0.0)
            pool.memset(QT[64:128, :, 0, :, :].rearrange("p w h n -> p w (h n)"), 0.0)

            def store_entry(i):
                for s in range(2):
                    b = i * 2 + s
                    pool.wait_ge(n2["base"], i * 2 + (s + 1))
                    hold(pool)
                    pool.dma_start(rows(based, b), ibase[s]).then_inc(n2_b[s], 16)
                    pool.wait_ge(n2["hid"], i * 2 + (s + 1))
                    hold(pool)
                    pool.dma_start(rows(hidd, b), ihid[s]).then_inc(n2_h[s], 16)
            pairs(pool, store_entry)
            for s in range(2):
                pool.wait_ge(n2_b[s], 16 * HALF)
                pool.wait_ge(n2_h[s], 16 * HALF)
            barrier(pool, B_N2)

            with pool.Fori(0, LAYERS) as l:
                pool.memset(acc1f, 0.0)

                def store_kv(i):
                    for s in range(2):
                        pool.wait_ge(pa["kv"], l * BLOCKS + i * 2 + (s + 1))
                        hold(pool)
                        pool.dma_start(rows(kvrows, i * 2 + s), akv[s]).then_inc(pa_out[s], 16)
                pairs(pool, store_kv)
                for s in range(2):
                    pool.wait_ge(pa_out[s], (l + 1) * (16 * HALF))
                layer_barrier(pool, l, 1)

                pool.memset(mkall, 0.0).then_inc(e1["mask_rows"], 1)

                def gather_kv(it):
                    for g in range(RING):
                        pool.wait_ge(e1_pk[g], (l * ITERS + it) * 16 + 16)
                        hold(pool)
                        for k in range(GT):
                            t = GT * g + k
                            if not isinstance(it, int):
                                pool.wait_ge(e1["o_psum"], l * TILES + it * BODY + (t + 1 - BODY))
                                hold(pool)
                            pool.indirect_dma_start(kv[t], None, kvrows, bass.IndirectOffsetOnAxis(
                                ap=pk[g][:, k, PK - 1:PK].bitcast(I32), axis=0), bounds_check=all_nodes,
                                oob_is_err=False).then_inc(e1_kv[g], 16)
                bodies(pool, gather_kv)
                layer_barrier(pool, l, 2)

                def store_sum(i):
                    for s in range(2):
                        pool.wait_ge(pb["y"], l * BLOCKS + i * 2 + (s + 1))
                        hold(pool)
                        pool.dma_start(rows(yd, i * 2 + s), cy[s]).then_inc(pb_out[s], 16)
                pairs(pool, store_sum)
                for s in range(2):
                    pool.wait_ge(pb_out[s], (l + 1) * (16 * HALF))
                layer_barrier(pool, l, 3)

                def store_hidden(i):
                    for s in range(2):
                        pool.wait_ge(pc["o"], l * BLOCKS + i * 2 + (s + 1))
                        hold(pool)
                        pool.dma_start(rows(hidd, i * 2 + s), du[s]).then_inc(pc_out[s], 16)
                pairs(pool, store_hidden)
                for s in range(2):
                    pool.wait_ge(pc_out[s], (l + 1) * (16 * HALF))
                layer_barrier(pool, l, 4)

            def store_out(i):
                for s in range(2):
                    pool.wait_ge(pf["o"], i * 2 + (s + 1))
                    hold(pool)
                    pool.dma_start(rows(out, i * 2 + s), fo[s]).then_inc(pf_out[s], 16)
            pairs(pool, store_out)
            for s in range(2):
                pool.wait_ge(pf_out[s], 16 * HALF)

        @block.scalar
        def _(act_):
            sc_ = nc.scalar
            stats_a(pr["var"], pr["root"], 1)
            act_.wait_ge(pr["norm"], 1)

            def nodes0(i):
                for s in range(2):
                    b = i * 2 + s
                    act_.wait_ge(n0_x[s], i * 16 + 16)
                    need(act_, n0["hT_psum"], i, i * 2, s - 1)
                    need(act_, n0_h[s], i, 0, i * 16)
                    hold(act_)
                    sc_.activation(hb[s], xb[s], ACT.Relu, bias=nmr[:, bass.ds(b, 1)],
                                   scale=rstd[:, bass.ds(b, 1)]).then_inc(n0["h"], 1)
                    act_.wait_ge(n0["h"], i * 2 + (s + 1))
                    act_.dma_start(rows(h0d, b), hb[s]).then_inc(n0_h[s], 16)
                    act_.wait_ge(n0["hT_psum"], i * 2 + (s + 1))
                    need(act_, n0["pq_psum"], i, i * 2, s - 1)
                    need(act_, n0_hT[s], i, 0, i * 16)
                    hold(act_)
                    sc_.activation(hTf[s], banks[s][:, 0:256], ACT.Copy).then_inc(n0["hT"], 1)
                    act_.wait_ge(n0["hT"], i * 2 + (s + 1))
                    act_.dma_start(rows(h0Td, b), hTf[s]).then_inc(n0_hT[s], 16)
                    act_.wait_ge(n0["pq_psum"], i * 2 + (s + 1))
                    need(act_, n0_q[s], i, 0, i * 16)
                    hold(act_)
                    for w in range(WPB):
                        sc_.activation(big[64:96, bass.ds(b * WPB + w, 1), :].rearrange("p a n -> p (a n)"),
                                       banks[2 + s][WIN * w:WIN * (w + 1), 0:256], ACT.Copy).then_inc(n0["pq"], 1)
                    sc_.activation(qst[s], banks[2 + s][:, 256:512], ACT.Copy).then_inc(n0["pq"], 1)
                    act_.wait_ge(n0["pq"], (i * 2 + (s + 1)) * 5)
                    act_.dma_start(rows(qrows, b), qst[s]).then_inc(n0_q[s], 16)
            pairs(act_, nodes0)
            for s in range(2):
                for q in (n0_h, n0_hT, n0_q):
                    act_.wait_ge(q[s], 16 * HALF)
            barrier(act_, B_PREP)

            def edges0(it):
                for g in range(RING):
                    n = it * BODY + g * GT
                    for k in range(GT):
                        act_.wait_ge(e0["T_psum"], n + (k + 1))
                        need(act_, e0["pre_psum"], it, n, k - 1, g * GT)
                        need(act_, e0["mask"], it, n, k - 1, g * GT)
                        hold(act_)
                        sc_.activation(lh[k % 2], banks[k % 2][0:96, 0:P], ACT.Copy).then_inc(e0["T"], 1)
                        if not (isinstance(it, int) and g == 0):
                            relu0(it, g, n - GT, k)

            def relu0(it, g, n, k):
                act_.wait_ge(e0["pre"], n + (k + 1))
                need(act_, e0["seg_psum"], it, n, k + 1 - GT, (g - 1) * GT)
                hold(act_)
                sc_.activation(act[k], pre[k], ACT.Relu).then_inc(e0["act"], 1)
            bodies(act_, edges0)
            for k in range(GT):
                relu0(ITERS, 0, TILES - GT, k)
            barrier(act_, B_E0)

            def update0(i):
                for s in range(2):
                    b = i * 2 + s
                    act_.wait_ge(n1["agg_psum"], b + 1)
                    need(act_, n1["gate_psum"], i, i * 2, s - 1)
                    hold(act_)
                    sc_.activation(aggTf[s], banks[s][:, 0:256], ACT.Copy).then_inc(n1["aggT"], 1)
                    act_.wait_ge(n1["rz_pre"], b + 1)
                    hold(act_)
                    sc_.activation(rz[s], rz[s], ACT.Sigmoid).then_inc(n1["rz"], 1)
                    act_.wait_ge(n1["n_pre"], b + 1)
                    hold(act_)
                    sc_.activation(cand[s], cand[s], ACT.Tanh).then_inc(n1["n"], 1)
            pairs(act_, update0)
            stats_a(pr["var"], pr["root"], 2)
            barrier(act_, B_N1)

            def entry(i):
                for s in range(2):
                    b = i * 2 + s
                    act_.wait_ge(n2_x[s], i * 16 + 16)
                    need(act_, n2["hT_psum"], i, i * 2, s - 1)
                    need(act_, n2["base"], i, i * 2, s - 1)
                    hold(act_)
                    sc_.activation(ih[s], ix[s], ACT.Relu, bias=nmr[:, bass.ds(b, 1)],
                                   scale=rstd[:, bass.ds(b, 1)]).then_inc(n2["h"], 1)
                    act_.wait_ge(n2["hT_psum"], b + 1)
                    need(act_, n2["hid_psum"], i, i * 2, s - 1)
                    hold(act_)
                    sc_.activation(ihTf[s], banks[s][:, 0:256], ACT.Copy).then_inc(n2["hT"], 1)
            pairs(act_, entry)
            barrier(act_, B_N2)

            with act_.Fori(0, LAYERS) as l:
                def project(i):
                    for s in range(2):
                        n = l * BLOCKS + i * 2
                        act_.wait_ge(pa["hT_psum"], n + (s + 1))
                        need(act_, pa["kv_psum"], i, n, s - 1)
                        hold(act_)
                        sc_.activation(ahTf[s], banks[s][:, 0:256], ACT.Copy).then_inc(pa["hT"], 1)
                pairs(act_, project)
                layer_barrier(act_, l, 1)

                def exps(n):
                    act_.wait_ge(e1["shifted"], l * GROUPS + n)
                    hold(act_)
                    sc_.activation(exf, exf, ACT.Exp, scale=DH ** -0.5).then_inc(e1["exp"], 1)

                def edges1(it):
                    for g in range(RING):
                        n = l * TILES + it * BODY + g * GT
                        for k in range(GT):
                            act_.wait_ge(e1["T_psum"], n + (k + 1))
                            if not (isinstance(it, int) and g == 0 and k < 2):
                                act_.wait_ge(e1["s_psum"], n + (k - 1))
                            hold(act_)
                            sc_.activation(kT[k % 2], banks[k % 2][:, 0:256], ACT.Copy).then_inc(e1["T"], 1)
                            if k == 1 and not (isinstance(it, int) and g == 0):
                                exps(it * RING + g)
                bodies(act_, edges1)
                exps(GROUPS)
                layer_barrier(act_, l, 2)

                act_.wait_ge(pb["eb_psum"], l + 1)
                hold(act_)
                sc_.activation(eb, banks[7][0:4, 0:HID], ACT.Copy).then_inc(pb["eb"], 1)

                def output(i):
                    for s in range(2):
                        b, n = i * 2 + s, l * BLOCKS + i * 2
                        need(act_, pb["T_psum"], i, n, s - 1)
                        if not isinstance(i, int):
                            hold(act_)
                        sc_.activation(cst[s], acc1[:, bass.ds(b * WPB, WPB), :], ACT.Copy).then_inc(pb["staged"], 1)
                        act_.wait_ge(pb["T_psum"], n + (s + 1))
                        need(act_, pb["m_psum"], i, n, s - 1)
                        hold(act_)
                        sc_.activation(cT[s].rearrange("p h (w n) -> p w h n", w=WPB),
                                       banks[s][0:DH, :].rearrange("p (w h n) -> p w h n", w=WPB, h=HEADS),
                                       ACT.Copy).then_inc(pb["aT"], 1)
                pairs(act_, output)
                stats_a(pb["var"], pb["root"], l + 1)
                layer_barrier(act_, l, 3)

                def norm(i):
                    for s in range(2):
                        b, n = i * 2 + s, l * BLOCKS + i * 2
                        act_.wait_ge(pc_in[s], (l * HALF + i) * 16 + 16)
                        need(act_, pc["u"], i, n, s - 1)
                        hold(act_)
                        sc_.activation(dt[s], dy[s], ACT.Identity, bias=nmr[:, bass.ds(b, 1)],
                                       scale=rstd[:, bass.ds(b, 1)]).then_inc(pc["t"], 1)
                pairs(act_, norm)
                layer_barrier(act_, l, 4)

            act_.wait_ge(pf["loads"], 64)

            def last(i):
                for s in range(2):
                    b = i * 2 + s
                    act_.wait_ge(pf["hT_psum"], b + 1)
                    need(act_, pf["u_psum"], i, i * 2, s - 1)
                    hold(act_)
                    sc_.activation(fhTf[s], banks[s][:, 0:256], ACT.Copy).then_inc(pf["hT"], 1)
                    act_.wait_ge(pf["u_psum"], b + 1)
                    need(act_, pf["o_psum"], i, i * 2, s - 1)
                    hold(act_)
                    for j in range(2):
                        sc_.activation(fuT[s][:, j, :], banks[2 + s][:, P * j:P * (j + 1)], ACT.Relu,
                                       bias=fb1[:, j:j + 1]).then_inc(pf["u"], 1)
            pairs(act_, last)

        @block.vector
        def _(v):
            def stat_x(i):
                for s in range(2):
                    v.wait_ge(pr_x[s], i * 16 + 16)
                    v.bn_stats(bst[:, bass.ds(i * 2 + s, 1), :].rearrange("p a c -> p (a c)"), xs[s]
                               ).then_inc(pr["x_read"], 1)
            pairs(v, stat_x)
            v.wait_ge(pr["x_read"], BLOCKS)
            step = Steps(v, pr["vstep"])
            stats_v(step, pr["var"], pr["root"], 1)
            v.sem_inc(pr["norm"], 1)

            v.wait_ge(pr["idx"], 48)
            v.wait_ge(pr["consts"], 1)
            hits = [hotf[:, 0:COLS], runf[:, 0:COLS]]
            scratch = hits[0].bitcast(I32)
            step(v.tensor_scalar(scratch, srci, 5, None, ALU.arith_shift_right))
            step(v.tensor_copy(win, scratch))
            step(v.tensor_scalar(scratch, srci, WIN - 1, None, ALU.bitwise_and))
            step(v.tensor_copy(loc, scratch))
            step(v.tensor_copy(typ, typi))
            step(v.tensor_scalar(pen, win, 0.0, float(FAR), ALU.is_lt, ALU.mult))
            step(v.tensor_scalar(pen, pen, -1.0, None, ALU.add))
            v.sem_inc(pr["cnt"], 2)
            with v.Fori(0, NWIN // 2) as i:
                for s in range(2):
                    w = bass.ds(i * 2 + s, 1)
                    v.wait_ge(pr["cnt"], i * 2 + (s + 1))
                    v.tensor_scalar(hits[s], win, iwin[:, w], 0.0, ALU.is_equal, ALU.add,
                                    accum_out=cnt[:, w]).then_inc(pr["cnt"], 1)
            v.wait_ge(pr["cnt"], NWIN + 2)
            hold(v)
            v.sem_inc(pr["tile_base"], 1)
            v.wait_ge(pr["pre_psum"], 1)
            step(v.tensor_scalar(toti, banks[4][:, P:P + NWIN], float(P - 1), None, ALU.add))
            step(v.tensor_scalar(toti, toti, 7, None, ALU.arith_shift_right))
            step(v.tensor_copy(ntl, toti))
            step(v.tensor_tensor_scan(tbi, ntl, zrow, 0.0, ALU.add, ALU.add))
            v.sem_inc(pr["tile_base"], 1)
            step(v.tensor_tensor(off, tbi, ntl, ALU.subtract))
            step(v.tensor_scalar(off, off, float(P), None, ALU.mult))
            step(v.tensor_tensor(off, off, banks[4][:, 0:NWIN], ALU.add))
            v.wait_ge(pr["base_psum"], 1)
            step(v.tensor_copy(tcol, banks[5][0:NWIN, 0:1]))
            v.tensor_scalar(lemat[0:NWIN, :], itile[0:NWIN, :], tcol, None, ALU.is_ge).then_inc(pr["below"], 1)
            v.wait_ge(pr["win_psum"], 1)
            step(v.tensor_scalar(wtab[:, :], banks[6][:, 0:TILES], float(NWIN - 1), None, ALU.min))

            RANK = 7

            rank_base = step.c

            def rank(q, j, n):
                st = Steps(v, pr["vstep"], n, RANK, 0)
                st.start = n * RANK + rank_start
                st = st
                cols, ws = bass.ds(q * QC, QC), bass.ds(j * WPP, WPP)
                st(v.tensor_copy(hot[:, :, 0:1], off[:, ws].unsqueeze(2)))
                st(v.tensor_tensor(hot[:, :, 1:PE1], win[:, cols].unsqueeze(1).broadcast_to([P, WPP, QC]),
                                   iwin[:, ws].unsqueeze(2).broadcast_to([P, WPP, QC]), ALU.is_equal))
                st(v.tensor_tensor_scan(runf, keepf, hotf, 0.0, ALU.mult, ALU.add))
                hold(v)
                st(v.tensor_copy(off[:, ws].unsqueeze(2), run[:, :, QC:PE1]))
                st(v.tensor_tensor(prod, run[:, :, 1:PE1], hot[:, :, 1:PE1], ALU.mult))
                st(v.tensor_reduce(psum_pos, prod.rearrange("p w c -> p c w"), AX.X, ALU.add))
                st(v.tensor_tensor(pos[:, cols], pos[:, cols], psum_pos, ALU.add))

            RECS = 9

            def record(i, s, q=None):
                cols = bass.ds(i * (2 * CH) + s * CH, CH)
                if isinstance(i, int):
                    v.wait_ge(pr["cleared"], 1)
                else:
                    v.wait_ge(pr_scat[s], i * (16 * CH))
                st = Steps(v, pr["rstep"], i * 2 + s, RECS)
                st(v.tensor_tensor(ni, pos[:, cols], pen[:, cols], ALU.add))
                st(v.tensor_scalar(na, ni, P - 1, 2, ALU.bitwise_and, ALU.arith_shift_left))
                st(v.tensor_scalar(nb, ni, 7, GT - 1, ALU.arith_shift_right, ALU.bitwise_and))
                st(v.tensor_tensor(na, na, nb, ALU.bitwise_or))
                st(v.tensor_scalar(nb, ni, 9, 9, ALU.arith_shift_right, ALU.arith_shift_left))
                st(v.tensor_tensor(slot[s], na, nb, ALU.bitwise_or))
                st(v.tensor_tensor(recc[s][:, :, R_OH:R_CNT], loc[:, cols].unsqueeze(2).broadcast_to([P, CH, WIN]),
                                   iloc.unsqueeze(1).broadcast_to([P, CH, WIN]), ALU.is_equal))
                st(v.tensor_tensor(recc[s][:, :, R_CNT + 1:R_DST], typ[:, cols].unsqueeze(2)
                                   .broadcast_to([P, CH, TYPES]),
                                   ityp.unsqueeze(1).broadcast_to([P, CH, TYPES]), ALU.is_equal))
                st(v.tensor_copy(recc[s][:, :, R_DST:R_DST + 1].bitcast(I32), dsti[:, cols].unsqueeze(2)))
                hold(v)
                v.sem_inc(pr["rec"], 1)

            rank_start = step.c
            hold(v)
            with v.Fori(0, PARTS) as j:
                rank(0, j, j)
            PH = PARTS // 2

            def chunk_pair(q, jj):
                i = q * PH + jj
                for s in range(2):
                    record(i, s)
                    rank(q + 1, jj * 2 + s, (q + 1) * PARTS + jj * 2 + s)
            chunk_pair(0, 0)
            with v.Fori(1, PH) as jj:
                chunk_pair(0, jj)
            with v.Fori(1, NQ - 1) as q:
                with v.Fori(0, PH) as jj:
                    chunk_pair(q, jj)
            with v.Fori((NQ - 1) * PH, CHUNKS // 2) as i:
                for s in range(2):
                    record(i, s)
            barrier(v, B_PREP)

            v.memset(accr[:, :], 0.0).then_inc(e0["vstep"], 1)
            v.wait_ge(e0["vstep"], 1)

            def add0(n, ws, k):
                if k % 2 == 0:
                    v.wait_ge(e0["seg_psum"], n + (k + 2))
                v.wait_ge(e0["added"], n + (k + 1))
                v.tensor_tensor(acc0[:, bass.ds(ws[k], 1), :], acc0[:, bass.ds(ws[k], 1), :],
                                sum_bank(k)[:, 96 * (k % 2):96 * (k % 2 + 1)].unsqueeze(1), ALU.add
                                ).then_inc(e0["added"], 1)

            def edges0(it):
                for g in range(RING):
                    n = it * BODY + g * GT
                    for k in range(GT):
                        t = g * GT + k
                        v.wait_ge(e0["pre_psum"], n + (k + 1))
                        if k == 0:
                            v.wait_ge(e0_q[g], it * (16 * GT) + 16 * GT)
                        if not (isinstance(it, int) and g == 0):
                            v.wait_ge(e0["act"], n + (k + 1 - GT))
                        hold(v)
                        v.tensor_tensor(pre[k], banks[2 + k][:, 0:HID], qg[t], ALU.add).then_inc(e0["pre"], 1)
                        if k == 0 and not isinstance(it, int):
                            v.wait_ge(e0_mask[g], it * 16)
                            hold(v)
                        v.wait_ge(e0["T"], n + (k + 1))
                        hold(v)
                        v.tensor_scalar(mk0[g][:, P * k:P * (k + 1)], lh[k % 2][64:96, :], -1.0, 1.0, ALU.mult,
                                        ALU.add).then_inc(e0["mask"], 1)
                    if not (isinstance(it, int) and g == 0):
                        ws = windows(mybir.EngineType.DVE, n - GT)
                        for k in range(GT):
                            add0(n - GT, ws, k)
            v.sem_inc(e0["added"], 1)
            bodies(v, edges0)
            ws = windows(mybir.EngineType.DVE, TILES - GT)
            for k in range(GT):
                add0(TILES - GT, ws, k)
            barrier(v, B_E0)

            v.wait_ge(n1["loads"], 80)
            v.tensor_tensor(brz, brz, brzh, ALU.add).then_inc(n1["vstep"], 1)
            v.wait_ge(n1["vstep"], 1)

            def update0(i):
                for s in range(2):
                    b = i * 2 + s
                    st = Steps(v, n1["vstep"], b, 7, 1)
                    v.wait_ge(n1["gate_psum"], b + 1)
                    hold(v)
                    v.tensor_tensor(rz[s], banks[2 + s][:, :], brz, ALU.add).then_inc(n1["rz_pre"], 1)
                    st(v.tensor_tensor(gt, banks[4 + s][:, 256:512], bhn, ALU.add))
                    v.wait_ge(n1["rz"], b + 1)
                    st(v.tensor_tensor(gt, gt, rz[s][:, 0:256], ALU.mult))
                    st(v.tensor_tensor(gt, gt, banks[4 + s][:, 0:256], ALU.add))
                    v.tensor_tensor(cand[s], gt, bxn, ALU.add).then_inc(n1["n_pre"], 1)
                    v.wait_ge(n1["n"], b + 1)
                    st(v.tensor_tensor(gt, gh[s], cand[s], ALU.subtract))
                    st(v.tensor_tensor(gt, gt, rz[s][:, 256:512], ALU.mult))
                    st(v.tensor_tensor(gt, gt, cand[s], ALU.add))
                    need(v, n1_out[s], i, 0, i * 16)
                    hold(v)
                    v.tensor_tensor(newx[s], gt, gx[s], ALU.add).then_inc(n1["x1"], 1)
                    v.wait_ge(n1["x1"], b + 1)
                    st(v.bn_stats(bst[:, bass.ds(b, 1), :].rearrange("p a c -> p (a c)"), newx[s]))
                    st.end()
            pairs(v, update0)
            stats_v(Steps(v, n1["vstep"], 0, 0, 1 + 7 * BLOCKS), pr["var"], pr["root"], 2)
            barrier(v, B_N1)

            v.wait_ge(n2["loads"], 32)

            def entry(i):
                for s in range(2):
                    b = i * 2 + s
                    v.wait_ge(n2["h"], b + 1)
                    need(v, n2_b[s], i, 0, i * 16)
                    hold(v)
                    v.tensor_tensor(ibase[s], ix[s], ih[s], ALU.add).then_inc(n2["base"], 1)
                    v.wait_ge(n2["hid_psum"], b + 1)
                    need(v, n2_h[s], i, 0, i * 16)
                    hold(v)
                    v.tensor_tensor(ihid[s], banks[2 + s][:, 0:HID], ib, ALU.add).then_inc(n2["hid"], 1)
            pairs(v, entry)
            barrier(v, B_N2)

            v.sem_inc(e1["added"], 1)
            with v.Fori(0, LAYERS) as l:
                v.wait_ge(pa["loads"], l * 64 + 64)
                hold(v)

                def project(i):
                    for s in range(2):
                        b, n = i * 2 + s, l * BLOCKS + i * 2
                        v.wait_ge(pa["q_psum"], n + (s + 1))
                        hold(v)
                        q = banks[2 + s][:, :].rearrange("p (h w n) -> p w h n", h=HEADS, w=WPB)
                        bias = bq.unsqueeze(1).unsqueeze(3).broadcast_to([P, WPB, HEADS, WIN])
                        for z in range(2):
                            ps = slice(64 * z, 64 * z + 64)
                            v.tensor_tensor(QT[ps, bass.ds(b * WPB, WPB), z, :, :], q[ps], bias[ps], ALU.add
                                            ).then_inc(pa["q"], 1)
                        v.wait_ge(pa["kv_psum"], n + (s + 1))
                        if not isinstance(i, int):
                            v.wait_ge(pa_out[s], (l * HALF + i) * 16)
                        hold(v)
                        v.tensor_tensor(akv[s], banks[4 + s][:, :], bkv, ALU.add).then_inc(pa["kv"], 1)
                pairs(v, project)
                layer_barrier(v, l, 1)

                def softmax_tail(n, groups):
                    v.wait_ge(e1["exp"], l * GROUPS + groups)
                    hold(v)
                    st = Steps(v, e1["vgroup"], l * GROUPS + (groups - 1), 3)
                    st(v.tensor_reduce(sm, ex.rearrange("p k (g h) -> p k h g", g=HEADS), AX.X, ALU.add))
                    st(v.reciprocal(smf, smf))
                    st(v.tensor_tensor(att.rearrange("p k (g h) -> p k g h", g=HEADS),
                                       ex.rearrange("p k (g h) -> p k g h", g=HEADS),
                                       sm.unsqueeze(2).broadcast_to([P, GT, HEADS, HEADS]), ALU.mult))

                def spread(n, g, k):
                    v.tensor_tensor(A[:, k, :, :], att[:, k, :].unsqueeze(2).broadcast_to([P, 16, WIN]),
                                    pk[g][:, k, 0:WIN].unsqueeze(1).broadcast_to([P, 16, WIN]), ALU.mult
                                    ).then_inc(e1["a"], 1)

                def add1(n, ws, k):
                    if k % 2 == 0:
                        v.wait_ge(e1["o_psum"], n + (k + 2))
                    v.wait_ge(e1["added"], n + (k + 1))
                    v.tensor_tensor(acc1[:, bass.ds(ws[k], 1), :], acc1[:, bass.ds(ws[k], 1), :],
                                    sum_bank(k)[:, DH * (k % 2):DH * (k % 2 + 1)].unsqueeze(1), ALU.add
                                    ).then_inc(e1["added"], 1)

                def edges1(it):
                    for g in range(RING):
                        t = it * BODY + g * GT
                        n = l * TILES + t
                        first = isinstance(it, int) and g == 0
                        if not first:
                            softmax_tail(n, it * RING + g)
                            for k in range(GT):
                                spread(n, (g - 1) % RING, k)
                        v.wait_ge(e1_pk[g], (l * ITERS + it) * 16 + 16)
                        hold(v)
                        for k in range(GT):
                            v.wait_ge(e1["s_psum"], n + (k + 1))
                            v.tensor_reduce(sc[:, k, :], banks[2 + k][:, :].rearrange("p (c n) -> p c n", n=WIN),
                                            AX.X, ALU.max).then_inc(e1["s_read"], 1)
                            if not first:
                                if k == 0:
                                    ws = windows(mybir.EngineType.DVE, t - GT)
                                elif k < 3:
                                    add1(n - GT, ws, k - 1)
                        v.wait_ge(e1["s_read"], n + GT)
                        v.tensor_reduce(mx, sc.rearrange("p k (g h) -> p k h g", g=HEADS), AX.X, ALU.max
                                        ).then_inc(e1["vstep"], 1)
                        v.wait_ge(e1["vstep"], l * GROUPS + it * RING + (g + 1))
                        v.tensor_tensor(ex.rearrange("p k (g h) -> p k g h", g=HEADS),
                                        sc.rearrange("p k (g h) -> p k g h", g=HEADS),
                                        mx.unsqueeze(2).broadcast_to([P, GT, HEADS, HEADS]), ALU.subtract
                                        ).then_inc(e1["shifted"], 1)
                        if not first:
                            for k in range(2, GT):
                                add1(n - GT, ws, k)
                bodies(v, edges1)
                softmax_tail(l * TILES + TILES, GROUPS)
                for k in range(GT):
                    spread(l * TILES + TILES, RING - 1, k)
                ws = windows(mybir.EngineType.DVE, TILES - GT)
                for k in range(GT):
                    add1(l * TILES + (TILES - GT), ws, k)
                layer_barrier(v, l, 2)

                def output(i):
                    for s in range(2):
                        b, n = i * 2 + s, l * BLOCKS + i * 2
                        v.wait_ge(pb["m_psum"], n + (s + 1))
                        v.wait_ge(pb_in[s], (l * HALF + i) * 32 + 32)
                        if not isinstance(i, int):
                            v.wait_ge(pb_out[s], (l * HALF + i) * 16)
                        hold(v)
                        v.tensor_tensor(cy[s], banks[2 + s][:, 0:HID], ch[s], ALU.add).then_inc(pb["y"], 1)
                        v.wait_ge(pb["y"], n + (s + 1))
                        v.bn_stats(bst[:, bass.ds(b, 1), :].rearrange("p a c -> p (a c)"), cy[s]
                                   ).then_inc(pb["vstep"], 1)
                pairs(v, output)
                v.wait_ge(pb["vstep"], l * BLOCKS + BLOCKS)
                hold(v)
                stats_v(Steps(v, pb["vstat"], l, STAT_STEPS), pb["var"], pb["root"], l + 1)
                layer_barrier(v, l, 3)

                v.wait_ge(pc["loads"], l * 32 + 32)
                hold(v)

                def norm(i):
                    for s in range(2):
                        n = l * BLOCKS + i * 2
                        st = Steps(v, pc["vstep"], n + s, 1)
                        v.wait_ge(pc["t"], n + (s + 1))
                        if not isinstance(i, int):
                            v.wait_ge(pc_out[s], (l * HALF + i) * 16)
                        hold(v)
                        v.tensor_tensor(du[s], dt[s], lng, ALU.mult).then_inc(pc["u"], 1)
                        v.wait_ge(pc["u"], n + (s + 1))
                        st(v.tensor_tensor(du[s], du[s], lnb, ALU.add))
                        v.tensor_scalar(du[s], du[s], 0.0, None, ALU.max).then_inc(pc["o"], 1)
                pairs(v, norm)
                layer_barrier(v, l, 4)

            v.wait_ge(pf["loads"], 64)

            def last(i):
                for s in range(2):
                    b = i * 2 + s
                    st = Steps(v, pf["vstep"], b, 1)
                    v.wait_ge(pf["o_psum"], b + 1)
                    v.wait_ge(pf_in[s], i * 32 + 32)
                    need(v, pf_out[s], i, 0, i * 16)
                    hold(v)
                    st(v.tensor_tensor(fo[s], banks[4 + s][:, 0:HID], fbase[s], ALU.add))
                    v.tensor_tensor(fo[s], fo[s], fb2, ALU.add).then_inc(pf["o"], 1)
            pairs(v, last)

        @block.tensor
        def _(pe):
            mm = nc.tensor.matmul

            pe.wait_ge(pr["consts"], 1)
            pe.wait_ge(pr["tile_base"], 1)
            mm(banks[4][:, 0:NWIN], before[:, :], cnt, start=True, stop=True)
            mm(banks[4][:, P:P + NWIN], ones[:, :], cnt, start=True, stop=True).then_inc(pr["pre_psum"], 1)
            pe.wait_ge(pr["tile_base"], 2)
            nc.tensor.transpose(banks[5][0:NWIN, 0:P], tbi, ident[:, :]).then_inc(pr["base_psum"], 1)
            pe.wait_ge(pr["below"], 1)
            mm(banks[6][:, 0:TILES], ones[0:NWIN, :], lemat[0:NWIN, :], start=True, stop=True
               ).then_inc(pr["win_psum"], 1)
            pe.wait_ge(pr["weights"], 144)

            def nodes0(i):
                for s in range(2):
                    b = i * 2 + s
                    pe.wait_ge(n0["h"], b + 1)
                    for k in range(2):
                        t = nc.tensor.transpose(banks[s][:, P * k:P * (k + 1)], hb[s][:, P * k:P * (k + 1)],
                                                ident[:, :])
                    t.then_inc(n0["hT_psum"], 1)
                    pe.wait_ge(n0["hT"], b + 1)
                    if not isinstance(i, int):
                        pe.wait_ge(n0["pq"], (i * 2 + (s - 1)) * 5)
                    mm(banks[2 + s][:, :], hT[s][:, 0, :], wpq[:, 0, :], start=True, stop=False)
                    mm(banks[2 + s][:, :], hT[s][:, 1, :], wpq[:, 1, :], start=False, stop=False)
                    mm(banks[2 + s][:, :], ones[0:1, :], b1row, start=False, stop=True).then_inc(n0["pq_psum"], 1)
            pairs(pe, nodes0)
            barrier(pe, B_PREP)

            def need_sums(added, n, k):
                if isinstance(n, int) and n == 0:
                    return
                pe.wait_ge(added, n + (k - 1))

            def trans0(it, g, k):
                n = it * BODY + g * GT
                if k == 0:
                    pe.wait_ge(e0_rec[g], it * 16 + 16)
                if not (isinstance(it, int) and g == 0 and k < 2):
                    pe.wait_ge(e0["T"], n + (k - 1))
                nc.tensor.transpose(banks[k % 2][0:96, 0:P], rec[g][:, k, 0:96], ident[:, :]
                                    ).then_inc(e0["T_psum"], 1)

            def pre0(it, g, k, w):
                n = it * BODY + g * GT
                pe.wait_ge(e0["T"], n + (k + 1))
                if not (isinstance(it, int) and g == 0):
                    pe.wait_ge(e0["pre"], n + (k + 1 - GT))
                mm(banks[2 + k][:, 0:HID], lh[k % 2], big[0:96, bass.ds(w, 1), :].rearrange("p a n -> p (a n)"),
                   start=True, stop=True).then_inc(e0["pre_psum"], 1)

            def sums0(n, g):
                for k in range(GT):
                    pe.wait_ge(e0["act"], n + (k + 1))
                    if k % 2 == 0:
                        need_sums(e0["added"], n, k)
                    onehot = rec[g][:, k, R_OH:R_CNT]
                    sums = sum_bank(k)[:, 96 * (k % 2):96 * (k % 2 + 1)]
                    for f in range(2):
                        mm(sums[:, 32 * f:32 * (f + 1)], act[k][:, P * f:P * (f + 1)], onehot, start=True, stop=True)
                    mm(sums[:, 64:96], rec[g][:, k, :], onehot, start=True, stop=True).then_inc(e0["seg_psum"], 1)

            def edges0(it):
                for g in range(RING):
                    trans0(it, g, 0)
                    ws = windows(mybir.EngineType.PE, it * BODY + g * GT)
                    for k in range(GT):
                        if k + 1 < GT:
                            trans0(it, g, k + 1)
                        pre0(it, g, k, ws[k])
                    if not (isinstance(it, int) and g == 0):
                        sums0(it * BODY + (g - 1) * GT, (g - 1) % RING)
            bodies(pe, edges0)
            sums0(TILES - GT, RING - 1)
            barrier(pe, B_E0)

            def update0(i):
                for s in range(2):
                    b = i * 2 + s
                    need(pe, n1["aggT"], i, i * 2, s - 1)
                    for f in range(2):
                        dst, fs = banks[s][:, P * f:P * (f + 1)], slice(P * f, P * (f + 1))
                        for j in range(2):
                            mm(dst, w2l0[:, j, fs], acc0[:, bass.ds(b * WPB, WPB), 32 * j:32 * (j + 1)],
                               start=j == 0, stop=False)
                        t = mm(dst, b2x[:, fs], acc0[:, bass.ds(b * WPB, WPB), 64:96], start=False, stop=True)
                    t.then_inc(n1["agg_psum"], 1)
                    pe.wait_ge(n1["aggT"], b + 1)
                    pe.wait_ge(n1_in[s], i * 48 + 48)
                    need(pe, n1["x1"], i, i * 2, s - 1)
                    for j, (src, w) in enumerate(((aggT[s], 0), (aggT[s], 1), (ghT[s], 2), (ghT[s], 3))):
                        mm(banks[2 + s][:, :], src[:, j % 2, :], wgate[:, w, 0:512], start=j == 0, stop=j == 3)
                    for part in range(2):
                        src = (aggT, ghT)[part][s]
                        for j in range(2):
                            t = mm(banks[4 + s][:, 256 * part:256 * (part + 1)], src[:, j, :],
                                   wgate[:, 2 * part + j, 512:768], start=j == 0, stop=j == 1)
                    t.then_inc(n1["gate_psum"], 1)
            pairs(pe, update0)
            barrier(pe, B_N1)

            pe.wait_ge(n2["loads"], 32)

            def entry(i):
                for s in range(2):
                    b = i * 2 + s
                    pe.wait_ge(n2["h"], b + 1)
                    need(pe, n2["hT"], i, i * 2, s - 1)
                    for k in range(2):
                        t = nc.tensor.transpose(banks[s][:, P * k:P * (k + 1)], ih[s][:, P * k:P * (k + 1)],
                                                ident[:, :])
                    t.then_inc(n2["hT_psum"], 1)
                    pe.wait_ge(n2["hT"], b + 1)
                    need(pe, n2["hid"], i, i * 2, s - 1)
                    mm(banks[2 + s][:, 0:HID], ihT[s][:, 0, :], iw[:, 0, :], start=True, stop=False)
                    mm(banks[2 + s][:, 0:HID], ihT[s][:, 1, :], iw[:, 1, :], start=False, stop=True
                       ).then_inc(n2["hid_psum"], 1)
            pairs(pe, entry)
            barrier(pe, B_N2)

            with pe.Fori(0, LAYERS) as l:
                pe.wait_ge(pa["loads"], l * 64 + 64)
                hold(pe)

                def project(i):
                    for s in range(2):
                        n = l * BLOCKS + i * 2
                        pe.wait_ge(pa_in[s], (l * HALF + i) * 16 + 16)
                        need(pe, pa["hT"], i, n, s - 1)
                        for k in range(2):
                            t = nc.tensor.transpose(banks[s][:, P * k:P * (k + 1)], ah[s][:, P * k:P * (k + 1)],
                                                    ident[:, :])
                        t.then_inc(pa["hT_psum"], 1)
                        pe.wait_ge(pa["hT"], n + (s + 1))
                        if not isinstance(i, int):
                            pe.wait_ge(pa["q"], (n + (s - 1)) * 2)
                        for h in range(HEADS):
                            for k in range(2):
                                t = mm(banks[2 + s][:, P * h:P * (h + 1)], wq[:, k, h, :], ahT[s][:, k, :],
                                       start=k == 0, stop=k == 1)
                        t.then_inc(pa["q_psum"], 1)
                        need(pe, pa["kv"], i, n, s - 1)
                        for k in range(2):
                            t = mm(banks[4 + s][:, :], ahT[s][:, k, :], wkv[:, k, :], start=k == 0, stop=k == 1)
                        t.then_inc(pa["kv_psum"], 1)
                pairs(pe, project)
                layer_barrier(pe, l, 1)

                def trans1(it, g, k):
                    n = l * TILES + it * BODY + g * GT
                    if k == 0:
                        pe.wait_ge(e1_kv[g], (l * ITERS + it + 1) * (16 * GT))
                    if not (isinstance(it, int) and g == 0 and k < 2):
                        pe.wait_ge(e1["T"], n + (k - 1))
                    for j in range(2):
                        t = nc.tensor.transpose(banks[k % 2][:, P * j:P * (j + 1)],
                                                kv[g * GT + k][:, P * j:P * (j + 1)], ident[:, :])
                    t.then_inc(e1["T_psum"], 1)

                def scores(it, g, k, w):
                    n = l * TILES + it * BODY + g * GT
                    if k == 0:
                        pe.wait_ge(e1_mk[g], (l * ITERS + it) * 16 + 16)
                    if not (isinstance(it, int) and g == 0):
                        pe.wait_ge(e1["s_read"], n + (k + 1 - GT))
                    pe.wait_ge(e1["T"], n + (k + 1))
                    hold(pe)
                    mm(banks[2 + k][:, :], mk[g][:, P * k:P * (k + 1)], neg[:, :], start=True, stop=False)
                    q = big[:, bass.ds(w, 1), :].rearrange("p a n -> p (a n)")
                    for j in range(2):
                        m = mm(banks[2 + k][:, 256 * j:256 * (j + 1)], kT[k % 2][:, P * j:P * (j + 1)], q,
                               start=False, stop=j == 1)
                    m.then_inc(e1["s_psum"], 1)

                def messages(t, g):
                    n = l * TILES + t
                    for k in range(GT):
                        pe.wait_ge(e1["a"], n + (k + 1))
                        if k % 2 == 0 and not (isinstance(t, int) and t == 0):
                            pe.wait_ge(e1["added"], n + (k - 1))
                        for j in range(HEADS):
                            m = mm(sum_bank(k)[:, DH * (k % 2):DH * (k % 2 + 1)],
                                   A[:, k, HEADS * j:HEADS * (j + 1), :].rearrange("p h n -> p (h n)"),
                                   kv[g * GT + k][:, HID + DH * j:HID + DH * (j + 1)], start=j == 0,
                                   stop=j == HEADS - 1)
                        m.then_inc(e1["o_psum"], 1)

                def edges1(it):
                    for g in range(RING):
                        trans1(it, g, 0)
                        ws = windows(mybir.EngineType.PE, it * BODY + g * GT)
                        for k in range(GT):
                            if k + 1 < GT:
                                trans1(it, g, k + 1)
                            scores(it, g, k, ws[k])
                        if not (isinstance(it, int) and g == 0):
                            messages(it * BODY + (g - 1) * GT, (g - 1) % RING)
                bodies(pe, edges1)
                messages(TILES - GT, RING - 1)
                layer_barrier(pe, l, 2)

                pe.wait_ge(pb["loads"], l * 48 + 48)
                hold(pe)
                for h in range(HEADS):
                    mm(banks[7][0:4, 0:HID], eeT[:, h, :], wo[:, h, :], start=h == 0, stop=False)
                mm(banks[7][0:4, 0:HID], ident[0:1, 0:4], borow, start=False, stop=True).then_inc(pb["eb_psum"], 1)
                pe.wait_ge(pb["eb"], l + 1)
                hold(pe)

                def output(i):
                    for s in range(2):
                        n = l * BLOCKS + i * 2
                        pe.wait_ge(pb["staged"], n + (s + 1))
                        need(pe, pb["aT"], i, n, s - 1)
                        hold(pe)
                        for w in range(WPB):
                            t = nc.tensor.transpose(banks[s][0:DH, P * w:P * (w + 1)], cst[s][:, w, :], ident[:, :])
                        t.then_inc(pb["T_psum"], 1)
                        pe.wait_ge(pb["aT"], n + (s + 1))
                        pe.wait_ge(pb_in[s], (l * HALF + i) * 32 + 32)
                        need(pe, pb["y"], i, n, s - 1)
                        hold(pe)
                        for h in range(HEADS):
                            mm(banks[2 + s][:, 0:HID], cT[s][:, h, :], wo[:, h, :], start=h == 0, stop=False)
                        mm(banks[2 + s][:, 0:HID], cc[s], eb, start=False, stop=True).then_inc(pb["m_psum"], 1)
                pairs(pe, output)
                layer_barrier(pe, l, 3)
                layer_barrier(pe, l, 4)

            pe.wait_ge(pf["loads"], 64)

            def last(i):
                for s in range(2):
                    b = i * 2 + s
                    pe.wait_ge(pf_in[s], i * 32 + 32)
                    need(pe, pf["hT"], i, i * 2, s - 1)
                    for k in range(2):
                        t = nc.tensor.transpose(banks[s][:, P * k:P * (k + 1)], fh[s][:, P * k:P * (k + 1)],
                                                ident[:, :])
                    t.then_inc(pf["hT_psum"], 1)
                    pe.wait_ge(pf["hT"], b + 1)
                    for f in range(2):
                        for k in range(2):
                            t = mm(banks[2 + s][:, P * f:P * (f + 1)], fw1[:, k, P * f:P * (f + 1)], fhT[s][:, k, :],
                                   start=k == 0, stop=k == 1)
                    t.then_inc(pf["u_psum"], 1)
                    pe.wait_ge(pf["u"], (b + 1) * 2)
                    need(pe, pf["o"], i, i * 2, s - 1)
                    for k in range(2):
                        t = mm(banks[4 + s][:, 0:HID], fuT[s][:, k, :], fw2[:, k, :], start=k == 0, stop=k == 1)
                    t.then_inc(pf["o_psum"], 1)
            pairs(pe, last)


def kernel(x, src, dst, edge_attr_64, edge_type_3, L0_gnn_W1, L0_gnn_b1, L0_gnn_W2, L0_gnn_b2, L0_gnn_W_ih,
           L0_gnn_b_ih, L0_gnn_W_hh, L0_gnn_b_hh, L1_gnn_Win, L1_gnn_b_in, L1_gnn_Wq, L1_gnn_bq, L1_gnn_Wk,
           L1_gnn_bk, L1_gnn_Wv, L1_gnn_bv, L1_gnn_Eemb, L1_gnn_Wo, L1_gnn_bo, L1_gnn_ln_g, L1_gnn_ln_b, L1_gnn_W1,
           L1_gnn_b1, L1_gnn_W2, L1_gnn_b2):
    import numpy as np
    import concourse.bacc as bacc
    from concourse.bass_utils import run_bass_kernel_spmd

    def arr(v):
        return np.asarray(v)

    def edge_columns(v, fill):
        return np.concatenate([arr(v), np.full(EPAD - EDGES, fill, np.int32)]).reshape(P, COLS)

    def halves(wT):
        return wT.reshape(2, P, -1).transpose(1, 0, 2)

    def layers_T(w):
        return arr(w).transpose(0, 2, 1)

    W1 = arr(L0_gnn_W1)
    b1_row = np.zeros((1, 512), np.float32)
    b1_row[0, 0:HID] = arr(L0_gnn_b1)
    b2_rows = np.zeros((P, HID), np.float32)
    b2_rows[R_CNT] = arr(L0_gnn_b2)
    wqT = layers_T(L1_gnn_Wq).reshape(LAYERS, 2, P, HEADS, DH).transpose(0, 2, 1, 3, 4)
    wkvT = np.concatenate([layers_T(L1_gnn_Wk), layers_T(L1_gnn_Wv)], 2)
    bq = arr(L1_gnn_bq).reshape(LAYERS, HEADS, DH).transpose(0, 2, 1)
    eT = np.zeros((LAYERS, DH, HEADS, 4), np.float32)
    eT[:, :, :, 1:] = arr(L1_gnn_Eemb).reshape(LAYERS, TYPES, HEADS, DH).transpose(0, 3, 2, 1)
    arrays = {
        "x": np.concatenate([arr(x), np.zeros((NPAD - NODES, HID), np.float32)]),
        "src": edge_columns(src, -1), "dst": edge_columns(dst, 0), "typ": edge_columns(edge_type_3, 0),
        "attr": np.concatenate([arr(edge_attr_64), np.zeros((EPAD - EDGES, ATTR), np.float32)]),
        "w_pq": halves(np.concatenate([W1[:, 0:HID].T, W1[:, HID:2 * HID].T], 1)),
        "w1_attr": W1[:, 2 * HID:].T, "b1_row": b1_row,
        "w2_l0": halves(arr(L0_gnn_W2).T), "b2_rows": b2_rows,
        "w_gate": np.concatenate([halves(arr(L0_gnn_W_ih).T), halves(arr(L0_gnn_W_hh).T)], 1),
        "b_ih": arr(L0_gnn_b_ih), "b_hh": arr(L0_gnn_b_hh),
        "w_in": halves(arr(L1_gnn_Win).T), "b_in": arr(L1_gnn_b_in),
        "w_q": np.concatenate([wqT, wqT], 4).reshape(LAYERS * P, -1),
        "b_q": np.concatenate([bq, bq], 1).reshape(LAYERS * P, HEADS),
        "w_kv": wkvT.reshape(LAYERS, 2, P, 512).transpose(0, 2, 1, 3).reshape(LAYERS * P, -1),
        "b_kv": np.concatenate([arr(L1_gnn_bk), arr(L1_gnn_bv)], 1),
        "w_o": layers_T(L1_gnn_Wo).reshape(LAYERS, HEADS, DH, HID).transpose(0, 2, 1, 3).reshape(LAYERS * DH, -1),
        "e_T": eT.reshape(LAYERS * DH, -1), "b_o": arr(L1_gnn_bo),
        "ln_g": arr(L1_gnn_ln_g), "ln_b": arr(L1_gnn_ln_b),
        "w_f1": halves(arr(L1_gnn_W1).T), "b_f1": arr(L1_gnn_b1).reshape(2, P).T,
        "w_f2": halves(arr(L1_gnn_W2).T), "b_f2": arr(L1_gnn_b2),
    }
    arrays = {f"in_{k}": np.ascontiguousarray(v) for k, v in arrays.items()}
    nc = bacc.Bacc("TRN2", target_bir_lowering=False, num_devices=1)
    a = {k[3:]: nc.dram_tensor(k, v.shape, mybir.dt.from_np(v.dtype), kind="ExternalInput").ap()
         for k, v in arrays.items()}
    out = nc.dram_tensor("out", (NPAD, HID), F32, kind="ExternalOutput").ap()
    gnn(nc, a, out)
    r = run_bass_kernel_spmd(nc, [arrays], core_ids=[0])
    return r.results[0]["out"][:NODES]
```

```python
from contextlib import ExitStack

import concourse.bass as bass
from concourse import mybir

F32 = mybir.dt.float32
BF16 = mybir.dt.bfloat16
I32 = mybir.dt.int32
ALU = mybir.AluOpType
ACT = mybir.ActivationFunctionType
AX = mybir.AxisListType

P = 128
NODES, HID, EDGES, ATTR = 3125, 256, 50000, 64
HEADS, DH, LAYERS, TYPES = 4, 64, 3, 3
WIN = 16
WIN0 = 32
BLOCKS = 26
NPAD = BLOCKS * P
NWIN = NPAD // WIN
WPB = P // WIN
NWIN0, WPB0 = NWIN // 2, WPB // 2
RWIN = -(-NODES // WIN)
GT = 4
RING = 4
BODY = GT * RING
NEED = (EDGES + RWIN * (P - 1)) // P
ITERS = -(-NEED // BODY)
TILES = ITERS * BODY
TH = TILES // 2
GROUPS = TILES // GT
ROWS = TILES * P
COLS = 392
EPAD = P * COLS
CH = 7
CHUNKS = COLS // CH
QC = 56
NQ = COLS // QC
WPP = 13
PARTS = NWIN // WPP
QFIRST = 4
REC = 128
R_OH0, R_OH, R_CNT, R_DST, R_END = 64, 96, 112, 116, 117
PK = R_END - R_OH
FAR = 1 << 22
NEGB = -(2.0 ** 100)
B_PREP, B_E0, B_N1, B_N2, PER_LAYER = 1, 2, 3, 4, 4
EPS = 1e-5


def gnn(nc, a, out):
    ctx = ExitStack()
    with ctx:
        def sb(name, shape, dt=F32):
            return ctx.enter_context(nc.sbuf_tensor(name, shape, dt))

        def sem(name):
            return ctx.enter_context(nc.semaphore(name))

        def sems(name, n):
            return [sem(f"{name}{i}") for i in range(n)]

        def dram(name, shape, dt=F32):
            return nc.dram_tensor(name, shape, dt).ap()

        rect = dram("edge_records", (ROWS, REC))
        packd = dram("edge_packs", (GROUPS, P, GT * PK))
        maskd = dram("edge_masks", (GROUPS, WIN, GT * P), BF16)
        qrows = dram("dst_rows", (NPAD, HID))
        kvrows = dram("kv_rows", (NPAD, 2 * HID))
        h0d = dram("h0", (NPAD, HID))
        h0Td = dram("h0T", (NPAD, HID))
        x1d = dram("x1", (NPAD, HID))
        based = dram("base", (NPAD, HID))
        hidd = dram("hidden", (NPAD, HID))
        yd = dram("y", (NPAD, HID))
        cntd = dram("counts", (4, NPAD))

        big = sb("big", [P, NWIN0, HID])
        work = sb("work", [P, NWIN0 * 96 + 6144])
        accr, node = work[:, 0:NWIN0 * 96], work[:, NWIN0 * 96:]
        ring = sb("ring", [P, BODY * 2 * HID])
        side = sb("side", [P, GT * HID])
        ident = sb("ident", [P, P])
        neg = sb("neg", [WIN, 4 * HEADS * WIN], BF16)
        wtab = sb("wtab", [P, TILES], I32)
        bst = sb("bst", [P, BLOCKS, 6])
        st4 = sb("st4", [P, 8, BLOCKS])
        rstd, nmr = st4[:, 0, :], st4[:, 1, :]
        banks = [ctx.enter_context(nc.psum_tensor(f"bank{i}", [P, 512], F32)) for i in range(8)]

        def at(region, off, *shape, parts=P):
            n = 1
            for d in shape:
                n *= d
            v = region[0:parts, off:off + n]
            if len(shape) == 2:
                v = v.rearrange("p (a b) -> p a b", a=shape[0])
            elif len(shape) == 3:
                v = v.rearrange("p (a b c) -> p a b c", a=shape[0], b=shape[1])
            return v

        phase_end, entered = sem("phase_end"), sem("entered")

        def events(phase, words):
            return {w: sem(f"{phase}_{w}") for w in words.split()}

        block = ctx.enter_context(nc.Block())

        def need(eng, s, i, base, count, peeled=0):
            if isinstance(i, int) and i == 0 and peeled + count <= 0:
                return
            eng.wait_ge(s, base + count)

        def hold(eng):
            eng.sem_inc(entered, 1)

        def barrier(eng, n):
            hold(eng)
            eng.drain().then_inc(phase_end, 1)
            eng.wait_ge(phase_end, n * 5)
            hold(eng)

        def layer_barrier(eng, l, k):
            barrier(eng, l * PER_LAYER + (B_N2 + k))

        def pairs(eng, body):
            body(0)
            with eng.Fori(1, BLOCKS // 2) as i:
                body(i)

        def bodies(eng, body):
            body(0)
            with eng.Fori(1, ITERS) as it:
                body(it)

        class Steps:

            def __init__(self, eng, s, n=0, per=0, base=0):
                self.eng, self.s, self.start, self.per, self.c = eng, s, n * per + base, per, 0

            def __call__(self, ins):
                ins.then_inc(self.s, 1)
                self.c += 1
                self.eng.wait_ge(self.s, self.start + self.c)

            def end(self):
                assert self.per in (0, self.c), (self.c, self.per)
                return self.c

        def rows(t, b, n=P):
            return t[bass.ds(b * P, n), :]

        def row_of(v):
            return v.rearrange("(a n) -> a n", a=1).broadcast_to([P, v.shape[0]])

        win = accr[:, 0:392]
        loc = accr[:, 392:784]
        typ = accr[:, 784:1176]
        pen = accr[:, 1176:1568]
        dsti = accr[:, 1568:1960].bitcast(I32)
        srci = accr[:, 1960:2352].bitcast(I32)
        typi = accr[:, 2352:2744].bitcast(I32)
        pos = accr[:, 2744:3136]
        loc0 = accr[:, 3136:3528]
        off, cnt, ntl, tbi, zrow = (accr[:, 3528 + NWIN * i:3528 + NWIN * (i + 1)] for i in range(5))
        toti = accr[:, 4568:4568 + NWIN].bitcast(I32)
        PE1 = QC + 1
        hot = at(accr, 4776, WPP, PE1)
        hotf = accr[:, 4776:4776 + WPP * PE1]
        run = at(accr, 5517, WPP, PE1)
        runf = accr[:, 5517:5517 + WPP * PE1]
        lemat = [accr[0:NWIN // 2, 4776 + TILES * z:4776 + TILES * (z + 1)] for z in range(2)]
        prod = at(accr, 6258, WPP, QC)
        psum_pos = accr[:, 6986:7042]
        keep = at(accr, 7042, WPP, PE1)
        keepf = accr[:, 7042:7042 + WPP * PE1]
        recc = [at(accr, 7783 + s * CH * REC, CH, REC) for s in range(2)]
        iwin = accr[:, 9575:9575 + NWIN]
        slot = [accr[:, 9784 + 8 * s:9784 + 8 * s + CH].bitcast(I32) for s in range(2)]
        ni, na, nb = (accr[:, 9800 + 8 * i:9800 + 8 * i + CH].bitcast(I32) for i in range(3))
        tcol = [accr[0:NWIN // 2, 9824 + z:9825 + z] for z in range(2)]
        iloc = accr[:, 9832:9832 + WIN0]
        ityp = accr[:, 9864:9867]
        itile = ring[:, BODY * REC:BODY * REC + TILES]
        wtab0 = node[0:1, 4608:4608 + TILES].bitcast(I32)
        ones, before = node[:, 4096:4096 + P], node[:, 5216:5216 + P]
        blank = at(ring, 0, BODY, REC)
        wgate = at(ring, BODY * HID, 4, 768)
        w2l0 = at(node, 5376, 2, HID)
        b2x = node[:, 5888:6144]
        wpq = at(node, 0, 2, 512)
        b1row = node[0:1, 1024:1536]
        xb = [node[:, 1536 + 256 * s:1792 + 256 * s] for s in range(2)]
        hb = [node[:, 2048 + 256 * s:2304 + 256 * s] for s in range(2)]
        hT = [at(node, 2560 + 256 * s, 2, P) for s in range(2)]
        hTf = [node[:, 2560 + 256 * s:2816 + 256 * s] for s in range(2)]
        qst = [node[:, 3072 + 256 * s:3328 + 256 * s] for s in range(2)]
        xs = [node[:, 3584 + 256 * s:3840 + 256 * s] for s in range(2)]
        rec = [at(node, 512 * g, GT, REC) for g in range(RING)]
        lh = [node[0:R_CNT, 2048 + P * k:2048 + P * (k + 1)] for k in range(GT)]
        pre = [node[:, 2560 + 256 * k:2816 + 256 * k] for k in range(GT)]
        act = [node[:, 3584 + 256 * k:3840 + 256 * k] for k in range(GT)]
        mk0 = [side[R_OH:R_CNT, 256 * g:256 * (g + 1)].bitcast(BF16) for g in range(RING)]
        qg = [ring[:, HID * t:HID * (t + 1)] for t in range(BODY)]
        acc0 = at(accr, 0, NWIN0, 96)
        E = NWIN * DH - NWIN0 * 96
        A = node[:, E:E + 1024].rearrange("p (k c n) -> p k c n", k=GT, c=16)
        pk = [at(node, E + 1024 + GT * PK * g, GT, PK) for g in range(RING)]
        pkf = [node[:, E + 1024 + GT * PK * g:E + 1024 + GT * PK * (g + 1)] for g in range(RING)]
        mk = [node[0:WIN, E + 1360 + 256 * g:E + 1616 + 256 * g].bitcast(BF16) for g in range(RING)]
        kT = [side[:, HID * k:HID * (k + 1)] for k in range(GT)]
        sc = at(node, E + 2384, GT, 16)
        ex = at(node, E + 2448, GT, 16)
        exf = node[:, E + 2448:E + 2512]
        att = at(node, E + 2512, GT, 16)
        mx = at(node, E + 2576, GT, HEADS)
        sm = at(node, E + 2592, GT, HEADS)
        smf = node[:, E + 2592:E + 2608]
        kv = [ring[:, 2 * HID * t:2 * HID * (t + 1)] for t in range(BODY)]
        acc1 = at(work, 0, NWIN, DH, parts=DH)

        ghT = [at(node, 256 * s, 2, P) for s in range(2)]
        ghTf = [node[:, 256 * s:256 * s + 256] for s in range(2)]
        gh = [node[:, 512 + 256 * s:768 + 256 * s] for s in range(2)]
        gx = [node[:, 1024 + 256 * s:1280 + 256 * s] for s in range(2)]
        aggT = [at(node, 1536 + 256 * s, 2, P) for s in range(2)]
        aggTf = [node[:, 1536 + 256 * s:1792 + 256 * s] for s in range(2)]
        rz = [node[:, 2048 + 512 * s:2560 + 512 * s] for s in range(2)]
        cand = [node[:, 3072 + 256 * s:3328 + 256 * s] for s in range(2)]
        newx = [node[:, 3584 + 256 * s:3840 + 256 * s] for s in range(2)]
        gt = node[:, 4096:4352]
        brz, brzh = ring[:, 0:512], ring[:, 512:1024]
        bxn, bhn = ring[:, 1024:1280], ring[:, 1280:1536]
        iw = at(node, 0, 2, HID)
        ib = node[:, 512:768]
        ix = [node[:, 768 + 256 * s:1024 + 256 * s] for s in range(2)]
        ih = [node[:, 1280 + 256 * s:1536 + 256 * s] for s in range(2)]
        ihT = [at(node, 1792 + 256 * s, 2, P) for s in range(2)]
        ihTf = [node[:, 1792 + 256 * s:2048 + 256 * s] for s in range(2)]
        ibase = [node[:, 2304 + 256 * s:2560 + 256 * s] for s in range(2)]
        ihid = [node[:, 2816 + 256 * s:3072 + 256 * s] for s in range(2)]
        wq = node[:, 0:1024].rearrange("p (k h m) -> p k h m", k=2, h=HEADS)
        wkv = at(node, 1024, 2, 512)
        bq = node[:, 2048:2052]
        bkv = node[:, 2052:2564]
        ah = [node[:, 2564 + 256 * s:2820 + 256 * s] for s in range(2)]
        ahT = [at(node, 3076 + 256 * s, 2, P) for s in range(2)]
        ahTf = [node[:, 3076 + 256 * s:3332 + 256 * s] for s in range(2)]
        akv = [node[:, 3588 + 512 * s:4100 + 512 * s] for s in range(2)]
        QT = big[:, :, :].rearrange("p v (w g h n) -> p (v w) g h n", w=2, g=2, h=HEADS)
        QW = big[:, :, :].rearrange("p v (w f) -> p (v w) f", w=2)
        wo = at(ring, 0, HEADS, HID, parts=DH)
        eeT = at(ring, 1024, HEADS, 4, parts=DH)
        borow = ring[0:1, 1040:1296]
        eb = ring[0:4, 1296:1552]
        cst = [at(ring, 1552 + 512 * s, HEADS, P, parts=DH) for s in range(2)]
        cc = [ring[0:4, 2576 + P * s:2576 + P * (s + 1)] for s in range(2)]
        ch = [ring[:, 2832 + 256 * s:3088 + 256 * s] for s in range(2)]
        cy = [ring[:, 3344 + 256 * s:3600 + 256 * s] for s in range(2)]
        lng, lnb = node[:, 0:256], node[:, 256:512]
        dy = [node[:, 512 + 256 * s:768 + 256 * s] for s in range(2)]
        dt = [node[:, 1024 + 256 * s:1280 + 256 * s] for s in range(2)]
        du = [node[:, 1536 + 256 * s:1792 + 256 * s] for s in range(2)]
        fw1, fw2 = at(node, 0, 2, HID), at(node, 512, 2, HID)
        fb1, fb2 = node[:, 1024:1026], node[:, 1026:1282]
        fh = [node[:, 1282 + 256 * s:1538 + 256 * s] for s in range(2)]
        fhT = [at(node, 1794 + 256 * s, 2, P) for s in range(2)]
        fhTf = [node[:, 1794 + 256 * s:2050 + 256 * s] for s in range(2)]
        fuT = [at(node, 2306 + 256 * s, 2, P) for s in range(2)]
        fbase = [node[:, 2818 + 256 * s:3074 + 256 * s] for s in range(2)]
        fo = [node[:, 3330 + 256 * s:3586 + 256 * s] for s in range(2)]

        pr = events("pr", "consts idx weights x_read var root norm cnt pre_psum tile_base base_psum below win_psum "
                          "blank cleared rec pool vstep rstep")
        pr_x, pr_attr, pr_scat = (sems(f"pr_{w}", 2) for w in ("x", "attr", "scat"))
        n0 = events("n0", "h hT_psum hT pq_psum pq")
        n0_x, n0_h, n0_hT, n0_q = (sems(f"n0_{w}", 2) for w in ("x", "hst", "hTst", "qst"))
        e0 = events("e0", "T_psum T pre_psum pre act seg_psum added mask vstep ")
        e0_rec, e0_store = (sems(f"e0_{w}", RING) for w in ("rec", "store"))
        e0_q = sems("e0_q", RING)
        n1 = events("n1", "loads agg_psum aggT gate_psum rz_pre rz n_pre n x1 vstep")
        n1_in, n1_out = sems("n1_in", 2), sems("n1_out", 2)
        n2 = events("n2", "loads h hT_psum hT hid_psum base hid")
        n2_x, n2_b, n2_h = (sems(f"n2_{w}", 2) for w in ("x", "bst", "hst"))
        pa = events("pa", "loads hT_psum hT q_psum kv_psum q kv")
        pa_in, pa_out = sems("pa_in", 2), sems("pa_out", 2)
        e1 = events("e1", "cleared T_psum T s_psum s_read shifted exp a o_psum added vstep vgroup")
        e1_in = sems("e1_in", RING)
        e1_kv = sems("e1_kv", RING)
        pb = events("pb", "loads eb_psum eb staged m_psum y vstep vstat var root")
        pb_in, pb_out = sems("pb_in", 2), sems("pb_out", 2)
        pc = events("pc", "loads t u o vstep")
        pc_in, pc_out = sems("pc_in", 2), sems("pc_out", 2)
        pf = events("pf", "loads hT_psum hT u_psum u o_psum o vstep")
        pf_in, pf_out = sems("pf_in", 2), sems("pf_out", 2)

        HALF = BLOCKS // 2

        def windows(engine, t, table, n):
            return nc.values_load_multi_w_load_instructions(
                table[0:1, bass.ds(t, GT)], engines=(engine,), min_val=0, max_val=n - 1,
                skip_runtime_bounds_check_because="the preparation cuts every entry at NWIN - 1")[1]

        def sum_bank(k):
            return banks[6 + k // 2]

        STAT_STEPS = 14

        def stats_v(step, var, root, n):
            v = nc.vector
            mean, var_, t0, t1, root_ = (st4[:, j, :] for j in range(2, 7))
            me, m2e, mo, m2o = bst[:, :, 1], bst[:, :, 2], bst[:, :, 4], bst[:, :, 5]
            step(v.tensor_tensor(t0, me, mo, ALU.subtract))
            step(v.tensor_tensor(mean, me, mo, ALU.add))
            step(v.tensor_scalar(mean, mean, 0.5, None, ALU.mult))
            step(v.tensor_scalar(t0, t0, 0.5, None, ALU.mult))
            step(v.tensor_tensor(t0, t0, t0, ALU.mult))
            step(v.tensor_tensor(t1, m2e, m2o, ALU.add))
            step(v.tensor_scalar(t1, t1, 1.0 / HID, EPS, ALU.mult, ALU.add))
            v.tensor_tensor(var_, t0, t1, ALU.add).then_inc(var, 1)
            v.wait_ge(root, n)
            step(v.reciprocal(rstd, root_))
            step(v.tensor_tensor(t0, rstd, rstd, ALU.mult))
            step(v.tensor_tensor(t0, t0, var_, ALU.mult))
            step(v.tensor_scalar(t0, t0, -0.5, 1.5, ALU.mult, ALU.add))
            step(v.tensor_tensor(rstd, rstd, t0, ALU.mult))
            step(v.tensor_tensor(t1, mean, rstd, ALU.mult))
            step(v.tensor_scalar(nmr, t1, -1.0, None, ALU.mult))

        def stats_a(var, root, n):
            nc.scalar.wait_ge(var, n)
            hold(nc.scalar)
            nc.scalar.activation(st4[:, 6, :], st4[:, 3, :], ACT.Sqrt).then_inc(root, 1)

        @block.sync
        def _(sp):
            def after(s, count):
                sp.wait_ge(s, count)
                hold(sp)

            def need_sp(s, i, base, count):
                if not (isinstance(i, int) and count <= 0):
                    after(s, base + count)

            for v, w in ((srci, "src"), (dsti, "dst"), (typi, "typ")):
                sp.dma_start(v, a[w]).then_inc(pr["idx"], 16)

            def load_x(i):
                for s in range(2):
                    need_sp(pr["x_read"], i, i * 2, s - 1)
                    sp.dma_start(xs[s], rows(a["x"], i * 2 + s)).then_inc(pr_x[s], 16)
            pairs(sp, load_x)
            for v, w in ((wpq, "w_pq"), (b1row, "b1_row"), (w2l0, "w2_l0"), (b2x, "b2_rows")):
                sp.dma_start(v, a[w]).then_inc(pr["weights"], 16)
            for half in range(4):
                sp.dma_start(wgate[:, half, :], a["w_gate"][:, half, :]).then_inc(pr["weights"], 16)
            sp.dma_start(big[0:ATTR, :, :], a["w1_attr"].unsqueeze(1).broadcast_to([ATTR, NWIN0, HID])
                         ).then_inc(pr["weights"], 16)

            def load_x_again(i):
                for s in range(2):
                    need_sp(n0["h"], i, i * 2, s - 1)
                    sp.dma_start(xb[s], rows(a["x"], i * 2 + s)).then_inc(n0_x[s], 16)

            def load_attr(i):
                for s in range(2):
                    if isinstance(i, int):
                        after(pr["cleared"], 1)
                    else:
                        after(pr_scat[s], i * (16 * CH))
                    sp.dma_start(recc[s][:, :, 0:ATTR], a["attr"].rearrange("(p c) f -> p c f", p=P)[
                        :, bass.ds(i * (2 * CH) + s * CH, CH), :]).then_inc(pr_attr[s], 16)
            load_attr(0)
            pairs(sp, load_x_again)
            with sp.Fori(1, CHUNKS // 2) as i:
                load_attr(i)
            after(pr["weights"], 144)
            barrier(sp, B_PREP)

            def load_records(it, g):
                if not isinstance(it, int):
                    after(e0["seg_psum"], it * BODY + (g + 1 - RING) * GT)
                    after(e0_store[g], it * 32)
                sp.dma_start(rec[g], rect[bass.ds((it * RING + g) * (GT * P), GT * P), :]
                             .rearrange("(p k) f -> p k f", k=GT)).then_inc(e0_rec[g], 16)

            def store_pack(it, g):
                after(e0_rec[g], it * 16 + 16)
                sp.dma_start(packd[bass.ds(it * RING + g, 1), :, :].rearrange("a p (k f) -> (a p) k f", k=GT),
                             rec[g][:, :, R_OH:R_END]).then_inc(e0_store[g], 16)
                after(e0["mask"], it * BODY + (g + 1) * GT)
                sp.dma_start(maskd[bass.ds(it * RING + g, 1), :, :].rearrange("a p f -> (a p) f"),
                             mk0[g]).then_inc(e0_store[g], 16)

            for g in range(RING):
                load_records(0, g)
            with sp.Fori(1, ITERS) as it:
                for g in range(RING):
                    store_pack(it - 1, g)
                    load_records(it, g)
            for g in range(RING):
                store_pack(ITERS - 1, g)
            for g in range(RING):
                after(e0_store[g], 32 * ITERS)
            barrier(sp, B_E0)

            sp.dma_start(cntd.rearrange("c (w n) -> c w n", n=WIN0), acc0[0:4, :, 64:96]
                         ).then_inc(n1["loads"], 16)
            for v, w in ((brz, a["b_ih"][0:512]), (brzh, a["b_hh"][0:512]), (bxn, a["b_ih"][512:768]),
                         (bhn, a["b_hh"][512:768])):
                sp.dma_start(v, row_of(w)).then_inc(n1["loads"], 16)

            def load_gate(i):
                for s in range(2):
                    b = i * 2 + s
                    need_sp(n1["x1"], i, i * 2, s - 1)
                    for v, t in ((ghTf[s], h0Td), (gh[s], h0d), (gx[s], a["x"])):
                        sp.dma_start(v, rows(t, b)).then_inc(n1_in[s], 16)
            pairs(sp, load_gate)
            after(n1["loads"], 80)
            barrier(sp, B_N1)

            sp.dma_start(iw, a["w_in"]).then_inc(n2["loads"], 16)
            sp.dma_start(ib, row_of(a["b_in"])).then_inc(n2["loads"], 16)

            def load_entry(i):
                for s in range(2):
                    need_sp(n2["base"], i, i * 2, s - 1)
                    sp.dma_start(ix[s], rows(x1d, i * 2 + s)).then_inc(n2_x[s], 16)
            pairs(sp, load_entry)
            barrier(sp, B_N2)

            with sp.Fori(0, LAYERS) as l:
                def lay(w):
                    return a[w][bass.ds(l * (a[w].shape[0] // LAYERS), a[w].shape[0] // LAYERS)]
                sp.dma_start(node[:, 0:1024], lay("w_q")).then_inc(pa["loads"], 16)
                sp.dma_start(node[:, 1024:2048], lay("w_kv")).then_inc(pa["loads"], 16)
                sp.dma_start(bq, lay("b_q")).then_inc(pa["loads"], 16)
                sp.dma_start(bkv, lay("b_kv").broadcast_to([P, 512])).then_inc(pa["loads"], 16)

                def load_hidden(i):
                    for s in range(2):
                        need_sp(pa["hT_psum"], i, l * BLOCKS + i * 2, s - 1)
                        sp.dma_start(ah[s], rows(hidd, i * 2 + s)).then_inc(pa_in[s], 16)
                pairs(sp, load_hidden)
                layer_barrier(sp, l, 1)

                def load_pack(it):
                    for g in range(RING):
                        if not isinstance(it, int):
                            after(e1["a"], l * TILES + it * BODY + (g + 1 - RING) * GT)
                            after(e1["s_psum"], l * TILES + it * BODY + (g + 1 - RING) * GT)
                        n = it * RING + g
                        sp.dma_start(pkf[g], packd[bass.ds(n, 1), :, :].rearrange("a p f -> (a p) f")
                                     ).then_inc(e1_in[g], 16)
                        sp.dma_start(mk[g], maskd[bass.ds(n, 1), :, :].rearrange("a p f -> (a p) f")
                                     ).then_inc(e1_in[g], 16)
                bodies(sp, load_pack)
                layer_barrier(sp, l, 2)

                sp.dma_start(ring[0:DH, 0:1024], lay("w_o")).then_inc(pb["loads"], 16)
                sp.dma_start(ring[0:DH, 1024:1040], lay("e_T")).then_inc(pb["loads"], 16)
                sp.dma_start(borow, lay("b_o")).then_inc(pb["loads"], 16)

                def load_residual(i):
                    for s in range(2):
                        b = i * 2 + s
                        need_sp(pb["y"], i, l * BLOCKS + i * 2, s - 1)
                        sp.dma_start(ch[s], rows(hidd, b)).then_inc(pb_in[s], 16)
                        sp.dma_start(cc[s], cntd[:, bass.ds(b * P, P)]).then_inc(pb_in[s], 16)
                pairs(sp, load_residual)
                layer_barrier(sp, l, 3)

                sp.dma_start(lng, lay("ln_g").broadcast_to([P, HID])).then_inc(pc["loads"], 16)
                sp.dma_start(lnb, lay("ln_b").broadcast_to([P, HID])).then_inc(pc["loads"], 16)

                def load_sum(i):
                    for s in range(2):
                        need_sp(pc["t"], i, l * BLOCKS + i * 2, s - 1)
                        sp.dma_start(dy[s], rows(yd, i * 2 + s)).then_inc(pc_in[s], 16)
                pairs(sp, load_sum)
                layer_barrier(sp, l, 4)

            for v, w in ((fw1, "w_f1"), (fw2, "w_f2"), (fb1, "b_f1")):
                sp.dma_start(v, a[w]).then_inc(pf["loads"], 16)
            sp.dma_start(fb2, row_of(a["b_f2"])).then_inc(pf["loads"], 16)

            def load_last(i):
                for s in range(2):
                    b = i * 2 + s
                    need_sp(pf["o"], i, i * 2, s - 1)
                    sp.dma_start(fh[s], rows(hidd, b)).then_inc(pf_in[s], 16)
                    sp.dma_start(fbase[s], rows(based, b)).then_inc(pf_in[s], 16)
            pairs(sp, load_last)

        @block.gpsimd
        def _(pool):
            steps = Steps(pool, pr["pool"])
            for m in (ident, before, ones):
                last = pool.memset(m[:, :], 1.0 if m is ones else 0.0)
                steps(last)
            steps(pool.affine_select(out=ident[:, :], in_=ident[:, :], compare_op=ALU.not_equal, fill=1.0, base=0,
                                     pattern=[[-1, P]], channel_multiplier=1))
            steps(pool.affine_select(out=before[:, :], in_=before[:, :], compare_op=ALU.is_ge, fill=1.0, base=0,
                                     pattern=[[-1, P]], channel_multiplier=1))
            steps(pool.memset(neg[:, :], 0.0))
            steps(pool.affine_select(out=neg[:, :].rearrange("p (c n) -> p c n", n=WIN),
                                     in_=neg[:, :].rearrange("p (c n) -> p c n", n=WIN),
                                     compare_op=ALU.not_equal, fill=NEGB, base=0, pattern=[[0, 16], [-1, WIN]],
                                     channel_multiplier=1))
            for v, n in ((iwin, NWIN), (iloc, WIN0), (ityp, TYPES), (itile, TILES)):
                steps(pool.iota(v, pattern=[[1, n]], base=0, channel_multiplier=0,
                                allow_small_or_imprecise_dtypes=True))
            for v, val in ((keepf, 1.0), (zrow, 0.0), (pos, 0.0)):
                steps(pool.memset(v, val))
            steps(pool.memset(keep[:, :, 0:1], 0.0))
            pool.sem_inc(pr["consts"], 1)
            steps(pool.memset(blank[:, :, :], 0.0))
            steps(pool.memset(blank[:, :, R_DST:R_DST + 1].bitcast(I32), FAR))
            for s in range(2):
                steps(pool.memset(recc[s], 0.0))
                steps(pool.memset(recc[s][:, :, R_CNT:R_CNT + 1], 1.0))
            pool.sem_inc(pr["cleared"], 1)
            all_rows = pool.to_reg(ROWS - 1)
            all_nodes = pool.to_reg(NPAD - 1)
            with pool.Fori(0, ITERS) as i:
                pool.dma_start(rect[bass.ds(i * (BODY * P), BODY * P), :].rearrange("(p k) f -> p k f", k=BODY),
                               blank).then_inc(pr["blank"], 16)
            pool.wait_ge(pr["blank"], 16 * ITERS)

            def scatter(i):
                for s in range(2):
                    pool.wait_ge(pr["rec"], i * 2 + (s + 1))
                    pool.wait_ge(pr_attr[s], i * 16 + 16)
                    hold(pool)
                    for j in range(CH):
                        pool.indirect_dma_start(rect, bass.IndirectOffsetOnAxis(ap=slot[s][:, j:j + 1], axis=0),
                                                recc[s][:, j, :], None, bounds_check=all_rows, oob_is_err=False
                                                ).then_inc(pr_scat[s], 16)
            scatter(0)
            with pool.Fori(1, CHUNKS // 2) as i:
                scatter(i)
            for s in range(2):
                pool.wait_ge(pr_scat[s], 16 * CH * (CHUNKS // 2))
            barrier(pool, B_PREP)

            steps(pool.memset(ring[:, 0:BODY * HID], 0.0))
            pool.memset(ring[:, BODY * HID + 4 * 768:], 0.0)

            def gather_rows(it):
                for g in range(RING):
                    pool.wait_ge(e0_rec[g], it * 16 + 16)
                    hold(pool)
                    for k in range(GT):
                        t = GT * g + k
                        if not isinstance(it, int):
                            pool.wait_ge(e0["pre"], it * BODY + (t + 1 - BODY))
                            hold(pool)
                        pool.indirect_dma_start(qg[t], None, qrows, bass.IndirectOffsetOnAxis(
                            ap=rec[g][:, k, R_DST:R_DST + 1].bitcast(I32), axis=0), bounds_check=all_nodes,
                            oob_is_err=False).then_inc(e0_q[g], 16)
            bodies(pool, gather_rows)
            barrier(pool, B_E0)

            def store_x1(i):
                for s in range(2):
                    pool.wait_ge(n1["x1"], i * 2 + (s + 1))
                    hold(pool)
                    pool.dma_start(rows(x1d, i * 2 + s), newx[s]).then_inc(n1_out[s], 16)
            pairs(pool, store_x1)
            for s in range(2):
                pool.wait_ge(n1_out[s], 16 * HALF)
            barrier(pool, B_N1)

            pool.memset(QW[0:64, :, 64:128], 0.0)
            pool.memset(QW[64:128, :, 0:64], 0.0)

            def store_entry(i):
                for s in range(2):
                    b = i * 2 + s
                    pool.wait_ge(n2["base"], i * 2 + (s + 1))
                    hold(pool)
                    pool.dma_start(rows(based, b), ibase[s]).then_inc(n2_b[s], 16)
                    pool.wait_ge(n2["hid"], i * 2 + (s + 1))
                    hold(pool)
                    pool.dma_start(rows(hidd, b), ihid[s]).then_inc(n2_h[s], 16)
            pairs(pool, store_entry)
            for s in range(2):
                pool.wait_ge(n2_b[s], 16 * HALF)
                pool.wait_ge(n2_h[s], 16 * HALF)
            barrier(pool, B_N2)

            with pool.Fori(0, LAYERS) as l:
                pool.memset(accr[0:DH, :], 0.0)

                def store_kv(i):
                    for s in range(2):
                        pool.wait_ge(pa["kv"], l * BLOCKS + i * 2 + (s + 1))
                        hold(pool)
                        pool.dma_start(rows(kvrows, i * 2 + s), akv[s]).then_inc(pa_out[s], 16)
                pairs(pool, store_kv)
                for s in range(2):
                    pool.wait_ge(pa_out[s], (l + 1) * (16 * HALF))
                layer_barrier(pool, l, 1)

                def gather_kv(it):
                    for g in range(RING):
                        pool.wait_ge(e1_in[g], (l * ITERS + it) * 32 + 32)
                        hold(pool)
                        for k in range(GT):
                            t = GT * g + k
                            if not isinstance(it, int):
                                pool.wait_ge(e1["o_psum"], l * TILES + it * BODY + (t + 1 - BODY))
                                hold(pool)
                            pool.indirect_dma_start(kv[t], None, kvrows, bass.IndirectOffsetOnAxis(
                                ap=pk[g][:, k, PK - 1:PK].bitcast(I32), axis=0), bounds_check=all_nodes,
                                oob_is_err=False).then_inc(e1_kv[g], 16)
                bodies(pool, gather_kv)
                layer_barrier(pool, l, 2)

                def store_sum(i):
                    for s in range(2):
                        pool.wait_ge(pb["y"], l * BLOCKS + i * 2 + (s + 1))
                        hold(pool)
                        pool.dma_start(rows(yd, i * 2 + s), cy[s]).then_inc(pb_out[s], 16)
                pairs(pool, store_sum)
                for s in range(2):
                    pool.wait_ge(pb_out[s], (l + 1) * (16 * HALF))
                layer_barrier(pool, l, 3)

                def store_hidden(i):
                    for s in range(2):
                        pool.wait_ge(pc["o"], l * BLOCKS + i * 2 + (s + 1))
                        hold(pool)
                        pool.dma_start(rows(hidd, i * 2 + s), du[s]).then_inc(pc_out[s], 16)
                pairs(pool, store_hidden)
                for s in range(2):
                    pool.wait_ge(pc_out[s], (l + 1) * (16 * HALF))
                layer_barrier(pool, l, 4)

            def store_out(i):
                for s in range(2):
                    pool.wait_ge(pf["o"], i * 2 + (s + 1))
                    hold(pool)
                    pool.dma_start(rows(out, i * 2 + s), fo[s]).then_inc(pf_out[s], 16)
            pairs(pool, store_out)
            for s in range(2):
                pool.wait_ge(pf_out[s], 16 * HALF)

        @block.scalar
        def _(act_):
            sc_ = nc.scalar
            stats_a(pr["var"], pr["root"], 1)
            act_.wait_ge(pr["norm"], 1)

            def nodes0(i):
                for s in range(2):
                    b = i * 2 + s
                    act_.wait_ge(n0_x[s], i * 16 + 16)
                    need(act_, n0["hT_psum"], i, i * 2, s - 1)
                    need(act_, n0_h[s], i, 0, i * 16)
                    hold(act_)
                    sc_.activation(hb[s], xb[s], ACT.Relu, bias=nmr[:, bass.ds(b, 1)],
                                   scale=rstd[:, bass.ds(b, 1)]).then_inc(n0["h"], 1)
                    act_.wait_ge(n0["h"], i * 2 + (s + 1))
                    act_.dma_start(rows(h0d, b), hb[s]).then_inc(n0_h[s], 16)
                    act_.wait_ge(n0["hT_psum"], i * 2 + (s + 1))
                    need(act_, n0["pq_psum"], i, i * 2, s - 1)
                    need(act_, n0_hT[s], i, 0, i * 16)
                    hold(act_)
                    sc_.activation(hTf[s], banks[s][:, 0:256], ACT.Copy).then_inc(n0["hT"], 1)
                    act_.wait_ge(n0["hT"], i * 2 + (s + 1))
                    act_.dma_start(rows(h0Td, b), hTf[s]).then_inc(n0_hT[s], 16)
                    act_.wait_ge(n0["pq_psum"], i * 2 + (s + 1))
                    need(act_, n0_q[s], i, 0, i * 16)
                    hold(act_)
                    for w in range(WPB0):
                        sc_.activation(big[64:96, bass.ds(b * WPB0 + w, 1), :].rearrange("p a n -> p (a n)"),
                                       banks[2 + s][WIN0 * w:WIN0 * (w + 1), 0:256], ACT.Copy).then_inc(n0["pq"], 1)
                    sc_.activation(qst[s], banks[2 + s][:, 256:512], ACT.Copy).then_inc(n0["pq"], 1)
                    act_.wait_ge(n0["pq"], (i * 2 + (s + 1)) * 5)
                    act_.dma_start(rows(qrows, b), qst[s]).then_inc(n0_q[s], 16)
            pairs(act_, nodes0)
            for s in range(2):
                for q in (n0_h, n0_hT, n0_q):
                    act_.wait_ge(q[s], 16 * HALF)
            barrier(act_, B_PREP)

            def edges0(it):
                for g in range(RING):
                    n = it * BODY + g * GT
                    for k in range(GT):
                        act_.wait_ge(e0["T_psum"], n + (k + 1))
                        need(act_, e0["pre_psum"], it, n, k + 1 - GT, g * GT)
                        need(act_, e0["mask"], it, n, k + 1 - GT, g * GT)
                        hold(act_)
                        sc_.activation(lh[k], banks[k % 2][0:R_CNT, 0:P], ACT.Copy).then_inc(e0["T"], 1)
                        if not (isinstance(it, int) and g == 0):
                            relu0(it, g, n - GT, k)

            def relu0(it, g, n, k):
                act_.wait_ge(e0["pre"], n + (k + 1))
                need(act_, e0["seg_psum"], it, n, k + 1 - GT, (g - 1) * GT)
                hold(act_)
                sc_.activation(act[k], pre[k], ACT.Relu).then_inc(e0["act"], 1)
            bodies(act_, edges0)
            for k in range(GT):
                relu0(ITERS, 0, TILES - GT, k)
            barrier(act_, B_E0)

            def update0(i):
                for s in range(2):
                    b = i * 2 + s
                    act_.wait_ge(n1["agg_psum"], b + 1)
                    need(act_, n1["gate_psum"], i, i * 2, s - 1)
                    hold(act_)
                    sc_.activation(aggTf[s], banks[s][:, 0:256], ACT.Copy).then_inc(n1["aggT"], 1)
                    act_.wait_ge(n1["rz_pre"], b + 1)
                    hold(act_)
                    sc_.activation(rz[s], rz[s], ACT.Sigmoid).then_inc(n1["rz"], 1)
                    act_.wait_ge(n1["n_pre"], b + 1)
                    hold(act_)
                    sc_.activation(cand[s], cand[s], ACT.Tanh).then_inc(n1["n"], 1)
            pairs(act_, update0)
            stats_a(pr["var"], pr["root"], 2)
            barrier(act_, B_N1)

            def entry(i):
                for s in range(2):
                    b = i * 2 + s
                    act_.wait_ge(n2_x[s], i * 16 + 16)
                    need(act_, n2["hT_psum"], i, i * 2, s - 1)
                    need(act_, n2["base"], i, i * 2, s - 1)
                    hold(act_)
                    sc_.activation(ih[s], ix[s], ACT.Relu, bias=nmr[:, bass.ds(b, 1)],
                                   scale=rstd[:, bass.ds(b, 1)]).then_inc(n2["h"], 1)
                    act_.wait_ge(n2["hT_psum"], b + 1)
                    need(act_, n2["hid_psum"], i, i * 2, s - 1)
                    hold(act_)
                    sc_.activation(ihTf[s], banks[s][:, 0:256], ACT.Copy).then_inc(n2["hT"], 1)
            pairs(act_, entry)
            barrier(act_, B_N2)

            with act_.Fori(0, LAYERS) as l:
                def project(i):
                    for s in range(2):
                        n = l * BLOCKS + i * 2
                        act_.wait_ge(pa["hT_psum"], n + (s + 1))
                        need(act_, pa["kv_psum"], i, n, s - 1)
                        hold(act_)
                        sc_.activation(ahTf[s], banks[s][:, 0:256], ACT.Copy).then_inc(pa["hT"], 1)
                pairs(act_, project)
                layer_barrier(act_, l, 1)

                def exps(n):
                    act_.wait_ge(e1["shifted"], l * GROUPS + n)
                    hold(act_)
                    sc_.activation(exf, exf, ACT.Exp, scale=DH ** -0.5).then_inc(e1["exp"], 1)

                def edges1(it):
                    for g in range(RING):
                        n = l * TILES + it * BODY + g * GT
                        for k in range(GT):
                            act_.wait_ge(e1["T_psum"], n + (k + 1))
                            if not (isinstance(it, int) and g == 0):
                                act_.wait_ge(e1["s_psum"], n + (k + 1 - GT))
                            hold(act_)
                            sc_.activation(kT[k], banks[k % 2][:, 0:256], ACT.Copy).then_inc(e1["T"], 1)
                            if k == 2 and not (isinstance(it, int) and g == 0):
                                exps(it * RING + g)
                bodies(act_, edges1)
                exps(GROUPS)
                layer_barrier(act_, l, 2)

                act_.wait_ge(pb["eb_psum"], l + 1)
                hold(act_)
                sc_.activation(eb, banks[7][0:4, 0:HID], ACT.Copy).then_inc(pb["eb"], 1)

                def output(i):
                    for s in range(2):
                        b, n = i * 2 + s, l * BLOCKS + i * 2
                        need(act_, pb["m_psum"], i, n, s - 1)
                        if not isinstance(i, int):
                            hold(act_)
                        sc_.activation(cst[s].rearrange("p h (w n) -> p w h n", w=WPB),
                                       acc1[:, bass.ds(b * WPB, WPB), :].rearrange("p w (h n) -> p w h n", h=HEADS),
                                       ACT.Copy).then_inc(pb["staged"], 1)
                pairs(act_, output)
                stats_a(pb["var"], pb["root"], l + 1)
                layer_barrier(act_, l, 3)

                def norm(i):
                    for s in range(2):
                        b, n = i * 2 + s, l * BLOCKS + i * 2
                        act_.wait_ge(pc_in[s], (l * HALF + i) * 16 + 16)
                        need(act_, pc["u"], i, n, s - 1)
                        hold(act_)
                        sc_.activation(dt[s], dy[s], ACT.Identity, bias=nmr[:, bass.ds(b, 1)],
                                       scale=rstd[:, bass.ds(b, 1)]).then_inc(pc["t"], 1)
                pairs(act_, norm)
                layer_barrier(act_, l, 4)

            act_.wait_ge(pf["loads"], 64)

            def last(i):
                for s in range(2):
                    b = i * 2 + s
                    act_.wait_ge(pf["hT_psum"], b + 1)
                    need(act_, pf["u_psum"], i, i * 2, s - 1)
                    hold(act_)
                    sc_.activation(fhTf[s], banks[s][:, 0:256], ACT.Copy).then_inc(pf["hT"], 1)
                    act_.wait_ge(pf["u_psum"], b + 1)
                    need(act_, pf["o_psum"], i, i * 2, s - 1)
                    hold(act_)
                    for j in range(2):
                        sc_.activation(fuT[s][:, j, :], banks[2 + s][:, P * j:P * (j + 1)], ACT.Relu,
                                       bias=fb1[:, j:j + 1]).then_inc(pf["u"], 1)
            pairs(act_, last)

        @block.vector
        def _(v):
            def stat_x(i):
                for s in range(2):
                    v.wait_ge(pr_x[s], i * 16 + 16)
                    v.bn_stats(bst[:, bass.ds(i * 2 + s, 1), :].rearrange("p a c -> p (a c)"), xs[s]
                               ).then_inc(pr["x_read"], 1)
            pairs(v, stat_x)
            v.wait_ge(pr["x_read"], BLOCKS)
            step = Steps(v, pr["vstep"])
            stats_v(step, pr["var"], pr["root"], 1)
            v.sem_inc(pr["norm"], 1)

            v.wait_ge(pr["idx"], 48)
            v.wait_ge(pr["consts"], 1)
            hits = [hotf[:, 0:COLS], runf[:, 0:COLS]]
            scratch = hits[0].bitcast(I32)
            step(v.tensor_scalar(scratch, srci, 4, None, ALU.arith_shift_right))
            step(v.tensor_copy(win, scratch))
            step(v.tensor_scalar(scratch, srci, WIN - 1, None, ALU.bitwise_and))
            step(v.tensor_copy(loc, scratch))
            step(v.tensor_scalar(scratch, srci, WIN0 - 1, None, ALU.bitwise_and))
            step(v.tensor_copy(loc0, scratch))
            step(v.tensor_copy(typ, typi))
            step(v.tensor_scalar(pen, win, 0.0, float(FAR), ALU.is_lt, ALU.mult))
            step(v.tensor_scalar(pen, pen, -1.0, None, ALU.add))
            v.sem_inc(pr["cnt"], 2)
            with v.Fori(0, NWIN // 2) as i:
                for s in range(2):
                    w = bass.ds(i * 2 + s, 1)
                    v.wait_ge(pr["cnt"], i * 2 + (s + 1))
                    v.tensor_scalar(hits[s], win, iwin[:, w], 0.0, ALU.is_equal, ALU.add,
                                    accum_out=cnt[:, w]).then_inc(pr["cnt"], 1)
            v.wait_ge(pr["cnt"], NWIN + 2)
            hold(v)
            v.sem_inc(pr["tile_base"], 1)
            v.wait_ge(pr["pre_psum"], 1)
            step(v.tensor_scalar(toti, banks[4][:, 256:256 + NWIN], float(P - 1), None, ALU.add))
            step(v.tensor_scalar(toti, toti, 7, None, ALU.arith_shift_right))
            step(v.tensor_copy(ntl, toti))
            step(v.tensor_tensor_scan(tbi, ntl, zrow, 0.0, ALU.add, ALU.add))
            v.sem_inc(pr["tile_base"], 1)
            step(v.tensor_tensor(off, tbi, ntl, ALU.subtract))
            step(v.tensor_scalar(off, off, float(P), None, ALU.mult))
            step(v.tensor_tensor(off, off, banks[4][:, 0:NWIN], ALU.add))
            v.wait_ge(pr["base_psum"], 1)
            for z in range(2):
                step(v.tensor_copy(tcol[z], banks[5][0:NWIN // 2, P * z:P * z + 1]))
                v.tensor_scalar(lemat[z], itile[0:NWIN // 2, :], tcol[z], None, ALU.is_ge).then_inc(pr["below"], 1)
            v.wait_ge(pr["win_psum"], 1)
            for z in range(2):
                step(v.tensor_scalar(wtab[:, z * TH:(z + 1) * TH], banks[6 + z][:, 0:TH], float(NWIN - 1), None,
                                     ALU.min))
            step(v.tensor_scalar(wtab0, wtab[0:1, :], 1, None, ALU.arith_shift_right))

            RANK = 7

            def rank(q, j, n):
                st = Steps(v, pr["vstep"], n, RANK, rank_start)
                cols, ws = bass.ds(q * QC, QC), bass.ds(j * WPP, WPP)
                st(v.tensor_copy(hot[:, :, 0:1], off[:, ws].unsqueeze(2)))
                st(v.tensor_tensor(hot[:, :, 1:PE1], win[:, cols].unsqueeze(1).broadcast_to([P, WPP, QC]),
                                   iwin[:, ws].unsqueeze(2).broadcast_to([P, WPP, QC]), ALU.is_equal))
                st(v.tensor_tensor_scan(runf, keepf, hotf, 0.0, ALU.mult, ALU.add))
                hold(v)
                st(v.tensor_copy(off[:, ws].unsqueeze(2), run[:, :, QC:PE1]))
                st(v.tensor_tensor(prod, run[:, :, 1:PE1], hot[:, :, 1:PE1], ALU.mult))
                st(v.tensor_reduce(psum_pos, prod.rearrange("p w c -> p c w"), AX.X, ALU.add))
                st(v.tensor_tensor(pos[:, cols], pos[:, cols], psum_pos, ALU.add))

            RECS = 10

            def record(i, s):
                cols = bass.ds(i * (2 * CH) + s * CH, CH)
                if isinstance(i, int):
                    v.wait_ge(pr["cleared"], 1)
                else:
                    v.wait_ge(pr_scat[s], i * (16 * CH))
                st = Steps(v, pr["rstep"], i * 2 + s, RECS)
                st(v.tensor_tensor(ni, pos[:, cols], pen[:, cols], ALU.add))
                st(v.tensor_scalar(na, ni, P - 1, 2, ALU.bitwise_and, ALU.arith_shift_left))
                st(v.tensor_scalar(nb, ni, 7, GT - 1, ALU.arith_shift_right, ALU.bitwise_and))
                st(v.tensor_tensor(na, na, nb, ALU.bitwise_or))
                st(v.tensor_scalar(nb, ni, 9, 9, ALU.arith_shift_right, ALU.arith_shift_left))
                st(v.tensor_tensor(slot[s], na, nb, ALU.bitwise_or))
                for first, n, l in ((R_OH0, WIN0, loc0), (R_OH, WIN, loc)):
                    st(v.tensor_tensor(recc[s][:, :, first:first + n], l[:, cols].unsqueeze(2).broadcast_to([P, CH, n]),
                                       iloc[:, 0:n].unsqueeze(1).broadcast_to([P, CH, n]), ALU.is_equal))
                st(v.tensor_tensor(recc[s][:, :, R_CNT + 1:R_DST], typ[:, cols].unsqueeze(2)
                                   .broadcast_to([P, CH, TYPES]),
                                   ityp.unsqueeze(1).broadcast_to([P, CH, TYPES]), ALU.is_equal))
                st(v.tensor_copy(recc[s][:, :, R_DST:R_DST + 1].bitcast(I32), dsti[:, cols].unsqueeze(2)))
                hold(v)
                v.sem_inc(pr["rec"], 1)

            rank_start = step.c
            hold(v)
            with v.Fori(0, QFIRST) as q:
                with v.Fori(0, PARTS) as j:
                    rank(q, j, q * PARTS + j)

            def chunk_pair(q, jj):
                i = q * (PARTS // 2) + jj
                for s in range(2):
                    record(i, s)
                    rank(QFIRST + q, jj * 2 + s, (QFIRST + q) * PARTS + jj * 2 + s)
            chunk_pair(0, 0)
            with v.Fori(1, PARTS // 2) as jj:
                chunk_pair(0, jj)
            with v.Fori(1, NQ - QFIRST) as q:
                with v.Fori(0, PARTS // 2) as jj:
                    chunk_pair(q, jj)
            with v.Fori((NQ - QFIRST) * (PARTS // 2), CHUNKS // 2) as i:
                for s in range(2):
                    record(i, s)
            barrier(v, B_PREP)

            v.memset(accr[:, :], 0.0).then_inc(e0["vstep"], 1)
            for bank in banks[6:8]:
                v.memset(bank[:, :], 0.0).then_inc(e0["vstep"], 1)
            v.wait_ge(e0["vstep"], 3)

            def add0(n, ws, k):
                if k % 2 == 0:
                    v.wait_ge(e0["seg_psum"], n + (k + 2))
                v.wait_ge(e0["added"], n + (k + 1))
                v.tensor_tensor(acc0[:, bass.ds(ws[k], 1), :], acc0[:, bass.ds(ws[k], 1), :],
                                sum_bank(k)[:, 96 * (k % 2):96 * (k % 2 + 1)].unsqueeze(1), ALU.add
                                ).then_inc(e0["added"], 1)

            def edges0(it):
                for g in range(RING):
                    n = it * BODY + g * GT
                    for k in range(GT):
                        t = g * GT + k
                        v.wait_ge(e0["pre_psum"], n + (k + 1))
                        if k == 0:
                            v.wait_ge(e0_q[g], it * (16 * GT) + 16 * GT)
                        if not (isinstance(it, int) and g == 0):
                            v.wait_ge(e0["act"], n + (k + 1 - GT))
                        hold(v)
                        v.tensor_tensor(pre[k], banks[2 + k][:, 0:HID], qg[t], ALU.add).then_inc(e0["pre"], 1)
                        if k == 0 and not isinstance(it, int):
                            v.wait_ge(e0_store[g], it * 32)
                            hold(v)
                        v.wait_ge(e0["T"], n + (k + 1))
                        hold(v)
                        v.tensor_scalar(mk0[g][:, P * k:P * (k + 1)], lh[k][R_OH:R_CNT, :], -1.0, 1.0, ALU.mult,
                                        ALU.add).then_inc(e0["mask"], 1)
                    if not (isinstance(it, int) and g == 0):
                        ws = windows(mybir.EngineType.DVE, n - GT, wtab0, NWIN0)
                        for k in range(GT):
                            add0(n - GT, ws, k)
            v.sem_inc(e0["added"], 1)
            bodies(v, edges0)
            ws = windows(mybir.EngineType.DVE, TILES - GT, wtab0, NWIN0)
            for k in range(GT):
                add0(TILES - GT, ws, k)
            barrier(v, B_E0)

            v.wait_ge(n1["loads"], 80)
            v.tensor_tensor(brz, brz, brzh, ALU.add).then_inc(n1["vstep"], 1)
            v.wait_ge(n1["vstep"], 1)

            def update0(i):
                for s in range(2):
                    b = i * 2 + s
                    st = Steps(v, n1["vstep"], b, 7, 1)
                    v.wait_ge(n1["gate_psum"], b + 1)
                    hold(v)
                    v.tensor_tensor(rz[s], banks[2 + s][:, :], brz, ALU.add).then_inc(n1["rz_pre"], 1)
                    st(v.tensor_tensor(gt, banks[4 + s][:, 256:512], bhn, ALU.add))
                    v.wait_ge(n1["rz"], b + 1)
                    st(v.tensor_tensor(gt, gt, rz[s][:, 0:256], ALU.mult))
                    st(v.tensor_tensor(gt, gt, banks[4 + s][:, 0:256], ALU.add))
                    v.tensor_tensor(cand[s], gt, bxn, ALU.add).then_inc(n1["n_pre"], 1)
                    v.wait_ge(n1["n"], b + 1)
                    st(v.tensor_tensor(gt, gh[s], cand[s], ALU.subtract))
                    st(v.tensor_tensor(gt, gt, rz[s][:, 256:512], ALU.mult))
                    st(v.tensor_tensor(gt, gt, cand[s], ALU.add))
                    need(v, n1_out[s], i, 0, i * 16)
                    hold(v)
                    v.tensor_tensor(newx[s], gt, gx[s], ALU.add).then_inc(n1["x1"], 1)
                    v.wait_ge(n1["x1"], b + 1)
                    st(v.bn_stats(bst[:, bass.ds(b, 1), :].rearrange("p a c -> p (a c)"), newx[s]))
                    st.end()
            pairs(v, update0)
            stats_v(Steps(v, n1["vstep"], 0, 0, 1 + 7 * BLOCKS), pr["var"], pr["root"], 2)
            barrier(v, B_N1)

            v.wait_ge(n2["loads"], 32)

            def entry(i):
                for s in range(2):
                    b = i * 2 + s
                    v.wait_ge(n2["h"], b + 1)
                    need(v, n2_b[s], i, 0, i * 16)
                    hold(v)
                    v.tensor_tensor(ibase[s], ix[s], ih[s], ALU.add).then_inc(n2["base"], 1)
                    v.wait_ge(n2["hid_psum"], b + 1)
                    need(v, n2_h[s], i, 0, i * 16)
                    hold(v)
                    v.tensor_tensor(ihid[s], banks[2 + s][:, 0:HID], ib, ALU.add).then_inc(n2["hid"], 1)
            pairs(v, entry)
            barrier(v, B_N2)

            v.sem_inc(e1["added"], 1)
            with v.Fori(0, LAYERS) as l:
                v.wait_ge(pa["loads"], l * 64 + 64)
                hold(v)

                def project(i):
                    for s in range(2):
                        b, n = i * 2 + s, l * BLOCKS + i * 2
                        v.wait_ge(pa["q_psum"], n + (s + 1))
                        hold(v)
                        q = banks[2 + s][:, :].rearrange("p (h w n) -> p w h n", h=HEADS, w=WPB)
                        bias = bq.unsqueeze(1).unsqueeze(3).broadcast_to([P, WPB, HEADS, WIN])
                        for z in range(2):
                            ps = slice(64 * z, 64 * z + 64)
                            v.tensor_tensor(QT[ps, bass.ds(b * WPB, WPB), z, :, :], q[ps], bias[ps], ALU.add
                                            ).then_inc(pa["q"], 1)
                        v.wait_ge(pa["kv_psum"], n + (s + 1))
                        if not isinstance(i, int):
                            v.wait_ge(pa_out[s], (l * HALF + i) * 16)
                        hold(v)
                        v.tensor_tensor(akv[s], banks[4 + s][:, :], bkv, ALU.add).then_inc(pa["kv"], 1)
                pairs(v, project)
                layer_barrier(v, l, 1)

                def softmax_tail(n, groups):
                    v.wait_ge(e1["exp"], l * GROUPS + groups)
                    hold(v)
                    st = Steps(v, e1["vgroup"], l * GROUPS + (groups - 1), 3)
                    st(v.tensor_reduce(sm, ex.rearrange("p k (g h) -> p k h g", g=HEADS), AX.X, ALU.add))
                    st(v.reciprocal(smf, smf))
                    st(v.tensor_tensor(att.rearrange("p k (g h) -> p k g h", g=HEADS),
                                       ex.rearrange("p k (g h) -> p k g h", g=HEADS),
                                       sm.unsqueeze(2).broadcast_to([P, GT, HEADS, HEADS]), ALU.mult))

                def spread(n, g, k, earlier=True):
                    if earlier:
                        v.wait_ge(e1["o_psum"], n + (k + 1 - 2 * GT))
                    v.tensor_tensor(A[:, k, :, :], att[:, k, :].unsqueeze(2).broadcast_to([P, 16, WIN]),
                                    pk[g][:, k, 0:WIN].unsqueeze(1).broadcast_to([P, 16, WIN]), ALU.mult
                                    ).then_inc(e1["a"], 1)

                v.memset(node[0:DH, 0:E], 0.0).then_inc(e1["cleared"], 1)

                def add1(n, ws, k):
                    if k % 2 == 0:
                        v.wait_ge(e1["o_psum"], n + (k + 2))
                    v.wait_ge(e1["added"], n + (k + 1))
                    v.tensor_tensor(acc1[:, bass.ds(ws[k], 1), :], acc1[:, bass.ds(ws[k], 1), :],
                                    sum_bank(k)[0:DH, DH * (k % 2):DH * (k % 2 + 1)].unsqueeze(1), ALU.add
                                    ).then_inc(e1["added"], 1)

                def edges1(it):
                    for g in range(RING):
                        t = it * BODY + g * GT
                        n = l * TILES + t
                        first = isinstance(it, int) and g == 0
                        if not first:
                            softmax_tail(n, it * RING + g)
                            second = isinstance(it, int) and g == 1
                            for k in range(GT):
                                spread(n, (g - 1) % RING, k, not second)
                            if not second:
                                ws = windows(mybir.EngineType.DVE, t - 2 * GT, wtab, NWIN)
                        v.wait_ge(e1_in[g], (l * ITERS + it) * 32 + 32)
                        hold(v)
                        for k in range(GT):
                            v.wait_ge(e1["s_psum"], n + (k + 1))
                            v.tensor_reduce(sc[:, k, :], banks[2 + k][:, 0:16 * WIN].rearrange("p (c n) -> p c n", n=WIN),
                                            AX.X, ALU.max).then_inc(e1["s_read"], 1)
                            if not (first or second):
                                add1(n - 2 * GT, ws, k)
                        v.wait_ge(e1["s_read"], n + GT)
                        v.tensor_reduce(mx, sc.rearrange("p k (g h) -> p k h g", g=HEADS), AX.X, ALU.max
                                        ).then_inc(e1["vstep"], 1)
                        v.wait_ge(e1["vstep"], l * GROUPS + it * RING + (g + 1))
                        v.tensor_tensor(ex.rearrange("p k (g h) -> p k g h", g=HEADS),
                                        sc.rearrange("p k (g h) -> p k g h", g=HEADS),
                                        mx.unsqueeze(2).broadcast_to([P, GT, HEADS, HEADS]), ALU.subtract
                                        ).then_inc(e1["shifted"], 1)
                v.wait_ge(e1["cleared"], l + 1)
                hold(v)
                bodies(v, edges1)
                softmax_tail(l * TILES + TILES, GROUPS)
                for k in range(GT):
                    spread(l * TILES + TILES, RING - 1, k)
                for t in (TILES - 2 * GT, TILES - GT):
                    ws = windows(mybir.EngineType.DVE, t, wtab, NWIN)
                    for k in range(GT):
                        add1(l * TILES + t, ws, k)
                layer_barrier(v, l, 2)

                def output(i):
                    for s in range(2):
                        b, n = i * 2 + s, l * BLOCKS + i * 2
                        v.wait_ge(pb["m_psum"], n + (s + 1))
                        v.wait_ge(pb_in[s], (l * HALF + i) * 32 + 32)
                        if not isinstance(i, int):
                            v.wait_ge(pb_out[s], (l * HALF + i) * 16)
                        hold(v)
                        v.tensor_tensor(cy[s], banks[2 + s][:, 0:HID], ch[s], ALU.add).then_inc(pb["y"], 1)
                        v.wait_ge(pb["y"], n + (s + 1))
                        v.bn_stats(bst[:, bass.ds(b, 1), :].rearrange("p a c -> p (a c)"), cy[s]
                                   ).then_inc(pb["vstep"], 1)
                pairs(v, output)
                v.wait_ge(pb["vstep"], l * BLOCKS + BLOCKS)
                hold(v)
                stats_v(Steps(v, pb["vstat"], l, STAT_STEPS), pb["var"], pb["root"], l + 1)
                layer_barrier(v, l, 3)

                v.wait_ge(pc["loads"], l * 32 + 32)
                hold(v)

                def norm(i):
                    for s in range(2):
                        n = l * BLOCKS + i * 2
                        st = Steps(v, pc["vstep"], n + s, 1)
                        v.wait_ge(pc["t"], n + (s + 1))
                        if not isinstance(i, int):
                            v.wait_ge(pc_out[s], (l * HALF + i) * 16)
                        hold(v)
                        v.tensor_tensor(du[s], dt[s], lng, ALU.mult).then_inc(pc["u"], 1)
                        v.wait_ge(pc["u"], n + (s + 1))
                        st(v.tensor_tensor(du[s], du[s], lnb, ALU.add))
                        v.tensor_scalar(du[s], du[s], 0.0, None, ALU.max).then_inc(pc["o"], 1)
                pairs(v, norm)
                layer_barrier(v, l, 4)

            v.wait_ge(pf["loads"], 64)

            def last(i):
                for s in range(2):
                    b = i * 2 + s
                    st = Steps(v, pf["vstep"], b, 1)
                    v.wait_ge(pf["o_psum"], b + 1)
                    v.wait_ge(pf_in[s], i * 32 + 32)
                    need(v, pf_out[s], i, 0, i * 16)
                    hold(v)
                    st(v.tensor_tensor(fo[s], banks[4 + s][:, 0:HID], fbase[s], ALU.add))
                    v.tensor_tensor(fo[s], fo[s], fb2, ALU.add).then_inc(pf["o"], 1)
            pairs(v, last)

        @block.tensor
        def _(pe):
            mm = nc.tensor.matmul

            pe.wait_ge(pr["consts"], 1)
            pe.wait_ge(pr["tile_base"], 1)
            mm(banks[4][:, 0:NWIN], before[:, :], cnt, start=True, stop=True)
            mm(banks[4][:, 256:256 + NWIN], ones[:, :], cnt, start=True, stop=True).then_inc(pr["pre_psum"], 1)
            pe.wait_ge(pr["tile_base"], 2)
            for z in range(2):
                t = nc.tensor.transpose(banks[5][0:NWIN // 2, P * z:P * (z + 1)],
                                        tbi[:, NWIN // 2 * z:NWIN // 2 * (z + 1)], ident[:, :])
            t.then_inc(pr["base_psum"], 1)
            pe.wait_ge(pr["below"], 2)
            for half in range(2):
                for z in range(2):
                    t = mm(banks[6 + half][:, 0:TH], ones[0:NWIN // 2, :], lemat[z][:, half * TH:(half + 1) * TH],
                           start=z == 0, stop=z == 1)
            t.then_inc(pr["win_psum"], 1)
            pe.wait_ge(pr["weights"], 144)

            def nodes0(i):
                for s in range(2):
                    b = i * 2 + s
                    pe.wait_ge(n0["h"], b + 1)
                    for k in range(2):
                        t = nc.tensor.transpose(banks[s][:, P * k:P * (k + 1)], hb[s][:, P * k:P * (k + 1)],
                                                ident[:, :])
                    t.then_inc(n0["hT_psum"], 1)
                    pe.wait_ge(n0["hT"], b + 1)
                    if not isinstance(i, int):
                        pe.wait_ge(n0["pq"], (i * 2 + (s - 1)) * 5)
                    mm(banks[2 + s][:, :], hT[s][:, 0, :], wpq[:, 0, :], start=True, stop=False)
                    mm(banks[2 + s][:, :], hT[s][:, 1, :], wpq[:, 1, :], start=False, stop=False)
                    mm(banks[2 + s][:, :], ones[0:1, :], b1row, start=False, stop=True).then_inc(n0["pq_psum"], 1)
            pairs(pe, nodes0)
            barrier(pe, B_PREP)

            def need_sums(added, n, k):
                if not (isinstance(n, int) and n == 0):
                    pe.wait_ge(added, n + (k - 1))
                elif k == 0:
                    pe.wait_ge(added, 1)

            def trans0(it, g, k):
                n = it * BODY + g * GT
                if k == 0:
                    pe.wait_ge(e0_rec[g], it * 16 + 16)
                if not (isinstance(it, int) and it == 0 and g == 0 and k < 2):
                    pe.wait_ge(e0["T"], n + (k - 1))
                nc.tensor.transpose(banks[k % 2][0:R_CNT, 0:P], rec[g][:, k, 0:R_CNT], ident[:, :]
                                    ).then_inc(e0["T_psum"], 1)

            def pre0(it, g, k, w):
                n = it * BODY + g * GT
                pe.wait_ge(e0["T"], n + (k + 1))
                if not (isinstance(it, int) and it == 0 and g == 0):
                    pe.wait_ge(e0["pre"], n + (k + 1 - GT))
                mm(banks[2 + k][:, 0:HID], lh[k][0:R_OH, :], big[0:R_OH, bass.ds(w, 1), :].rearrange("p a n -> p (a n)"),
                   start=True, stop=True).then_inc(e0["pre_psum"], 1)

            def sums0(n, g):
                for k in range(GT):
                    pe.wait_ge(e0["act"], n + (k + 1))
                    if k % 2 == 0:
                        need_sums(e0["added"], n, k)
                    onehot = rec[g][:, k, R_OH0:R_OH]
                    sums = sum_bank(k)[:, 96 * (k % 2):96 * (k % 2 + 1)]
                    for f in range(2):
                        mm(sums[:, 32 * f:32 * (f + 1)], act[k][:, P * f:P * (f + 1)], onehot, start=True, stop=True)
                    mm(sums[0:4, 64:96], rec[g][:, k, R_CNT:R_DST], onehot, start=True, stop=True).then_inc(e0["seg_psum"], 1)

            def edges0(it, more=True):
                for g in range(RING):
                    ws = windows(mybir.EngineType.PE, it * BODY + g * GT, wtab0, NWIN0)
                    for k in range(GT):
                        if k < 2:
                            trans0(it, g, k + 2)
                        elif g < RING - 1:
                            trans0(it, g + 1, k - 2)
                        elif more:
                            trans0(it + 1, 0, k - 2)
                        pre0(it, g, k, ws[k])
                        if k == 1 and not (isinstance(it, int) and it == 0 and g == 0):
                            sums0(it * BODY + (g - 1) * GT, (g - 1) % RING)
            trans0(0, 0, 0)
            trans0(0, 0, 1)
            edges0(0)
            with pe.Fori(1, ITERS - 1) as it:
                edges0(it)
            edges0(ITERS - 1, more=False)
            sums0(TILES - GT, RING - 1)
            barrier(pe, B_E0)

            def update0(i):
                for s in range(2):
                    b = i * 2 + s
                    need(pe, n1["aggT"], i, i * 2, s - 1)
                    for f in range(2):
                        dst, fs = banks[s][:, P * f:P * (f + 1)], slice(P * f, P * (f + 1))
                        for j in range(2):
                            mm(dst, w2l0[:, j, fs], acc0[:, bass.ds(b * WPB0, WPB0), 32 * j:32 * (j + 1)],
                               start=j == 0, stop=False)
                        t = mm(dst, b2x[:, fs], acc0[:, bass.ds(b * WPB0, WPB0), 64:96], start=False, stop=True)
                    t.then_inc(n1["agg_psum"], 1)
                    pe.wait_ge(n1["aggT"], b + 1)
                    pe.wait_ge(n1_in[s], i * 48 + 48)
                    need(pe, n1["x1"], i, i * 2, s - 1)
                    for j, (src, w) in enumerate(((aggT[s], 0), (aggT[s], 1), (ghT[s], 2), (ghT[s], 3))):
                        mm(banks[2 + s][:, :], src[:, j % 2, :], wgate[:, w, 0:512], start=j == 0, stop=j == 3)
                    for part in range(2):
                        src = (aggT, ghT)[part][s]
                        for j in range(2):
                            t = mm(banks[4 + s][:, 256 * part:256 * (part + 1)], src[:, j, :],
                                   wgate[:, 2 * part + j, 512:768], start=j == 0, stop=j == 1)
                    t.then_inc(n1["gate_psum"], 1)
            pairs(pe, update0)
            barrier(pe, B_N1)

            pe.wait_ge(n2["loads"], 32)

            def entry(i):
                for s in range(2):
                    b = i * 2 + s
                    pe.wait_ge(n2["h"], b + 1)
                    need(pe, n2["hT"], i, i * 2, s - 1)
                    for k in range(2):
                        t = nc.tensor.transpose(banks[s][:, P * k:P * (k + 1)], ih[s][:, P * k:P * (k + 1)],
                                                ident[:, :])
                    t.then_inc(n2["hT_psum"], 1)
                    pe.wait_ge(n2["hT"], b + 1)
                    need(pe, n2["hid"], i, i * 2, s - 1)
                    mm(banks[2 + s][:, 0:HID], ihT[s][:, 0, :], iw[:, 0, :], start=True, stop=False)
                    mm(banks[2 + s][:, 0:HID], ihT[s][:, 1, :], iw[:, 1, :], start=False, stop=True
                       ).then_inc(n2["hid_psum"], 1)
            pairs(pe, entry)
            barrier(pe, B_N2)

            with pe.Fori(0, LAYERS) as l:
                pe.wait_ge(pa["loads"], l * 64 + 64)
                hold(pe)

                def project(i):
                    for s in range(2):
                        n = l * BLOCKS + i * 2
                        pe.wait_ge(pa_in[s], (l * HALF + i) * 16 + 16)
                        need(pe, pa["hT"], i, n, s - 1)
                        for k in range(2):
                            t = nc.tensor.transpose(banks[s][:, P * k:P * (k + 1)], ah[s][:, P * k:P * (k + 1)],
                                                    ident[:, :])
                        t.then_inc(pa["hT_psum"], 1)
                        pe.wait_ge(pa["hT"], n + (s + 1))
                        if not isinstance(i, int):
                            pe.wait_ge(pa["q"], (n + (s - 1)) * 2)
                        for h in range(HEADS):
                            for k in range(2):
                                t = mm(banks[2 + s][:, P * h:P * (h + 1)], wq[:, k, h, :], ahT[s][:, k, :],
                                       start=k == 0, stop=k == 1)
                        t.then_inc(pa["q_psum"], 1)
                        need(pe, pa["kv"], i, n, s - 1)
                        for k in range(2):
                            t = mm(banks[4 + s][:, :], ahT[s][:, k, :], wkv[:, k, :], start=k == 0, stop=k == 1)
                        t.then_inc(pa["kv_psum"], 1)
                pairs(pe, project)
                layer_barrier(pe, l, 1)

                def trans1(it, g, k):
                    n = l * TILES + it * BODY + g * GT
                    if k == 0:
                        pe.wait_ge(e1_kv[g], (l * ITERS + it + 1) * (16 * GT))
                    if not (isinstance(it, int) and it == 0 and g == 0 and k < 2):
                        pe.wait_ge(e1["T"], n + (k - 1))
                    for j in range(2):
                        t = nc.tensor.transpose(banks[k % 2][:, P * j:P * (j + 1)],
                                                kv[g * GT + k][:, P * j:P * (j + 1)], ident[:, :])
                    t.then_inc(e1["T_psum"], 1)

                def scores(it, g, k, w):
                    n = l * TILES + it * BODY + g * GT
                    if k == 0:
                        pe.wait_ge(e1_in[g], (l * ITERS + it) * 32 + 32)
                    if not (isinstance(it, int) and it == 0 and g == 0):
                        pe.wait_ge(e1["s_read"], n + (k + 1 - GT))
                    pe.wait_ge(e1["T"], n + (k + 1))
                    hold(pe)
                    mm(banks[2 + k][:, 0:16 * WIN], mk[g][:, P * k:P * (k + 1)], neg[:, :], start=True, stop=False)
                    q = QW[:, bass.ds(w, 1), :].rearrange("p a n -> p (a n)")
                    for j in range(2):
                        m = mm(banks[2 + k][:, 8 * WIN * j:8 * WIN * (j + 1)], kT[k][:, P * j:P * (j + 1)], q,
                               start=False, stop=j == 1)
                    m.then_inc(e1["s_psum"], 1)

                def messages(t, g):
                    n = l * TILES + t
                    for k in range(GT):
                        pe.wait_ge(e1["a"], n + (k + 1))
                        if k % 2 == 0 and not (isinstance(t, int) and t == 0):
                            pe.wait_ge(e1["added"], n + (k - 1))
                        for j in range(HEADS):
                            m = mm(sum_bank(k)[0:DH, DH * (k % 2):DH * (k % 2 + 1)],
                                   kv[g * GT + k][:, HID + DH * j:HID + DH * (j + 1)],
                                   A[:, k, HEADS * j:HEADS * (j + 1), :].rearrange("p h n -> p (h n)"),
                                   start=j == 0, stop=j == HEADS - 1)
                        m.then_inc(e1["o_psum"], 1)

                def edges1(it, more=True):
                    for g in range(RING):
                        ws = windows(mybir.EngineType.PE, it * BODY + g * GT, wtab, NWIN)
                        for k in range(GT):
                            if k < 2:
                                trans1(it, g, k + 2)
                            elif g < RING - 1:
                                trans1(it, g + 1, k - 2)
                            elif more:
                                trans1(it + 1, 0, k - 2)
                            scores(it, g, k, ws[k])
                        if not (isinstance(it, int) and it == 0 and g == 0):
                            messages(it * BODY + (g - 1) * GT, (g - 1) % RING)
                trans1(0, 0, 0)
                trans1(0, 0, 1)
                edges1(0)
                with pe.Fori(1, ITERS - 1) as it:
                    edges1(it)
                edges1(ITERS - 1, more=False)
                messages(TILES - GT, RING - 1)
                layer_barrier(pe, l, 2)

                pe.wait_ge(pb["loads"], l * 48 + 48)
                hold(pe)
                for h in range(HEADS):
                    mm(banks[7][0:4, 0:HID], eeT[:, h, :], wo[:, h, :], start=h == 0, stop=False)
                mm(banks[7][0:4, 0:HID], ident[0:1, 0:4], borow, start=False, stop=True).then_inc(pb["eb_psum"], 1)
                pe.wait_ge(pb["eb"], l + 1)
                hold(pe)

                def output(i):
                    for s in range(2):
                        n = l * BLOCKS + i * 2
                        pe.wait_ge(pb["staged"], n + (s + 1))
                        pe.wait_ge(pb_in[s], (l * HALF + i) * 32 + 32)
                        need(pe, pb["y"], i, n, s - 1)
                        hold(pe)
                        for h in range(HEADS):
                            mm(banks[2 + s][:, 0:HID], cst[s][:, h, :], wo[:, h, :], start=h == 0, stop=False)
                        mm(banks[2 + s][:, 0:HID], cc[s], eb, start=False, stop=True).then_inc(pb["m_psum"], 1)
                pairs(pe, output)
                layer_barrier(pe, l, 3)
                layer_barrier(pe, l, 4)

            pe.wait_ge(pf["loads"], 64)

            def last(i):
                for s in range(2):
                    b = i * 2 + s
                    pe.wait_ge(pf_in[s], i * 32 + 32)
                    need(pe, pf["hT"], i, i * 2, s - 1)
                    for k in range(2):
                        t = nc.tensor.transpose(banks[s][:, P * k:P * (k + 1)], fh[s][:, P * k:P * (k + 1)],
                                                ident[:, :])
                    t.then_inc(pf["hT_psum"], 1)
                    pe.wait_ge(pf["hT"], b + 1)
                    for f in range(2):
                        for k in range(2):
                            t = mm(banks[2 + s][:, P * f:P * (f + 1)], fw1[:, k, P * f:P * (f + 1)], fhT[s][:, k, :],
                                   start=k == 0, stop=k == 1)
                    t.then_inc(pf["u_psum"], 1)
                    pe.wait_ge(pf["u"], (b + 1) * 2)
                    need(pe, pf["o"], i, i * 2, s - 1)
                    for k in range(2):
                        t = mm(banks[4 + s][:, 0:HID], fuT[s][:, k, :], fw2[:, k, :], start=k == 0, stop=k == 1)
                    t.then_inc(pf["o_psum"], 1)
            pairs(pe, last)


def kernel(x, src, dst, edge_attr_64, edge_type_3, L0_gnn_W1, L0_gnn_b1, L0_gnn_W2, L0_gnn_b2, L0_gnn_W_ih,
           L0_gnn_b_ih, L0_gnn_W_hh, L0_gnn_b_hh, L1_gnn_Win, L1_gnn_b_in, L1_gnn_Wq, L1_gnn_bq, L1_gnn_Wk,
           L1_gnn_bk, L1_gnn_Wv, L1_gnn_bv, L1_gnn_Eemb, L1_gnn_Wo, L1_gnn_bo, L1_gnn_ln_g, L1_gnn_ln_b, L1_gnn_W1,
           L1_gnn_b1, L1_gnn_W2, L1_gnn_b2):
    import numpy as np
    import concourse.bacc as bacc
    from concourse.bass_utils import run_bass_kernel_spmd

    def arr(v):
        return np.asarray(v)

    def edge_columns(v, fill):
        return np.concatenate([arr(v), np.full(EPAD - EDGES, fill, np.int32)]).reshape(P, COLS)

    def halves(wT):
        return wT.reshape(2, P, -1).transpose(1, 0, 2)

    def layers_T(w):
        return arr(w).transpose(0, 2, 1)

    W1 = arr(L0_gnn_W1)
    b1_row = np.zeros((1, 512), np.float32)
    b1_row[0, 0:HID] = arr(L0_gnn_b1)
    b2_rows = np.zeros((P, HID), np.float32)
    b2_rows[0] = arr(L0_gnn_b2)
    wqT = layers_T(L1_gnn_Wq).reshape(LAYERS, 2, P, HEADS, DH).transpose(0, 2, 1, 3, 4)
    wkvT = np.concatenate([layers_T(L1_gnn_Wk), layers_T(L1_gnn_Wv)], 2)
    bq = arr(L1_gnn_bq).reshape(LAYERS, HEADS, DH).transpose(0, 2, 1)
    eT = np.zeros((LAYERS, DH, HEADS, 4), np.float32)
    eT[:, :, :, 1:] = arr(L1_gnn_Eemb).reshape(LAYERS, TYPES, HEADS, DH).transpose(0, 3, 2, 1)
    arrays = {
        "x": np.concatenate([arr(x), np.zeros((NPAD - NODES, HID), np.float32)]),
        "src": edge_columns(src, -1), "dst": edge_columns(dst, 0), "typ": edge_columns(edge_type_3, 0),
        "attr": np.concatenate([arr(edge_attr_64), np.zeros((EPAD - EDGES, ATTR), np.float32)]),
        "w_pq": halves(np.concatenate([W1[:, 0:HID].T, W1[:, HID:2 * HID].T], 1)),
        "w1_attr": W1[:, 2 * HID:].T, "b1_row": b1_row,
        "w2_l0": halves(arr(L0_gnn_W2).T), "b2_rows": b2_rows,
        "w_gate": np.concatenate([halves(arr(L0_gnn_W_ih).T), halves(arr(L0_gnn_W_hh).T)], 1),
        "b_ih": arr(L0_gnn_b_ih), "b_hh": arr(L0_gnn_b_hh),
        "w_in": halves(arr(L1_gnn_Win).T), "b_in": arr(L1_gnn_b_in),
        "w_q": np.concatenate([wqT, wqT], 4).reshape(LAYERS * P, -1),
        "b_q": np.concatenate([bq, bq], 1).reshape(LAYERS * P, HEADS),
        "w_kv": wkvT.reshape(LAYERS, 2, P, 512).transpose(0, 2, 1, 3).reshape(LAYERS * P, -1),
        "b_kv": np.concatenate([arr(L1_gnn_bk), arr(L1_gnn_bv)], 1),
        "w_o": layers_T(L1_gnn_Wo).reshape(LAYERS, HEADS, DH, HID).transpose(0, 2, 1, 3).reshape(LAYERS * DH, -1),
        "e_T": eT.reshape(LAYERS * DH, -1), "b_o": arr(L1_gnn_bo),
        "ln_g": arr(L1_gnn_ln_g), "ln_b": arr(L1_gnn_ln_b),
        "w_f1": halves(arr(L1_gnn_W1).T), "b_f1": arr(L1_gnn_b1).reshape(2, P).T,
        "w_f2": halves(arr(L1_gnn_W2).T), "b_f2": arr(L1_gnn_b2),
    }
    arrays = {f"in_{k}": np.ascontiguousarray(v) for k, v in arrays.items()}
    nc = bacc.Bacc("TRN2", target_bir_lowering=False, num_devices=1)
    a = {k[3:]: nc.dram_tensor(k, v.shape, mybir.dt.from_np(v.dtype), kind="ExternalInput").ap()
         for k, v in arrays.items()}
    out = nc.dram_tensor("out", (NPAD, HID), F32, kind="ExternalOutput").ap()
    gnn(nc, a, out)
    r = run_bass_kernel_spmd(nc, [arrays], core_ids=[0])
    return r.results[0]["out"][:NODES]
```

```python
from contextlib import ExitStack

import concourse.bass as bass
from concourse import mybir

F32 = mybir.dt.float32
BF16 = mybir.dt.bfloat16
I32 = mybir.dt.int32
ALU = mybir.AluOpType
ACT = mybir.ActivationFunctionType
AX = mybir.AxisListType

P = 128
NODES, HID, EDGES, ATTR = 3125, 256, 50000, 64
HEADS, DH, LAYERS, TYPES = 4, 64, 3, 3
WIN = 16
WIN0 = 32
BLOCKS = 26
NPAD = BLOCKS * P
NWIN = NPAD // WIN
WPB = P // WIN
NWIN0, WPB0 = NWIN // 2, WPB // 2
RWIN = -(-NODES // WIN)
GT = 4
RING = 4
BODY = GT * RING
NEED = (EDGES + RWIN * (P - 1)) // P
ITERS = -(-NEED // BODY)
TILES = ITERS * BODY
TH = TILES // 2
GROUPS = TILES // GT
ROWS = TILES * P
COLS = 392
EPAD = P * COLS
CH = 7
CHUNKS = COLS // CH
QC = 56
NQ = COLS // QC
WPP = 26
PARTS = NWIN // WPP
PAIRS = QC // (2 * CH)
REC = 128
R_OH0, R_OH, R_CNT, R_DST, R_END = 64, 96, 112, 116, 117
PK = R_DST - R_OH
FAR = 1 << 22
NEGB = -(2.0 ** 100)
B_PREP, B_E0, B_N1, B_N2, PER_LAYER = 1, 2, 3, 4, 4
EPS = 1e-5


def gnn(nc, a, out):
    ctx = ExitStack()
    with ctx:
        def sb(name, shape, dt=F32):
            return ctx.enter_context(nc.sbuf_tensor(name, shape, dt))

        def sem(name):
            return ctx.enter_context(nc.semaphore(name))

        def sems(name, n):
            return [sem(f"{name}{i}") for i in range(n)]

        def dram(name, shape, dt=F32):
            return nc.dram_tensor(name, shape, dt).ap()

        rect = dram("edge_records", (ROWS, REC))
        packd = dram("edge_packs", (GROUPS, P, GT * PK))
        indexd = dram("edge_destinations", (GROUPS, P, GT))
        maskd = dram("edge_masks", (GROUPS, WIN, GT * P), BF16)
        qrows = dram("dst_rows", (NPAD, HID))
        kvrows = dram("kv_rows", (NPAD, 2 * HID))
        h0d = dram("h0", (NPAD, HID))
        h0Td = dram("h0T", (NPAD, HID))
        x1d = dram("x1", (NPAD, HID))
        based = dram("base", (NPAD, HID))
        hidd = dram("hidden", (NPAD, HID))
        yd = dram("y", (NPAD, HID))
        cntd = dram("counts", (4, NPAD))

        big = sb("big", [P, NWIN0, HID])
        work = sb("work", [P, NWIN0 * 96 + 6144])
        accr, node = work[:, 0:NWIN0 * 96], work[:, NWIN0 * 96:]
        ring = sb("ring", [P, BODY * 2 * HID])
        side = sb("side", [P, GT * HID])
        ident = sb("ident", [P, P])
        neg = sb("neg", [WIN, 4 * HEADS * WIN], BF16)
        wtab = sb("wtab", [P, TILES], I32)
        bst = sb("bst", [P, BLOCKS, 6])
        st4 = sb("st4", [P, 8, BLOCKS])
        rstd, nmr = st4[:, 0, :], st4[:, 1, :]
        banks = [ctx.enter_context(nc.psum_tensor(f"bank{i}", [P, 512], F32)) for i in range(8)]

        def at(region, off, *shape, parts=P):
            n = 1
            for d in shape:
                n *= d
            v = region[0:parts, off:off + n]
            if len(shape) == 2:
                v = v.rearrange("p (a b) -> p a b", a=shape[0])
            elif len(shape) == 3:
                v = v.rearrange("p (a b c) -> p a b c", a=shape[0], b=shape[1])
            return v

        phase_end, entered = sem("phase_end"), sem("entered")

        def events(phase, words):
            return {w: sem(f"{phase}_{w}") for w in words.split()}

        block = ctx.enter_context(nc.Block())

        def need(eng, s, i, base, count, peeled=0):
            if isinstance(i, int) and i == 0 and peeled + count <= 0:
                return
            eng.wait_ge(s, base + count)

        def hold(eng):
            eng.sem_inc(entered, 1)

        def barrier(eng, n):
            hold(eng)
            eng.drain().then_inc(phase_end, 1)
            eng.wait_ge(phase_end, n * 5)
            hold(eng)

        def layer_barrier(eng, l, k):
            barrier(eng, l * PER_LAYER + (B_N2 + k))

        def pairs(eng, body):
            body(0)
            with eng.Fori(1, BLOCKS // 2) as i:
                body(i)

        def ahead(eng, early, late):
            def body(i, more=True):
                early(i, 1)
                late(i, 0)
                if more:
                    early(i + 1, 0)
                late(i, 1)
            early(0, 0)
            body(0)
            with eng.Fori(1, BLOCKS // 2 - 1) as i:
                body(i)
            body(BLOCKS // 2 - 1, more=False)

        def bodies(eng, body):
            body(0)
            with eng.Fori(1, ITERS) as it:
                body(it)

        class Steps:

            def __init__(self, eng, s, n=0, per=0, base=0):
                self.eng, self.s, self.start, self.per, self.c = eng, s, n * per + base, per, 0

            def go(self, ins):
                ins.then_inc(self.s, 1)
                self.c += 1

            def wait(self):
                self.eng.wait_ge(self.s, self.start + self.c)

            def __call__(self, ins):
                self.go(ins)
                self.wait()

            def end(self):
                assert self.per in (0, self.c), (self.c, self.per)
                return self.c

        def rows(t, b, n=P):
            return t[bass.ds(b * P, n), :]

        def row_of(v):
            return v.rearrange("(a n) -> a n", a=1).broadcast_to([P, v.shape[0]])

        win = accr[:, 0:392]
        loc = accr[:, 392:784]
        typ = accr[:, 784:1176]
        pen = accr[:, 1176:1568]
        dsti = accr[:, 1568:1960].bitcast(I32)
        srci = accr[:, 1960:2352].bitcast(I32)
        typi = accr[:, 2352:2744].bitcast(I32)
        pos = accr[:, 2744:3136]
        loc0 = accr[:, 3136:3528]
        off, cnt, ntl, tbi, zrow = (accr[:, 3528 + NWIN * i:3528 + NWIN * (i + 1)] for i in range(5))
        toti = accr[:, 4568:4568 + NWIN].bitcast(I32)
        PE1 = QC + 1
        hot = at(accr, 4776, WPP, PE1)
        hotf = accr[:, 4776:4776 + WPP * PE1]
        run = at(accr, 6258, WPP, PE1)
        runf = accr[:, 6258:6258 + WPP * PE1]
        lemat = [accr[0:NWIN // 2, 4776 + TILES * z:4776 + TILES * (z + 1)] for z in range(2)]
        keep = at(accr, 7740, WPP, PE1)
        keepf = accr[:, 7740:7740 + WPP * PE1]
        placed = accr[:, 9222:9278]
        iwin = accr[:, 9278:9278 + NWIN]
        slot = [accr[:, 9784 + 8 * s:9784 + 8 * s + CH].bitcast(I32) for s in range(2)]
        ni, na, nb = (accr[:, 9800 + 8 * i:9800 + 8 * i + CH].bitcast(I32) for i in range(3))
        tcol = [accr[0:NWIN // 2, 9824 + z:9825 + z] for z in range(2)]
        iloc = accr[:, 9832:9832 + WIN0]
        ityp = accr[:, 9864:9867]
        prod = at(ring, BODY * HID - WPP * QC, WPP, QC)
        recc = [at(side, 0, CH, REC), at(ring, BODY * HID + 4 * 768, CH, REC)]
        xall = big[:, 0:BLOCKS, :]
        itile = ring[:, BODY * REC:BODY * REC + TILES]
        index0 = [node[:, 5200 + GT * g:5200 + GT * (g + 1)] for g in range(RING)]
        wtab0 = node[0:1, 4608:4608 + TILES].bitcast(I32)
        ones, before = node[:, 4096:4096 + P], node[:, 5216:5216 + P]
        blank = at(ring, 0, BODY, REC)
        wgate = at(ring, BODY * HID, 4, 768)
        w2l0 = at(node, 5376, 2, HID)
        b2x = node[:, 5888:6144]
        wpq = at(node, 0, 2, 512)
        b1row = node[0:1, 1024:1536]
        xb = [node[:, 1536 + 256 * s:1792 + 256 * s] for s in range(2)]
        hb = [node[:, 2048 + 256 * s:2304 + 256 * s] for s in range(2)]
        hT = [at(node, 2560 + 256 * s, 2, P) for s in range(2)]
        hTf = [node[:, 2560 + 256 * s:2816 + 256 * s] for s in range(2)]
        qst = [node[:, 3072 + 256 * s:3328 + 256 * s] for s in range(2)]
        rec = [at(node, 512 * g, GT, REC) for g in range(RING)]
        lh = [node[0:R_CNT, 2048 + P * k:2048 + P * (k + 1)] for k in range(GT)]
        pre = [node[:, 2560 + 256 * k:2816 + 256 * k] for k in range(GT)]
        act = [node[:, 3584 + 256 * k:3840 + 256 * k] for k in range(GT)]
        mk0 = [side[R_OH:R_CNT, 256 * g:256 * (g + 1)].bitcast(BF16) for g in range(RING)]
        qg = [ring[:, HID * t:HID * (t + 1)] for t in range(BODY)]
        acc0 = at(accr, 0, NWIN0, 96)
        E = NWIN * DH - NWIN0 * 96
        A = node[:, E:E + 1024].rearrange("p (k c n) -> p k c n", k=GT, c=16)
        pk = [at(node, E + 1024 + GT * PK * g, GT, PK) for g in range(RING)]
        index = [node[:, E + 2608 + GT * g:E + 2608 + GT * (g + 1)] for g in range(RING)]
        pkf = [node[:, E + 1024 + GT * PK * g:E + 1024 + GT * PK * (g + 1)] for g in range(RING)]
        mk = [node[0:WIN, E + 1360 + 256 * g:E + 1616 + 256 * g].bitcast(BF16) for g in range(RING)]
        kT = [side[:, HID * k:HID * (k + 1)] for k in range(GT)]
        sc = at(node, E + 2384, GT, 16)
        ex = at(node, E + 2448, GT, 16)
        exf = node[:, E + 2448:E + 2512]
        att = at(node, E + 2512, GT, 16)
        mx = at(node, E + 2576, GT, HEADS)
        sm = at(node, E + 2592, GT, HEADS)
        smf = node[:, E + 2592:E + 2608]
        kv = [ring[:, 2 * HID * t:2 * HID * (t + 1)] for t in range(BODY)]
        acc1 = at(work, 0, NWIN, DH, parts=DH)

        ghT = [at(node, 256 * s, 2, P) for s in range(2)]
        ghTf = [node[:, 256 * s:256 * s + 256] for s in range(2)]
        gh = [node[:, 512 + 256 * s:768 + 256 * s] for s in range(2)]
        gx = [node[:, 1024 + 256 * s:1280 + 256 * s] for s in range(2)]
        aggT = [at(node, 1536 + 256 * s, 2, P) for s in range(2)]
        aggTf = [node[:, 1536 + 256 * s:1792 + 256 * s] for s in range(2)]
        rz = [node[:, 2048 + 512 * s:2560 + 512 * s] for s in range(2)]
        cand = [node[:, 3072 + 256 * s:3328 + 256 * s] for s in range(2)]
        newx = [node[:, 3584 + 256 * s:3840 + 256 * s] for s in range(2)]
        gt = node[:, 4096:4352]
        brz, brzh = ring[:, 0:512], ring[:, 512:1024]
        bxn, bhn = ring[:, 1024:1280], ring[:, 1280:1536]
        iw = at(node, 0, 2, HID)
        ib = node[:, 512:768]
        ix = [node[:, 768 + 256 * s:1024 + 256 * s] for s in range(2)]
        ih = [node[:, 1280 + 256 * s:1536 + 256 * s] for s in range(2)]
        ihT = [at(node, 1792 + 256 * s, 2, P) for s in range(2)]
        ihTf = [node[:, 1792 + 256 * s:2048 + 256 * s] for s in range(2)]
        ibase = [node[:, 2304 + 256 * s:2560 + 256 * s] for s in range(2)]
        ihid = [node[:, 2816 + 256 * s:3072 + 256 * s] for s in range(2)]
        wq = node[:, 0:1024].rearrange("p (k h m) -> p k h m", k=2, h=HEADS)
        wkv = at(node, 1024, 2, 512)
        bq = node[:, 2048:2052]
        bkv = node[:, 2052:2564]
        ah = [node[:, 2564 + 256 * s:2820 + 256 * s] for s in range(2)]
        ahT = [at(node, 3076 + 256 * s, 2, P) for s in range(2)]
        ahTf = [node[:, 3076 + 256 * s:3332 + 256 * s] for s in range(2)]
        akv = [node[:, 3588 + 512 * s:4100 + 512 * s] for s in range(2)]
        QT = big[:, :, :].rearrange("p v (w g h n) -> p (v w) g h n", w=2, g=2, h=HEADS)
        QW = big[:, :, :].rearrange("p v (w f) -> p (v w) f", w=2)
        wo = at(ring, 0, HEADS, HID, parts=DH)
        eeT = at(ring, 1024, HEADS, 4, parts=DH)
        borow = ring[0:1, 1040:1296]
        eb = ring[0:4, 1296:1552]
        cst = [at(ring, 1552 + 512 * s, HEADS, P, parts=DH) for s in range(2)]
        cc = [ring[0:4, 2576 + P * s:2576 + P * (s + 1)] for s in range(2)]
        ch = [ring[:, 2832 + 256 * s:3088 + 256 * s] for s in range(2)]
        cy = [ring[:, 3344 + 256 * s:3600 + 256 * s] for s in range(2)]
        lng, lnb = node[:, 0:256], node[:, 256:512]
        dy = [node[:, 512 + 256 * s:768 + 256 * s] for s in range(2)]
        dt = [node[:, 1024 + 256 * s:1280 + 256 * s] for s in range(2)]
        du = [node[:, 1536 + 256 * s:1792 + 256 * s] for s in range(2)]
        fw1, fw2 = at(node, 0, 2, HID), at(node, 512, 2, HID)
        fb1, fb2 = node[:, 1024:1026], node[:, 1026:1282]
        fh = [node[:, 1282 + 256 * s:1538 + 256 * s] for s in range(2)]
        fhT = [at(node, 1794 + 256 * s, 2, P) for s in range(2)]
        fhTf = [node[:, 1794 + 256 * s:2050 + 256 * s] for s in range(2)]
        fuT = [at(node, 2306 + 256 * s, 2, P) for s in range(2)]
        fbase = [node[:, 2818 + 256 * s:3074 + 256 * s] for s in range(2)]
        fo = [node[:, 3330 + 256 * s:3586 + 256 * s] for s in range(2)]

        pr = events("pr", "consts idx weights x x_read var root norm cnt pre_psum tile_base base_psum below win_psum "
                          "blank cleared rec pool vstep rstep")
        pr_attr, pr_scat = sems("pr_attr", 2), sems("pr_scat", 2)
        n0 = events("n0", "h hT_psum hT pq_psum pq")
        n0_x, n0_h, n0_hT, n0_q = (sems(f"n0_{w}", 2) for w in ("x", "hst", "hTst", "qst"))
        e0 = events("e0", "T_psum T pre_psum pre act seg_psum added mask vstep ")
        e0_rec, e0_store = (sems(f"e0_{w}", RING) for w in ("rec", "store"))
        e0_q = sems("e0_q", RING)
        n1 = events("n1", "loads agg_psum aggT gate_psum rz_pre rz n_pre n x1 vstep")
        n1_hT, n1_in, n1_out = sems("n1_hT", 2), sems("n1_in", 2), sems("n1_out", 2)
        n2 = events("n2", "loads h hT_psum hT hid_psum base hid")
        n2_x, n2_out = sems("n2_x", 2), sems("n2_out", 2)
        pa = events("pa", "loads hT_psum hT q_psum kv_psum q kv")
        pa_in, pa_out = sems("pa_in", 2), sems("pa_out", 2)
        e1 = events("e1", "cleared T_psum T s_psum s_read shifted exp a o_psum added vstep vgroup")
        e1_in, e1_index = sems("e1_in", RING), sems("e1_index", RING)
        e1_kv = sems("e1_kv", RING)
        pb = events("pb", "loads eb_psum eb staged m_psum y vstep vstat var root")
        pb_in, pb_out = sems("pb_in", 2), sems("pb_out", 2)
        pc = events("pc", "loads t u o vstep")
        pc_in, pc_out = sems("pc_in", 2), sems("pc_out", 2)
        pf = events("pf", "loads hT_psum hT u_psum u o_psum o vstep")
        pf_in, pf_out = sems("pf_in", 2), sems("pf_out", 2)

        HALF = BLOCKS // 2

        def windows(engine, t, table, n):
            return nc.values_load_multi_w_load_instructions(
                table[0:1, bass.ds(t, GT)], engines=(engine,), min_val=0, max_val=n - 1,
                skip_runtime_bounds_check_because="the preparation cuts every entry at NWIN - 1")[1]

        def sum_bank(g):
            return banks[6 + g % 2]

        STAT_STEPS = 14

        def stats_v(step, var, root, n):
            v = nc.vector
            mean, var_, t0, t1, root_ = (st4[:, j, :] for j in range(2, 7))
            me, m2e, mo, m2o = bst[:, :, 1], bst[:, :, 2], bst[:, :, 4], bst[:, :, 5]
            step(v.tensor_tensor(t0, me, mo, ALU.subtract))
            step(v.tensor_tensor(mean, me, mo, ALU.add))
            step(v.tensor_scalar(mean, mean, 0.5, None, ALU.mult))
            step(v.tensor_scalar(t0, t0, 0.5, None, ALU.mult))
            step(v.tensor_tensor(t0, t0, t0, ALU.mult))
            step(v.tensor_tensor(t1, m2e, m2o, ALU.add))
            step(v.tensor_scalar(t1, t1, 1.0 / HID, EPS, ALU.mult, ALU.add))
            v.tensor_tensor(var_, t0, t1, ALU.add).then_inc(var, 1)
            v.wait_ge(root, n)
            step(v.reciprocal(rstd, root_))
            step(v.tensor_tensor(t0, rstd, rstd, ALU.mult))
            step(v.tensor_tensor(t0, t0, var_, ALU.mult))
            step(v.tensor_scalar(t0, t0, -0.5, 1.5, ALU.mult, ALU.add))
            step(v.tensor_tensor(rstd, rstd, t0, ALU.mult))
            step(v.tensor_tensor(t1, mean, rstd, ALU.mult))
            step(v.tensor_scalar(nmr, t1, -1.0, None, ALU.mult))

        def stats_a(var, root, n):
            nc.scalar.wait_ge(var, n)
            hold(nc.scalar)
            nc.scalar.activation(st4[:, 6, :], st4[:, 3, :], ACT.Sqrt).then_inc(root, 1)

        @block.sync
        def _(sp):
            def after(s, count):
                sp.wait_ge(s, count)
                hold(sp)

            def need_sp(s, i, base, count):
                if not (isinstance(i, int) and count <= 0):
                    after(s, base + count)

            for v, w in ((srci, "src"), (dsti, "dst"), (typi, "typ")):
                sp.dma_start(v, a[w]).then_inc(pr["idx"], 16)

            sp.dma_start(xall, a["x"].rearrange("(b p) f -> p b f", p=P)).then_inc(pr["x"], 16)
            for v, w in ((wpq, "w_pq"), (b1row, "b1_row"), (w2l0, "w2_l0"), (b2x, "b2_rows")):
                sp.dma_start(v, a[w]).then_inc(pr["weights"], 16)
            for half in range(4):
                sp.dma_start(wgate[:, half, :], a["w_gate"][:, half, :]).then_inc(pr["weights"], 16)
            def load_x_again(i):
                for s in range(2):
                    need_sp(n0["h"], i, i * 2, s - 1)
                    sp.dma_start(xb[s], rows(a["x"], i * 2 + s)).then_inc(n0_x[s], 16)

            def load_attr(i):
                for s in range(2):
                    if isinstance(i, int):
                        after(pr["cleared"], 1)
                    else:
                        after(pr_scat[s], i * (16 * CH))
                    sp.dma_start(recc[s][:, :, 0:ATTR], a["attr"].rearrange("(p c) f -> p c f", p=P)[
                        :, bass.ds(i * (2 * CH) + s * CH, CH), :]).then_inc(pr_attr[s], 16)
            load_attr(0)
            after(pr["x_read"], BLOCKS)
            sp.dma_start(big[0:ATTR, :, :], a["w1_attr"].unsqueeze(1).broadcast_to([ATTR, NWIN0, HID])
                         ).then_inc(pr["weights"], 16)
            load_x_again(0)
            with sp.Fori(1, HALF) as i:
                load_attr(i)
                load_x_again(i)
            with sp.Fori(HALF, CHUNKS // 2) as i:
                load_attr(i)
            after(pr["weights"], 144)
            barrier(sp, B_PREP)

            def load_records(it, g):
                if not isinstance(it, int):
                    after(e0["seg_psum"], it * BODY + (g + 1 - RING) * GT)
                    after(e0_store[g], it * 48)
                sp.dma_start(rec[g], rect[bass.ds((it * RING + g) * (GT * P), GT * P), :]
                             .rearrange("(p k) f -> p k f", k=GT)).then_inc(e0_rec[g], 16)

            def store_pack(it, g):
                after(e0_rec[g], it * 16 + 16)
                sp.dma_start(packd[bass.ds(it * RING + g, 1), :, :].rearrange("a p (k f) -> (a p) k f", k=GT),
                             rec[g][:, :, R_OH:R_DST]).then_inc(e0_store[g], 16)
                after(e0["mask"], it * BODY + (g + 1) * GT)
                after(e0["vstep"], it * RING + (g + 4))
                sp.dma_start(indexd[bass.ds(it * RING + g, 1), :, :].rearrange("a p k -> (a p) k"), index0[g]
                             ).then_inc(e0_store[g], 16)
                sp.dma_start(maskd[bass.ds(it * RING + g, 1), :, :].rearrange("a p f -> (a p) f"),
                             mk0[g]).then_inc(e0_store[g], 16)

            for g in range(RING):
                load_records(0, g)
            with sp.Fori(1, ITERS) as it:
                for g in range(RING):
                    store_pack(it - 1, g)
                    load_records(it, g)
            for g in range(RING):
                store_pack(ITERS - 1, g)
            for g in range(RING):
                after(e0_store[g], 48 * ITERS)
            barrier(sp, B_E0)

            sp.dma_start(cntd.rearrange("c (w n) -> c w n", n=WIN0), acc0[0:4, :, 64:96]
                         ).then_inc(n1["loads"], 16)
            for v, w in ((brz, a["b_ih"][0:512]), (brzh, a["b_hh"][0:512]), (bxn, a["b_ih"][512:768]),
                         (bhn, a["b_hh"][512:768])):
                sp.dma_start(v, row_of(w)).then_inc(n1["loads"], 16)

            def load_gate(i):
                for s in range(2):
                    b = i * 2 + s
                    need_sp(n1["gate_psum"], i, i * 2, s - 1)
                    sp.dma_start(ghTf[s], rows(h0Td, b)).then_inc(n1_hT[s], 16)
                    need_sp(n1["x1"], i, i * 2, s - 1)
                    for v, t in ((gh[s], h0d), (gx[s], a["x"])):
                        sp.dma_start(v, rows(t, b)).then_inc(n1_in[s], 16)
            pairs(sp, load_gate)
            after(n1["loads"], 80)
            barrier(sp, B_N1)

            sp.dma_start(iw, a["w_in"]).then_inc(n2["loads"], 16)
            sp.dma_start(ib, row_of(a["b_in"])).then_inc(n2["loads"], 16)

            def load_entry(i):
                for s in range(2):
                    need_sp(n2["base"], i, i * 2, s - 1)
                    sp.dma_start(ix[s], rows(x1d, i * 2 + s)).then_inc(n2_x[s], 16)
            pairs(sp, load_entry)
            barrier(sp, B_N2)

            with sp.Fori(0, LAYERS) as l:
                def lay(w):
                    return a[w][bass.ds(l * (a[w].shape[0] // LAYERS), a[w].shape[0] // LAYERS)]
                sp.dma_start(node[:, 0:1024], lay("w_q")).then_inc(pa["loads"], 16)
                sp.dma_start(node[:, 1024:2048], lay("w_kv")).then_inc(pa["loads"], 16)
                sp.dma_start(bq, lay("b_q")).then_inc(pa["loads"], 16)
                sp.dma_start(bkv, lay("b_kv").broadcast_to([P, 512])).then_inc(pa["loads"], 16)

                def load_hidden(i):
                    for s in range(2):
                        need_sp(pa["hT_psum"], i, l * BLOCKS + i * 2, s - 1)
                        sp.dma_start(ah[s], rows(hidd, i * 2 + s)).then_inc(pa_in[s], 16)
                pairs(sp, load_hidden)
                layer_barrier(sp, l, 1)

                def load_pack(it):
                    for g in range(RING):
                        n = it * RING + g
                        if not isinstance(it, int):
                            after(e1_kv[g], (l * ITERS + it) * (16 * GT))
                        sp.dma_start(index[g], indexd[bass.ds(n, 1), :, :].rearrange("a p k -> (a p) k")
                                     ).then_inc(e1_index[g], 16)
                        if not isinstance(it, int):
                            after(e1["a"], l * TILES + it * BODY + (g + 1 - RING) * GT)
                            after(e1["s_psum"], l * TILES + it * BODY + (g + 1 - RING) * GT)
                        sp.dma_start(pkf[g], packd[bass.ds(n, 1), :, :].rearrange("a p f -> (a p) f")
                                     ).then_inc(e1_in[g], 16)
                        sp.dma_start(mk[g], maskd[bass.ds(n, 1), :, :].rearrange("a p f -> (a p) f")
                                     ).then_inc(e1_in[g], 16)
                bodies(sp, load_pack)
                layer_barrier(sp, l, 2)

                sp.dma_start(ring[0:DH, 0:1024], lay("w_o")).then_inc(pb["loads"], 16)
                sp.dma_start(ring[0:DH, 1024:1040], lay("e_T")).then_inc(pb["loads"], 16)
                sp.dma_start(borow, lay("b_o")).then_inc(pb["loads"], 16)

                def load_residual(i):
                    for s in range(2):
                        b = i * 2 + s
                        need_sp(pb["y"], i, l * BLOCKS + i * 2, s - 1)
                        sp.dma_start(ch[s], rows(hidd, b)).then_inc(pb_in[s], 16)
                        sp.dma_start(cc[s], cntd[:, bass.ds(b * P, P)]).then_inc(pb_in[s], 16)
                pairs(sp, load_residual)
                layer_barrier(sp, l, 3)

                sp.dma_start(lng, lay("ln_g").broadcast_to([P, HID])).then_inc(pc["loads"], 16)
                sp.dma_start(lnb, lay("ln_b").broadcast_to([P, HID])).then_inc(pc["loads"], 16)

                def load_sum(i):
                    for s in range(2):
                        need_sp(pc["t"], i, l * BLOCKS + i * 2, s - 1)
                        sp.dma_start(dy[s], rows(yd, i * 2 + s)).then_inc(pc_in[s], 16)

                def store_odd(i):
                    after(pc["o"], l * BLOCKS + i * 2 + 2)
                    sp.dma_start(rows(hidd, i * 2 + 1), du[1]).then_inc(pc_out[1], 16)
                load_sum(0)
                with sp.Fori(1, HALF) as i:
                    load_sum(i)
                    store_odd(i - 1)
                store_odd(HALF - 1)
                after(pc_out[1], (l + 1) * (16 * HALF))
                layer_barrier(sp, l, 4)

            for v, w in ((fw1, "w_f1"), (fw2, "w_f2"), (fb1, "b_f1")):
                sp.dma_start(v, a[w]).then_inc(pf["loads"], 16)
            sp.dma_start(fb2, row_of(a["b_f2"])).then_inc(pf["loads"], 16)

            def load_last(i):
                for s in range(2):
                    b = i * 2 + s
                    need_sp(pf["o"], i, i * 2, s - 1)
                    sp.dma_start(fh[s], rows(hidd, b)).then_inc(pf_in[s], 16)
                    sp.dma_start(fbase[s], rows(based, b)).then_inc(pf_in[s], 16)
            pairs(sp, load_last)

        @block.gpsimd
        def _(pool):
            steps = Steps(pool, pr["pool"])
            for m in (ident, before, ones):
                last = pool.memset(m[:, :], 1.0 if m is ones else 0.0)
                steps(last)
            steps(pool.affine_select(out=ident[:, :], in_=ident[:, :], compare_op=ALU.not_equal, fill=1.0, base=0,
                                     pattern=[[-1, P]], channel_multiplier=1))
            steps(pool.affine_select(out=before[:, :], in_=before[:, :], compare_op=ALU.is_ge, fill=1.0, base=0,
                                     pattern=[[-1, P]], channel_multiplier=1))
            steps(pool.memset(neg[:, :], 0.0))
            steps(pool.affine_select(out=neg[:, :].rearrange("p (c n) -> p c n", n=WIN),
                                     in_=neg[:, :].rearrange("p (c n) -> p c n", n=WIN),
                                     compare_op=ALU.not_equal, fill=NEGB, base=0, pattern=[[0, 16], [-1, WIN]],
                                     channel_multiplier=1))
            for v, n in ((iwin, NWIN), (iloc, WIN0), (ityp, TYPES), (itile, TILES)):
                steps(pool.iota(v, pattern=[[1, n]], base=0, channel_multiplier=0,
                                allow_small_or_imprecise_dtypes=True))
            for v, val in ((keepf, 1.0), (zrow, 0.0), (pos, 0.0)):
                steps(pool.memset(v, val))
            steps(pool.memset(keep[:, :, 0:1], 0.0))
            pool.sem_inc(pr["consts"], 1)
            steps(pool.memset(blank[:, :, :], 0.0))
            steps(pool.memset(blank[:, :, R_DST:R_DST + 1].bitcast(I32), FAR))
            for s in range(2):
                steps(pool.memset(recc[s], 0.0))
                steps(pool.memset(recc[s][:, :, R_CNT:R_CNT + 1], 1.0))
            pool.sem_inc(pr["cleared"], 1)
            all_rows = pool.to_reg(ROWS - 1)
            all_nodes = pool.to_reg(NPAD - 1)
            with pool.Fori(0, ITERS) as i:
                pool.dma_start(rect[bass.ds(i * (BODY * P), BODY * P), :].rearrange("(p k) f -> p k f", k=BODY),
                               blank).then_inc(pr["blank"], 16)
            pool.wait_ge(pr["blank"], 16 * ITERS)

            def scatter(i):
                for s in range(2):
                    pool.wait_ge(pr["rec"], i * 2 + (s + 1))
                    pool.wait_ge(pr_attr[s], i * 16 + 16)
                    hold(pool)
                    for j in range(CH):
                        pool.indirect_dma_start(rect, bass.IndirectOffsetOnAxis(ap=slot[s][:, j:j + 1], axis=0),
                                                recc[s][:, j, :], None, bounds_check=all_rows, oob_is_err=False
                                                ).then_inc(pr_scat[s], 16)
            scatter(0)
            with pool.Fori(1, CHUNKS // 2) as i:
                scatter(i)
            for s in range(2):
                pool.wait_ge(pr_scat[s], 16 * CH * (CHUNKS // 2))
            barrier(pool, B_PREP)

            steps(pool.memset(ring[:, 0:BODY * HID], 0.0))
            pool.memset(ring[:, BODY * HID + 4 * 768:], 0.0)

            def gather_rows(it):
                for g in range(RING):
                    pool.wait_ge(e0_rec[g], it * 16 + 16)
                    hold(pool)
                    for k in range(GT):
                        t = GT * g + k
                        if not isinstance(it, int):
                            pool.wait_ge(e0["pre"], it * BODY + (t + 1 - BODY))
                            hold(pool)
                        pool.indirect_dma_start(qg[t], None, qrows, bass.IndirectOffsetOnAxis(
                            ap=rec[g][:, k, R_DST:R_DST + 1].bitcast(I32), axis=0), bounds_check=all_nodes,
                            oob_is_err=False).then_inc(e0_q[g], 16)
            bodies(pool, gather_rows)
            barrier(pool, B_E0)

            def store_x1(i):
                for s in range(2):
                    pool.wait_ge(n1["x1"], i * 2 + (s + 1))
                    hold(pool)
                    pool.dma_start(rows(x1d, i * 2 + s), newx[s]).then_inc(n1_out[s], 16)
            pairs(pool, store_x1)
            for s in range(2):
                pool.wait_ge(n1_out[s], 16 * HALF)
            barrier(pool, B_N1)

            pool.memset(QW[0:64, :, 64:128], 0.0)
            pool.memset(QW[64:128, :, 0:64], 0.0)

            def store_entry(i):
                for s in range(2):
                    b = i * 2 + s
                    pool.wait_ge(n2["base"], i * 2 + (s + 1))
                    hold(pool)
                    pool.dma_start(rows(based, b), ibase[s]).then_inc(n2_out[s], 16)
                    pool.wait_ge(n2["hid"], i * 2 + (s + 1))
                    hold(pool)
                    pool.dma_start(rows(hidd, b), ihid[s]).then_inc(n2_out[s], 16)
            pairs(pool, store_entry)
            for s in range(2):
                pool.wait_ge(n2_out[s], 32 * HALF)
            barrier(pool, B_N2)

            with pool.Fori(0, LAYERS) as l:
                pool.memset(accr[0:DH, :], 0.0)

                def store_kv(i):
                    for s in range(2):
                        pool.wait_ge(pa["kv"], l * BLOCKS + i * 2 + (s + 1))
                        hold(pool)
                        pool.dma_start(rows(kvrows, i * 2 + s), akv[s]).then_inc(pa_out[s], 16)
                pairs(pool, store_kv)
                for s in range(2):
                    pool.wait_ge(pa_out[s], (l + 1) * (16 * HALF))
                layer_barrier(pool, l, 1)

                def gather_kv(it):
                    for g in range(RING):
                        pool.wait_ge(e1_index[g], (l * ITERS + it) * 16 + 16)
                        hold(pool)
                        for k in range(GT):
                            t = GT * g + k
                            if not isinstance(it, int):
                                pool.wait_ge(e1["o_psum"], l * TILES + it * BODY + (t + 1 - BODY))
                                hold(pool)
                            pool.indirect_dma_start(kv[t], None, kvrows, bass.IndirectOffsetOnAxis(
                                ap=index[g][:, k:k + 1].bitcast(I32), axis=0), bounds_check=all_nodes,
                                oob_is_err=False).then_inc(e1_kv[g], 16)
                bodies(pool, gather_kv)
                layer_barrier(pool, l, 2)

                def store_sum(i):
                    for s in range(2):
                        pool.wait_ge(pb["y"], l * BLOCKS + i * 2 + (s + 1))
                        hold(pool)
                        pool.dma_start(rows(yd, i * 2 + s), cy[s]).then_inc(pb_out[s], 16)
                pairs(pool, store_sum)
                for s in range(2):
                    pool.wait_ge(pb_out[s], (l + 1) * (16 * HALF))
                layer_barrier(pool, l, 3)

                def store_even(i):
                    pool.wait_ge(pc["o"], l * BLOCKS + i * 2 + 1)
                    hold(pool)
                    pool.dma_start(rows(hidd, i * 2), du[0]).then_inc(pc_out[0], 16)
                pairs(pool, store_even)
                pool.wait_ge(pc_out[0], (l + 1) * (16 * HALF))
                layer_barrier(pool, l, 4)

            def store_out(i):
                for s in range(2):
                    pool.wait_ge(pf["o"], i * 2 + (s + 1))
                    hold(pool)
                    pool.dma_start(rows(out, i * 2 + s), fo[s]).then_inc(pf_out[s], 16)
            pairs(pool, store_out)
            for s in range(2):
                pool.wait_ge(pf_out[s], 16 * HALF)

        @block.scalar
        def _(act_):
            sc_ = nc.scalar
            stats_a(pr["var"], pr["root"], 1)
            act_.wait_ge(pr["norm"], 1)

            def nodes0(i):
                for s in range(2):
                    b = i * 2 + s
                    act_.wait_ge(n0_x[s], i * 16 + 16)
                    need(act_, n0["hT_psum"], i, i * 2, s - 1)
                    need(act_, n0_h[s], i, 0, i * 16)
                    hold(act_)
                    sc_.activation(hb[s], xb[s], ACT.Relu, bias=nmr[:, bass.ds(b, 1)],
                                   scale=rstd[:, bass.ds(b, 1)]).then_inc(n0["h"], 1)
                    act_.wait_ge(n0["h"], i * 2 + (s + 1))
                    act_.dma_start(rows(h0d, b), hb[s]).then_inc(n0_h[s], 16)
                    act_.wait_ge(n0["hT_psum"], i * 2 + (s + 1))
                    need(act_, n0["pq_psum"], i, i * 2, s - 1)
                    need(act_, n0_hT[s], i, 0, i * 16)
                    hold(act_)
                    sc_.activation(hTf[s], banks[s][:, 0:256], ACT.Copy).then_inc(n0["hT"], 1)
                    act_.wait_ge(n0["hT"], i * 2 + (s + 1))
                    act_.dma_start(rows(h0Td, b), hTf[s]).then_inc(n0_hT[s], 16)
                    act_.wait_ge(n0["pq_psum"], i * 2 + (s + 1))
                    need(act_, n0_q[s], i, 0, i * 16)
                    hold(act_)
                    for w in range(WPB0):
                        sc_.activation(big[64:96, bass.ds(b * WPB0 + w, 1), :].rearrange("p a n -> p (a n)"),
                                       banks[2 + s][WIN0 * w:WIN0 * (w + 1), 0:256], ACT.Copy).then_inc(n0["pq"], 1)
                    sc_.activation(qst[s], banks[2 + s][:, 256:512], ACT.Copy).then_inc(n0["pq"], 1)
                    act_.wait_ge(n0["pq"], (i * 2 + (s + 1)) * 5)
                    act_.dma_start(rows(qrows, b), qst[s]).then_inc(n0_q[s], 16)
            pairs(act_, nodes0)
            for s in range(2):
                for q in (n0_h, n0_hT, n0_q):
                    act_.wait_ge(q[s], 16 * HALF)
            barrier(act_, B_PREP)

            def edges0(it):
                for g in range(RING):
                    n = it * BODY + g * GT
                    for k in range(GT):
                        act_.wait_ge(e0["T_psum"], n + (k + 1))
                        need(act_, e0["pre_psum"], it, n, k + 1 - GT, g * GT)
                        need(act_, e0["mask"], it, n, k + 1 - GT, g * GT)
                        hold(act_)
                        sc_.activation(lh[k], banks[k % 2][0:R_CNT, 0:P], ACT.Copy).then_inc(e0["T"], 1)
                        if not (isinstance(it, int) and g == 0):
                            relu0(it, g, n - GT, k)

            def relu0(it, g, n, k):
                act_.wait_ge(e0["pre"], n + (k + 1))
                need(act_, e0["seg_psum"], it, n, k + 1 - GT, (g - 1) * GT)
                hold(act_)
                sc_.activation(act[k], pre[k], ACT.Relu).then_inc(e0["act"], 1)
            bodies(act_, edges0)
            for k in range(GT):
                relu0(ITERS, 0, TILES - GT, k)
            barrier(act_, B_E0)

            def aggregate(i, s):
                act_.wait_ge(n1["agg_psum"], i * 2 + (s + 1))
                need(act_, n1["gate_psum"], i, i * 2, s - 1)
                hold(act_)
                sc_.activation(aggTf[s], banks[s][:, 0:256], ACT.Copy).then_inc(n1["aggT"], 1)

            def gates(i, s):
                act_.wait_ge(n1["rz_pre"], i * 2 + (s + 1))
                hold(act_)
                sc_.activation(rz[s], rz[s], ACT.Sigmoid).then_inc(n1["rz"], 1)
                act_.wait_ge(n1["n_pre"], i * 2 + (s + 1))
                hold(act_)
                sc_.activation(cand[s], cand[s], ACT.Tanh).then_inc(n1["n"], 1)
            ahead(act_, aggregate, gates)
            stats_a(pr["var"], pr["root"], 2)
            barrier(act_, B_N1)

            def entry(i):
                for s in range(2):
                    b = i * 2 + s
                    act_.wait_ge(n2_x[s], i * 16 + 16)
                    need(act_, n2["hT_psum"], i, i * 2, s - 1)
                    need(act_, n2["base"], i, i * 2, s - 1)
                    hold(act_)
                    sc_.activation(ih[s], ix[s], ACT.Relu, bias=nmr[:, bass.ds(b, 1)],
                                   scale=rstd[:, bass.ds(b, 1)]).then_inc(n2["h"], 1)
                    act_.wait_ge(n2["hT_psum"], b + 1)
                    need(act_, n2["hid_psum"], i, i * 2, s - 1)
                    hold(act_)
                    sc_.activation(ihTf[s], banks[s][:, 0:256], ACT.Copy).then_inc(n2["hT"], 1)
            pairs(act_, entry)
            barrier(act_, B_N2)

            with act_.Fori(0, LAYERS) as l:
                def project(i):
                    for s in range(2):
                        n = l * BLOCKS + i * 2
                        act_.wait_ge(pa["hT_psum"], n + (s + 1))
                        need(act_, pa["kv_psum"], i, n, s - 1)
                        hold(act_)
                        sc_.activation(ahTf[s], banks[s][:, 0:256], ACT.Copy).then_inc(pa["hT"], 1)
                pairs(act_, project)
                layer_barrier(act_, l, 1)

                def exps(n):
                    act_.wait_ge(e1["shifted"], l * GROUPS + n)
                    hold(act_)
                    sc_.activation(exf, exf, ACT.Exp, scale=DH ** -0.5).then_inc(e1["exp"], 1)

                def edges1(it):
                    for g in range(RING):
                        n = l * TILES + it * BODY + g * GT
                        for k in range(GT):
                            act_.wait_ge(e1["T_psum"], n + (k + 1))
                            if not (isinstance(it, int) and g == 0):
                                act_.wait_ge(e1["s_psum"], n + (k + 1 - GT))
                            hold(act_)
                            sc_.activation(kT[k], banks[k % 2][:, 0:256], ACT.Copy).then_inc(e1["T"], 1)
                            if k == 1 and not (isinstance(it, int) and g == 0):
                                exps(it * RING + g)
                bodies(act_, edges1)
                exps(GROUPS)
                layer_barrier(act_, l, 2)

                act_.wait_ge(pb["eb_psum"], l + 1)
                hold(act_)
                sc_.activation(eb, banks[7][0:4, 0:HID], ACT.Copy).then_inc(pb["eb"], 1)

                def output(i):
                    for s in range(2):
                        b, n = i * 2 + s, l * BLOCKS + i * 2
                        need(act_, pb["m_psum"], i, n, s - 1)
                        if not isinstance(i, int):
                            hold(act_)
                        sc_.activation(cst[s].rearrange("p h (w n) -> p w h n", w=WPB),
                                       acc1[:, bass.ds(b * WPB, WPB), :].rearrange("p w (h n) -> p w h n", h=HEADS),
                                       ACT.Copy).then_inc(pb["staged"], 1)
                pairs(act_, output)
                stats_a(pb["var"], pb["root"], l + 1)
                layer_barrier(act_, l, 3)

                def norm(i):
                    for s in range(2):
                        b, n = i * 2 + s, l * BLOCKS + i * 2
                        act_.wait_ge(pc_in[s], (l * HALF + i) * 16 + 16)
                        need(act_, pc["u"], i, n, s - 1)
                        hold(act_)
                        sc_.activation(dt[s], dy[s], ACT.Identity, bias=nmr[:, bass.ds(b, 1)],
                                       scale=rstd[:, bass.ds(b, 1)]).then_inc(pc["t"], 1)
                pairs(act_, norm)
                layer_barrier(act_, l, 4)

            act_.wait_ge(pf["loads"], 64)

            def last(i):
                for s in range(2):
                    b = i * 2 + s
                    act_.wait_ge(pf["hT_psum"], b + 1)
                    need(act_, pf["u_psum"], i, i * 2, s - 1)
                    hold(act_)
                    sc_.activation(fhTf[s], banks[s][:, 0:256], ACT.Copy).then_inc(pf["hT"], 1)
                    act_.wait_ge(pf["u_psum"], b + 1)
                    need(act_, pf["o_psum"], i, i * 2, s - 1)
                    hold(act_)
                    for j in range(2):
                        sc_.activation(fuT[s][:, j, :], banks[2 + s][:, P * j:P * (j + 1)], ACT.Relu,
                                       bias=fb1[:, j:j + 1]).then_inc(pf["u"], 1)
            pairs(act_, last)

        @block.vector
        def _(v):
            step = Steps(v, pr["vstep"])
            v.wait_ge(pr["idx"], 48)
            v.wait_ge(pr["consts"], 1)
            hits = [hotf[:, 0:COLS], runf[:, 0:COLS]]
            scratch = hits[0].bitcast(I32)
            step(v.tensor_scalar(scratch, srci, 4, None, ALU.arith_shift_right))
            step(v.tensor_copy(win, scratch))
            step(v.tensor_scalar(scratch, srci, WIN - 1, None, ALU.bitwise_and))
            step(v.tensor_copy(loc, scratch))
            step(v.tensor_scalar(scratch, srci, WIN0 - 1, None, ALU.bitwise_and))
            step(v.tensor_copy(loc0, scratch))
            step(v.tensor_copy(typ, typi))
            step(v.tensor_scalar(pen, win, 0.0, float(FAR), ALU.is_lt, ALU.mult))
            step(v.tensor_scalar(pen, pen, -1.0, None, ALU.add))
            v.sem_inc(pr["cnt"], 2)
            with v.Fori(0, NWIN // 2) as i:
                for s in range(2):
                    w = bass.ds(i * 2 + s, 1)
                    v.wait_ge(pr["cnt"], i * 2 + (s + 1))
                    v.tensor_scalar(hits[s], win, iwin[:, w], 0.0, ALU.is_equal, ALU.add,
                                    accum_out=cnt[:, w]).then_inc(pr["cnt"], 1)
            v.wait_ge(pr["cnt"], NWIN + 2)
            hold(v)
            v.sem_inc(pr["tile_base"], 1)
            v.wait_ge(pr["x"], 16)
            with v.Fori(0, BLOCKS // 2) as i:
                for s in range(2):
                    b = bass.ds(i * 2 + s, 1)
                    v.bn_stats(bst[:, b, :].rearrange("p a c -> p (a c)"), xall[:, b, :].rearrange("p a f -> p (a f)")
                               ).then_inc(pr["x_read"], 1)
            v.wait_ge(pr["x_read"], BLOCKS)
            stats_v(step, pr["var"], pr["root"], 1)
            v.sem_inc(pr["norm"], 1)
            v.wait_ge(pr["pre_psum"], 1)
            step(v.tensor_scalar(toti, banks[4][:, 256:256 + NWIN], float(P - 1), None, ALU.add))
            step(v.tensor_scalar(toti, toti, 7, None, ALU.arith_shift_right))
            step(v.tensor_copy(ntl, toti))
            step(v.tensor_tensor_scan(tbi, ntl, zrow, 0.0, ALU.add, ALU.add))
            v.sem_inc(pr["tile_base"], 1)
            step(v.tensor_tensor(off, tbi, ntl, ALU.subtract))
            step(v.tensor_scalar(off, off, float(P), None, ALU.mult))
            step(v.tensor_tensor(off, off, banks[4][:, 0:NWIN], ALU.add))
            v.wait_ge(pr["base_psum"], 1)
            for z in range(2):
                step(v.tensor_copy(tcol[z], banks[5][0:NWIN // 2, P * z:P * z + 1]))
                v.tensor_scalar(lemat[z], itile[0:NWIN // 2, :], tcol[z], None, ALU.is_ge).then_inc(pr["below"], 1)
            v.wait_ge(pr["win_psum"], 1)
            for z in range(2):
                step(v.tensor_scalar(wtab[:, z * TH:(z + 1) * TH], banks[6 + z][:, 0:TH], float(NWIN - 1), None,
                                     ALU.min))
            step(v.tensor_scalar(wtab0, wtab[0:1, :], 1, None, ALU.arith_shift_right))

            RANK = 7

            class Rank:

                def __init__(self, q, j, n):
                    self.st = Steps(v, pr["vstep"], n, RANK, rank_start)
                    self.cols, self.ws = bass.ds(q * QC, QC), bass.ds(j * WPP, WPP)

                def offsets(self):
                    self.st.go(v.tensor_copy(hot[:, :, 0:1], off[:, self.ws].unsqueeze(2)))

                def compare(self):
                    self.st.wait()
                    self.st.go(v.tensor_tensor(
                        hot[:, :, 1:PE1], win[:, self.cols].unsqueeze(1).broadcast_to([P, WPP, QC]),
                        iwin[:, self.ws].unsqueeze(2).broadcast_to([P, WPP, QC]), ALU.is_equal))

                def count(self):
                    self.st.wait()
                    self.st.go(v.tensor_tensor_scan(runf, keepf, hotf, 0.0, ALU.mult, ALU.add))

                def carry(self):
                    self.st.wait()
                    hold(v)
                    self.st.go(v.tensor_copy(off[:, self.ws].unsqueeze(2), run[:, :, QC:PE1]))

                def select(self):
                    self.st.go(v.tensor_tensor(prod, run[:, :, 1:PE1], hot[:, :, 1:PE1], ALU.mult))

                def reduce(self):
                    self.st.wait()
                    self.st.go(v.tensor_reduce(placed, prod.rearrange("p w c -> p c w"), AX.X, ALU.add))

                def place(self):
                    self.st.wait()
                    self.st.go(v.tensor_tensor(pos[:, self.cols], pos[:, self.cols], placed, ALU.add))
                    self.st.wait()

                def whole(self):
                    self.offsets(), self.compare(), self.count(), self.carry(), self.select(), self.reduce()
                    self.place()

            RECS = 10

            def record(i, s, r=None):
                cols = bass.ds(i * (2 * CH) + s * CH, CH)
                if isinstance(i, int):
                    v.wait_ge(pr["cleared"], 1)
                else:
                    v.wait_ge(pr_scat[s], i * (16 * CH))
                st = Steps(v, pr["rstep"], i * 2 + s, RECS)

                def one_hot(first, n, l):
                    st.go(v.tensor_tensor(recc[s][:, :, first:first + n],
                                          l[:, cols].unsqueeze(2).broadcast_to([P, CH, n]),
                                          iloc[:, 0:n].unsqueeze(1).broadcast_to([P, CH, n]), ALU.is_equal))
                if r:
                    r.offsets()
                st.go(v.tensor_tensor(ni, pos[:, cols], pen[:, cols], ALU.add))
                if r:
                    r.compare()
                st.wait()
                st.go(v.tensor_scalar(na, ni, P - 1, 2, ALU.bitwise_and, ALU.arith_shift_left))
                st.go(v.tensor_scalar(nb, ni, 7, GT - 1, ALU.arith_shift_right, ALU.bitwise_and))
                if r:
                    r.count()
                st.wait()
                st.go(v.tensor_tensor(na, na, nb, ALU.bitwise_or))
                one_hot(R_OH0, WIN0, loc0)
                if r:
                    r.carry()
                    r.select()
                st.wait()
                st.go(v.tensor_scalar(nb, ni, 9, 9, ALU.arith_shift_right, ALU.arith_shift_left))
                one_hot(R_OH, WIN, loc)
                if r:
                    r.reduce()
                st.wait()
                st.go(v.tensor_tensor(slot[s], na, nb, ALU.bitwise_or))
                st.go(v.tensor_tensor(recc[s][:, :, R_CNT + 1:R_DST], typ[:, cols].unsqueeze(2)
                                      .broadcast_to([P, CH, TYPES]),
                                      ityp.unsqueeze(1).broadcast_to([P, CH, TYPES]), ALU.is_equal))
                st.go(v.tensor_copy(recc[s][:, :, R_DST:R_END].bitcast(I32), dsti[:, cols].unsqueeze(2)))
                st.wait()
                hold(v)
                v.sem_inc(pr["rec"], 1)
                if r:
                    r.place()

            rank_start = step.c
            hold(v)
            with v.Fori(0, PARTS) as j:
                Rank(0, j, j).whole()
            assert PARTS == 2 * PAIRS

            def chunk_pair(q, jj):
                for s in range(2):
                    part = jj * 2 + s
                    record(q * PAIRS + jj, s, Rank(q + 1, part, (q + 1) * PARTS + part))
            chunk_pair(0, 0)
            with v.Fori(1, PAIRS) as jj:
                chunk_pair(0, jj)
            with v.Fori(1, NQ - 1) as q:
                with v.Fori(0, PAIRS) as jj:
                    chunk_pair(q, jj)
            with v.Fori((NQ - 1) * PAIRS, CHUNKS // 2) as i:
                for s in range(2):
                    record(i, s)
            barrier(v, B_PREP)

            v.memset(accr[:, :], 0.0).then_inc(e0["vstep"], 1)
            for bank in banks[6:8]:
                v.memset(bank[:, :], 0.0).then_inc(e0["vstep"], 1)
            v.wait_ge(e0["vstep"], 3)

            def add0(n, ws, g, k):
                if k == 0:
                    v.wait_ge(e0["seg_psum"], n + GT)
                v.wait_ge(e0["added"], n + (k + 1))
                v.tensor_tensor(acc0[:, bass.ds(ws[k], 1), :], acc0[:, bass.ds(ws[k], 1), :],
                                sum_bank(g)[:, 96 * k:96 * (k + 1)].unsqueeze(1), ALU.add
                                ).then_inc(e0["added"], 1)

            def edges0(it):
                for g in range(RING):
                    n = it * BODY + g * GT
                    for k in range(GT):
                        t = g * GT + k
                        v.wait_ge(e0["pre_psum"], n + (k + 1))
                        if k == 0:
                            v.wait_ge(e0_q[g], it * (16 * GT) + 16 * GT)
                        if not (isinstance(it, int) and g == 0):
                            v.wait_ge(e0["act"], n + (k + 1 - GT))
                        hold(v)
                        v.tensor_tensor(pre[k], banks[2 + k][:, 0:HID], qg[t], ALU.add).then_inc(e0["pre"], 1)
                        if k == 0:
                            if not isinstance(it, int):
                                v.wait_ge(e0_store[g], it * 48)
                            hold(v)
                            v.tensor_copy(index0[g].unsqueeze(2).bitcast(I32), rec[g][:, :, R_DST:R_END].bitcast(I32)
                                          ).then_inc(e0["vstep"], 1)
                        v.wait_ge(e0["T"], n + (k + 1))
                        hold(v)
                        v.tensor_scalar(mk0[g][:, P * k:P * (k + 1)], lh[k][R_OH:R_CNT, :], -1.0, 1.0, ALU.mult,
                                        ALU.add).then_inc(e0["mask"], 1)
                    if not (isinstance(it, int) and g == 0):
                        ws = windows(mybir.EngineType.DVE, n - GT, wtab0, NWIN0)
                        for k in range(GT):
                            add0(n - GT, ws, g - 1, k)
            v.sem_inc(e0["added"], 1)
            bodies(v, edges0)
            ws = windows(mybir.EngineType.DVE, TILES - GT, wtab0, NWIN0)
            for k in range(GT):
                add0(TILES - GT, ws, RING - 1, k)
            barrier(v, B_E0)

            v.wait_ge(n1["loads"], 80)
            v.tensor_tensor(brz, brz, brzh, ALU.add).then_inc(n1["vstep"], 1)
            v.wait_ge(n1["vstep"], 1)

            def update0(i):
                for s in range(2):
                    b = i * 2 + s
                    st = Steps(v, n1["vstep"], b, 7, 1)
                    v.wait_ge(n1["gate_psum"], b + 1)
                    hold(v)
                    v.tensor_tensor(rz[s], banks[2 + s][:, :], brz, ALU.add).then_inc(n1["rz_pre"], 1)
                    st(v.tensor_tensor(gt, banks[4 + s][:, 256:512], bhn, ALU.add))
                    v.wait_ge(n1["rz"], b + 1)
                    st(v.tensor_tensor(gt, gt, rz[s][:, 0:256], ALU.mult))
                    st(v.tensor_tensor(gt, gt, banks[4 + s][:, 0:256], ALU.add))
                    v.tensor_tensor(cand[s], gt, bxn, ALU.add).then_inc(n1["n_pre"], 1)
                    v.wait_ge(n1["n"], b + 1)
                    v.wait_ge(n1_in[s], i * 32 + 32)
                    st(v.tensor_tensor(gt, gh[s], cand[s], ALU.subtract))
                    st(v.tensor_tensor(gt, gt, rz[s][:, 256:512], ALU.mult))
                    st(v.tensor_tensor(gt, gt, cand[s], ALU.add))
                    need(v, n1_out[s], i, 0, i * 16)
                    hold(v)
                    v.tensor_tensor(newx[s], gt, gx[s], ALU.add).then_inc(n1["x1"], 1)
                    v.wait_ge(n1["x1"], b + 1)
                    st(v.bn_stats(bst[:, bass.ds(b, 1), :].rearrange("p a c -> p (a c)"), newx[s]))
                    st.end()
            pairs(v, update0)
            stats_v(Steps(v, n1["vstep"], 0, 0, 1 + 7 * BLOCKS), pr["var"], pr["root"], 2)
            barrier(v, B_N1)

            v.wait_ge(n2["loads"], 32)

            def entry(i):
                for s in range(2):
                    b = i * 2 + s
                    v.wait_ge(n2["h"], b + 1)
                    need(v, n2_out[s], i, 0, i * 32)
                    hold(v)
                    v.tensor_tensor(ibase[s], ix[s], ih[s], ALU.add).then_inc(n2["base"], 1)
                    v.wait_ge(n2["hid_psum"], b + 1)
                    hold(v)
                    v.tensor_tensor(ihid[s], banks[2 + s][:, 0:HID], ib, ALU.add).then_inc(n2["hid"], 1)
            pairs(v, entry)
            barrier(v, B_N2)

            v.sem_inc(e1["added"], 1)
            with v.Fori(0, LAYERS) as l:
                v.wait_ge(pa["loads"], l * 64 + 64)
                hold(v)

                def project(i):
                    for s in range(2):
                        b, n = i * 2 + s, l * BLOCKS + i * 2
                        v.wait_ge(pa["q_psum"], n + (s + 1))
                        hold(v)
                        q = banks[2 + s][:, :].rearrange("p (h w n) -> p w h n", h=HEADS, w=WPB)
                        bias = bq.unsqueeze(1).unsqueeze(3).broadcast_to([P, WPB, HEADS, WIN])
                        for z in range(2):
                            ps = slice(64 * z, 64 * z + 64)
                            v.tensor_tensor(QT[ps, bass.ds(b * WPB, WPB), z, :, :], q[ps], bias[ps], ALU.add
                                            ).then_inc(pa["q"], 1)
                        v.wait_ge(pa["kv_psum"], n + (s + 1))
                        if not isinstance(i, int):
                            v.wait_ge(pa_out[s], (l * HALF + i) * 16)
                        hold(v)
                        v.tensor_tensor(akv[s], banks[4 + s][:, :], bkv, ALU.add).then_inc(pa["kv"], 1)
                pairs(v, project)
                layer_barrier(v, l, 1)

                def softmax_tail(n, groups):
                    v.wait_ge(e1["exp"], l * GROUPS + groups)
                    hold(v)
                    st = Steps(v, e1["vgroup"], l * GROUPS + (groups - 1), 3)
                    st(v.tensor_reduce(sm, ex.rearrange("p k (g h) -> p k h g", g=HEADS), AX.X, ALU.add))
                    st(v.reciprocal(smf, smf))
                    st(v.tensor_tensor(att.rearrange("p k (g h) -> p k g h", g=HEADS),
                                       ex.rearrange("p k (g h) -> p k g h", g=HEADS),
                                       sm.unsqueeze(2).broadcast_to([P, GT, HEADS, HEADS]), ALU.mult))

                def spread(n, g, k, earlier=True):
                    if earlier:
                        v.wait_ge(e1["o_psum"], n + (k + 1 - 2 * GT))
                    v.tensor_tensor(A[:, k, :, :], att[:, k, :].unsqueeze(2).broadcast_to([P, 16, WIN]),
                                    pk[g][:, k, 0:WIN].unsqueeze(1).broadcast_to([P, 16, WIN]), ALU.mult
                                    ).then_inc(e1["a"], 1)

                v.memset(node[0:DH, 0:E], 0.0).then_inc(e1["cleared"], 1)

                def add1(n, ws, g, k):
                    if k == 0:
                        v.wait_ge(e1["o_psum"], n + GT)
                    v.wait_ge(e1["added"], n + (k + 1))
                    v.tensor_tensor(acc1[:, bass.ds(ws[k], 1), :], acc1[:, bass.ds(ws[k], 1), :],
                                    sum_bank(g)[0:DH, DH * k:DH * (k + 1)].unsqueeze(1), ALU.add
                                    ).then_inc(e1["added"], 1)

                def edges1(it):
                    for g in range(RING):
                        t = it * BODY + g * GT
                        n = l * TILES + t
                        first = isinstance(it, int) and g == 0
                        if not first:
                            softmax_tail(n, it * RING + g)
                            second = isinstance(it, int) and g == 1
                            for k in range(GT):
                                spread(n, (g - 1) % RING, k, not second)
                            if not second:
                                ws = windows(mybir.EngineType.DVE, t - 2 * GT, wtab, NWIN)
                        v.wait_ge(e1_in[g], (l * ITERS + it) * 32 + 32)
                        hold(v)
                        for k in range(GT):
                            v.wait_ge(e1["s_psum"], n + (k + 1))
                            v.tensor_reduce(sc[:, k, :], banks[2 + k][:, 0:16 * WIN].rearrange("p (c n) -> p c n", n=WIN),
                                            AX.X, ALU.max).then_inc(e1["s_read"], 1)
                            if not (first or second):
                                add1(n - 2 * GT, ws, g, k)
                        v.wait_ge(e1["s_read"], n + GT)
                        v.tensor_reduce(mx, sc.rearrange("p k (g h) -> p k h g", g=HEADS), AX.X, ALU.max
                                        ).then_inc(e1["vstep"], 1)
                        v.wait_ge(e1["vstep"], l * GROUPS + it * RING + (g + 1))
                        v.tensor_tensor(ex.rearrange("p k (g h) -> p k g h", g=HEADS),
                                        sc.rearrange("p k (g h) -> p k g h", g=HEADS),
                                        mx.unsqueeze(2).broadcast_to([P, GT, HEADS, HEADS]), ALU.subtract
                                        ).then_inc(e1["shifted"], 1)
                v.wait_ge(e1["cleared"], l + 1)
                hold(v)
                bodies(v, edges1)
                softmax_tail(l * TILES + TILES, GROUPS)
                for k in range(GT):
                    spread(l * TILES + TILES, RING - 1, k)
                for g in (RING - 2, RING - 1):
                    t = TILES + (g - RING) * GT
                    ws = windows(mybir.EngineType.DVE, t, wtab, NWIN)
                    for k in range(GT):
                        add1(l * TILES + t, ws, g, k)
                layer_barrier(v, l, 2)

                def output(i):
                    for s in range(2):
                        b, n = i * 2 + s, l * BLOCKS + i * 2
                        v.wait_ge(pb["m_psum"], n + (s + 1))
                        v.wait_ge(pb_in[s], (l * HALF + i) * 32 + 32)
                        if not isinstance(i, int):
                            v.wait_ge(pb_out[s], (l * HALF + i) * 16)
                        hold(v)
                        v.tensor_tensor(cy[s], banks[2 + s][:, 0:HID], ch[s], ALU.add).then_inc(pb["y"], 1)
                        v.wait_ge(pb["y"], n + (s + 1))
                        v.bn_stats(bst[:, bass.ds(b, 1), :].rearrange("p a c -> p (a c)"), cy[s]
                                   ).then_inc(pb["vstep"], 1)
                pairs(v, output)
                v.wait_ge(pb["vstep"], l * BLOCKS + BLOCKS)
                hold(v)
                stats_v(Steps(v, pb["vstat"], l, STAT_STEPS), pb["var"], pb["root"], l + 1)
                layer_barrier(v, l, 3)

                v.wait_ge(pc["loads"], l * 32 + 32)
                hold(v)

                def norm(i):
                    for s in range(2):
                        n = l * BLOCKS + i * 2
                        st = Steps(v, pc["vstep"], n + s, 1)
                        v.wait_ge(pc["t"], n + (s + 1))
                        if not isinstance(i, int):
                            v.wait_ge(pc_out[s], (l * HALF + i) * 16)
                        hold(v)
                        v.tensor_tensor(du[s], dt[s], lng, ALU.mult).then_inc(pc["u"], 1)
                        v.wait_ge(pc["u"], n + (s + 1))
                        st(v.tensor_tensor(du[s], du[s], lnb, ALU.add))
                        v.tensor_scalar(du[s], du[s], 0.0, None, ALU.max).then_inc(pc["o"], 1)
                pairs(v, norm)
                layer_barrier(v, l, 4)

            v.wait_ge(pf["loads"], 64)

            def last(i):
                for s in range(2):
                    b = i * 2 + s
                    st = Steps(v, pf["vstep"], b, 1)
                    v.wait_ge(pf["o_psum"], b + 1)
                    v.wait_ge(pf_in[s], i * 32 + 32)
                    need(v, pf_out[s], i, 0, i * 16)
                    hold(v)
                    st(v.tensor_tensor(fo[s], banks[4 + s][:, 0:HID], fbase[s], ALU.add))
                    v.tensor_tensor(fo[s], fo[s], fb2, ALU.add).then_inc(pf["o"], 1)
            pairs(v, last)

        @block.tensor
        def _(pe):
            mm = nc.tensor.matmul

            pe.wait_ge(pr["consts"], 1)
            pe.wait_ge(pr["tile_base"], 1)
            mm(banks[4][:, 0:NWIN], before[:, :], cnt, start=True, stop=True)
            mm(banks[4][:, 256:256 + NWIN], ones[:, :], cnt, start=True, stop=True).then_inc(pr["pre_psum"], 1)
            pe.wait_ge(pr["tile_base"], 2)
            for z in range(2):
                t = nc.tensor.transpose(banks[5][0:NWIN // 2, P * z:P * (z + 1)],
                                        tbi[:, NWIN // 2 * z:NWIN // 2 * (z + 1)], ident[:, :])
            t.then_inc(pr["base_psum"], 1)
            pe.wait_ge(pr["below"], 2)
            for half in range(2):
                for z in range(2):
                    t = mm(banks[6 + half][:, 0:TH], ones[0:NWIN // 2, :], lemat[z][:, half * TH:(half + 1) * TH],
                           start=z == 0, stop=z == 1)
            t.then_inc(pr["win_psum"], 1)
            pe.wait_ge(pr["weights"], 144)

            def nodes0(i):
                for s in range(2):
                    b = i * 2 + s
                    pe.wait_ge(n0["h"], b + 1)
                    for k in range(2):
                        t = nc.tensor.transpose(banks[s][:, P * k:P * (k + 1)], hb[s][:, P * k:P * (k + 1)],
                                                ident[:, :])
                    t.then_inc(n0["hT_psum"], 1)
                    pe.wait_ge(n0["hT"], b + 1)
                    if not isinstance(i, int):
                        pe.wait_ge(n0["pq"], (i * 2 + (s - 1)) * 5)
                    mm(banks[2 + s][:, :], hT[s][:, 0, :], wpq[:, 0, :], start=True, stop=False)
                    mm(banks[2 + s][:, :], hT[s][:, 1, :], wpq[:, 1, :], start=False, stop=False)
                    mm(banks[2 + s][:, :], ones[0:1, :], b1row, start=False, stop=True).then_inc(n0["pq_psum"], 1)
            pairs(pe, nodes0)
            barrier(pe, B_PREP)

            def need_sums(added, n):
                pe.wait_ge(added, 1 if isinstance(n, int) and n <= GT else n + (1 - GT))

            def trans0(it, g, k):
                n = it * BODY + g * GT
                if k == 0:
                    pe.wait_ge(e0_rec[g], it * 16 + 16)
                if not (isinstance(it, int) and it == 0 and g == 0 and k < 2):
                    pe.wait_ge(e0["T"], n + (k - 1))
                nc.tensor.transpose(banks[k % 2][0:R_CNT, 0:P], rec[g][:, k, 0:R_CNT], ident[:, :]
                                    ).then_inc(e0["T_psum"], 1)

            def pre0(it, g, k, w):
                n = it * BODY + g * GT
                pe.wait_ge(e0["T"], n + (k + 1))
                if not (isinstance(it, int) and it == 0 and g == 0):
                    pe.wait_ge(e0["pre"], n + (k + 1 - GT))
                mm(banks[2 + k][:, 0:HID], lh[k][0:R_OH, :], big[0:R_OH, bass.ds(w, 1), :].rearrange("p a n -> p (a n)"),
                   start=True, stop=True).then_inc(e0["pre_psum"], 1)

            def sums0(n, g):
                for k in range(GT):
                    pe.wait_ge(e0["act"], n + (k + 1))
                    if k == 0:
                        need_sums(e0["added"], n)
                    onehot = rec[g][:, k, R_OH0:R_OH]
                    sums = sum_bank(g)[:, 96 * k:96 * (k + 1)]
                    for f in range(2):
                        mm(sums[:, WIN0 * f:WIN0 * (f + 1)], act[k][:, P * f:P * (f + 1)], onehot, start=True,
                           stop=True)
                    mm(sums[0:4, 64:96], rec[g][:, k, R_CNT:R_DST], onehot, start=True, stop=True).then_inc(e0["seg_psum"], 1)

            def edges0(it, more=True):
                for g in range(RING):
                    ws = windows(mybir.EngineType.PE, it * BODY + g * GT, wtab0, NWIN0)
                    for k in range(GT):
                        if k < 2:
                            trans0(it, g, k + 2)
                        elif g < RING - 1:
                            trans0(it, g + 1, k - 2)
                        elif more:
                            trans0(it + 1, 0, k - 2)
                        pre0(it, g, k, ws[k])
                        if k == 1 and not (isinstance(it, int) and it == 0 and g == 0):
                            sums0(it * BODY + (g - 1) * GT, (g - 1) % RING)
            trans0(0, 0, 0)
            trans0(0, 0, 1)
            edges0(0)
            with pe.Fori(1, ITERS - 1) as it:
                edges0(it)
            edges0(ITERS - 1, more=False)
            sums0(TILES - GT, RING - 1)
            barrier(pe, B_E0)

            def aggregate(i, s):
                b = i * 2 + s
                need(pe, n1["aggT"], i, i * 2, s - 1)
                for f in range(2):
                    dst, fs = banks[s][:, P * f:P * (f + 1)], slice(P * f, P * (f + 1))
                    for j in range(2):
                        mm(dst, w2l0[:, j, fs], acc0[:, bass.ds(b * WPB0, WPB0), 32 * j:32 * (j + 1)],
                           start=j == 0, stop=False)
                    t = mm(dst, b2x[:, fs], acc0[:, bass.ds(b * WPB0, WPB0), 64:96], start=False, stop=True)
                t.then_inc(n1["agg_psum"], 1)

            def gates(i, s):
                pe.wait_ge(n1["aggT"], i * 2 + (s + 1))
                pe.wait_ge(n1_hT[s], i * 16 + 16)
                need(pe, n1["n_pre"], i, i * 2, s - 1)
                for j, (src, w) in enumerate(((aggT[s], 0), (aggT[s], 1), (ghT[s], 2), (ghT[s], 3))):
                    mm(banks[2 + s][:, :], src[:, j % 2, :], wgate[:, w, 0:512], start=j == 0, stop=j == 3)
                for part in range(2):
                    src = (aggT, ghT)[part][s]
                    for j in range(2):
                        t = mm(banks[4 + s][:, 256 * part:256 * (part + 1)], src[:, j, :],
                               wgate[:, 2 * part + j, 512:768], start=j == 0, stop=j == 1)
                t.then_inc(n1["gate_psum"], 1)
            ahead(pe, aggregate, gates)
            barrier(pe, B_N1)

            pe.wait_ge(n2["loads"], 32)

            def entry(i):
                for s in range(2):
                    b = i * 2 + s
                    pe.wait_ge(n2["h"], b + 1)
                    need(pe, n2["hT"], i, i * 2, s - 1)
                    for k in range(2):
                        t = nc.tensor.transpose(banks[s][:, P * k:P * (k + 1)], ih[s][:, P * k:P * (k + 1)],
                                                ident[:, :])
                    t.then_inc(n2["hT_psum"], 1)
                    pe.wait_ge(n2["hT"], b + 1)
                    need(pe, n2["hid"], i, i * 2, s - 1)
                    mm(banks[2 + s][:, 0:HID], ihT[s][:, 0, :], iw[:, 0, :], start=True, stop=False)
                    mm(banks[2 + s][:, 0:HID], ihT[s][:, 1, :], iw[:, 1, :], start=False, stop=True
                       ).then_inc(n2["hid_psum"], 1)
            pairs(pe, entry)
            barrier(pe, B_N2)

            with pe.Fori(0, LAYERS) as l:
                pe.wait_ge(pa["loads"], l * 64 + 64)
                hold(pe)

                def transposed(i, s):
                    pe.wait_ge(pa_in[s], (l * HALF + i) * 16 + 16)
                    need(pe, pa["hT"], i, l * BLOCKS + i * 2, s - 1)
                    for k in range(2):
                        t = nc.tensor.transpose(banks[s][:, P * k:P * (k + 1)], ah[s][:, P * k:P * (k + 1)],
                                                ident[:, :])
                    t.then_inc(pa["hT_psum"], 1)

                def project(i, s):
                    n = l * BLOCKS + i * 2
                    pe.wait_ge(pa["hT"], n + (s + 1))
                    if not (isinstance(i, int) and i == 0):
                        pe.wait_ge(pa["q"], (n + (s - 1)) * 2)
                    for h in range(HEADS):
                        for k in range(2):
                            t = mm(banks[2 + s][:, P * h:P * (h + 1)], wq[:, k, h, :], ahT[s][:, k, :],
                                   start=k == 0, stop=k == 1)
                    t.then_inc(pa["q_psum"], 1)
                    need(pe, pa["kv"], i, n, s - 1)
                    for k in range(2):
                        t = mm(banks[4 + s][:, :], ahT[s][:, k, :], wkv[:, k, :], start=k == 0, stop=k == 1)
                    t.then_inc(pa["kv_psum"], 1)
                ahead(pe, transposed, project)
                layer_barrier(pe, l, 1)

                def trans1(it, g, k):
                    n = l * TILES + it * BODY + g * GT
                    if k == 0:
                        pe.wait_ge(e1_kv[g], (l * ITERS + it + 1) * (16 * GT))
                    if not (isinstance(it, int) and it == 0 and g == 0 and k < 2):
                        pe.wait_ge(e1["T"], n + (k - 1))
                    for j in range(2):
                        t = nc.tensor.transpose(banks[k % 2][:, P * j:P * (j + 1)],
                                                kv[g * GT + k][:, P * j:P * (j + 1)], ident[:, :])
                    t.then_inc(e1["T_psum"], 1)

                def scores(it, g, k, w):
                    n = l * TILES + it * BODY + g * GT
                    if k == 0:
                        pe.wait_ge(e1_in[g], (l * ITERS + it) * 32 + 32)
                    if not (isinstance(it, int) and it == 0 and g == 0):
                        pe.wait_ge(e1["s_read"], n + (k + 1 - GT))
                    pe.wait_ge(e1["T"], n + (k + 1))
                    hold(pe)
                    mm(banks[2 + k][:, 0:16 * WIN], mk[g][:, P * k:P * (k + 1)], neg[:, :], start=True, stop=False)
                    q = QW[:, bass.ds(w, 1), :].rearrange("p a n -> p (a n)")
                    for j in range(2):
                        m = mm(banks[2 + k][:, 8 * WIN * j:8 * WIN * (j + 1)], kT[k][:, P * j:P * (j + 1)], q,
                               start=False, stop=j == 1)
                    m.then_inc(e1["s_psum"], 1)

                def messages(t, g):
                    n = l * TILES + t
                    for k in range(GT):
                        pe.wait_ge(e1["a"], n + (k + 1))
                        if k == 0 and not (isinstance(t, int) and t <= GT):
                            pe.wait_ge(e1["added"], n + (1 - GT))
                        for j in range(HEADS):
                            m = mm(sum_bank(g)[0:DH, DH * k:DH * (k + 1)],
                                   kv[g * GT + k][:, HID + DH * j:HID + DH * (j + 1)],
                                   A[:, k, HEADS * j:HEADS * (j + 1), :].rearrange("p h n -> p (h n)"),
                                   start=j == 0, stop=j == HEADS - 1)
                        m.then_inc(e1["o_psum"], 1)

                def edges1(it, more=True):
                    for g in range(RING):
                        ws = windows(mybir.EngineType.PE, it * BODY + g * GT, wtab, NWIN)
                        for k in range(GT):
                            if k < 2:
                                trans1(it, g, k + 2)
                            elif g < RING - 1:
                                trans1(it, g + 1, k - 2)
                            elif more:
                                trans1(it + 1, 0, k - 2)
                            scores(it, g, k, ws[k])
                        if not (isinstance(it, int) and it == 0 and g == 0):
                            messages(it * BODY + (g - 1) * GT, (g - 1) % RING)
                trans1(0, 0, 0)
                trans1(0, 0, 1)
                edges1(0)
                with pe.Fori(1, ITERS - 1) as it:
                    edges1(it)
                edges1(ITERS - 1, more=False)
                messages(TILES - GT, RING - 1)
                layer_barrier(pe, l, 2)

                pe.wait_ge(pb["loads"], l * 48 + 48)
                hold(pe)
                for h in range(HEADS):
                    mm(banks[7][0:4, 0:HID], eeT[:, h, :], wo[:, h, :], start=h == 0, stop=False)
                mm(banks[7][0:4, 0:HID], ident[0:1, 0:4], borow, start=False, stop=True).then_inc(pb["eb_psum"], 1)
                pe.wait_ge(pb["eb"], l + 1)
                hold(pe)

                def output(i):
                    for s in range(2):
                        n = l * BLOCKS + i * 2
                        pe.wait_ge(pb["staged"], n + (s + 1))
                        pe.wait_ge(pb_in[s], (l * HALF + i) * 32 + 32)
                        need(pe, pb["y"], i, n, s - 1)
                        hold(pe)
                        for h in range(HEADS):
                            mm(banks[2 + s][:, 0:HID], cst[s][:, h, :], wo[:, h, :], start=h == 0, stop=False)
                        mm(banks[2 + s][:, 0:HID], cc[s], eb, start=False, stop=True).then_inc(pb["m_psum"], 1)
                pairs(pe, output)
                layer_barrier(pe, l, 3)
                layer_barrier(pe, l, 4)

            pe.wait_ge(pf["loads"], 64)

            def last(i):
                for s in range(2):
                    b = i * 2 + s
                    pe.wait_ge(pf_in[s], i * 32 + 32)
                    need(pe, pf["hT"], i, i * 2, s - 1)
                    for k in range(2):
                        t = nc.tensor.transpose(banks[s][:, P * k:P * (k + 1)], fh[s][:, P * k:P * (k + 1)],
                                                ident[:, :])
                    t.then_inc(pf["hT_psum"], 1)
                    pe.wait_ge(pf["hT"], b + 1)
                    for f in range(2):
                        for k in range(2):
                            t = mm(banks[2 + s][:, P * f:P * (f + 1)], fw1[:, k, P * f:P * (f + 1)], fhT[s][:, k, :],
                                   start=k == 0, stop=k == 1)
                    t.then_inc(pf["u_psum"], 1)
                    pe.wait_ge(pf["u"], (b + 1) * 2)
                    need(pe, pf["o"], i, i * 2, s - 1)
                    for k in range(2):
                        t = mm(banks[4 + s][:, 0:HID], fuT[s][:, k, :], fw2[:, k, :], start=k == 0, stop=k == 1)
                    t.then_inc(pf["o_psum"], 1)
            pairs(pe, last)


def kernel(x, src, dst, edge_attr_64, edge_type_3, L0_gnn_W1, L0_gnn_b1, L0_gnn_W2, L0_gnn_b2, L0_gnn_W_ih,
           L0_gnn_b_ih, L0_gnn_W_hh, L0_gnn_b_hh, L1_gnn_Win, L1_gnn_b_in, L1_gnn_Wq, L1_gnn_bq, L1_gnn_Wk,
           L1_gnn_bk, L1_gnn_Wv, L1_gnn_bv, L1_gnn_Eemb, L1_gnn_Wo, L1_gnn_bo, L1_gnn_ln_g, L1_gnn_ln_b, L1_gnn_W1,
           L1_gnn_b1, L1_gnn_W2, L1_gnn_b2):
    import numpy as np
    import concourse.bacc as bacc
    from concourse.bass_utils import run_bass_kernel_spmd

    def arr(v):
        return np.asarray(v)

    def edge_columns(v, fill):
        return np.concatenate([arr(v), np.full(EPAD - EDGES, fill, np.int32)]).reshape(P, COLS)

    def halves(wT):
        return wT.reshape(2, P, -1).transpose(1, 0, 2)

    def layers_T(w):
        return arr(w).transpose(0, 2, 1)

    W1 = arr(L0_gnn_W1)
    b1_row = np.zeros((1, 512), np.float32)
    b1_row[0, 0:HID] = arr(L0_gnn_b1)
    b2_rows = np.zeros((P, HID), np.float32)
    b2_rows[0] = arr(L0_gnn_b2)
    wqT = layers_T(L1_gnn_Wq).reshape(LAYERS, 2, P, HEADS, DH).transpose(0, 2, 1, 3, 4)
    wkvT = np.concatenate([layers_T(L1_gnn_Wk), layers_T(L1_gnn_Wv)], 2)
    bq = arr(L1_gnn_bq).reshape(LAYERS, HEADS, DH).transpose(0, 2, 1)
    eT = np.zeros((LAYERS, DH, HEADS, 4), np.float32)
    eT[:, :, :, 1:] = arr(L1_gnn_Eemb).reshape(LAYERS, TYPES, HEADS, DH).transpose(0, 3, 2, 1)
    arrays = {
        "x": np.concatenate([arr(x), np.zeros((NPAD - NODES, HID), np.float32)]),
        "src": edge_columns(src, -1), "dst": edge_columns(dst, 0), "typ": edge_columns(edge_type_3, 0),
        "attr": np.concatenate([arr(edge_attr_64), np.zeros((EPAD - EDGES, ATTR), np.float32)]),
        "w_pq": halves(np.concatenate([W1[:, 0:HID].T, W1[:, HID:2 * HID].T], 1)),
        "w1_attr": W1[:, 2 * HID:].T, "b1_row": b1_row,
        "w2_l0": halves(arr(L0_gnn_W2).T), "b2_rows": b2_rows,
        "w_gate": np.concatenate([halves(arr(L0_gnn_W_ih).T), halves(arr(L0_gnn_W_hh).T)], 1),
        "b_ih": arr(L0_gnn_b_ih), "b_hh": arr(L0_gnn_b_hh),
        "w_in": halves(arr(L1_gnn_Win).T), "b_in": arr(L1_gnn_b_in),
        "w_q": np.concatenate([wqT, wqT], 4).reshape(LAYERS * P, -1),
        "b_q": np.concatenate([bq, bq], 1).reshape(LAYERS * P, HEADS),
        "w_kv": wkvT.reshape(LAYERS, 2, P, 512).transpose(0, 2, 1, 3).reshape(LAYERS * P, -1),
        "b_kv": np.concatenate([arr(L1_gnn_bk), arr(L1_gnn_bv)], 1),
        "w_o": layers_T(L1_gnn_Wo).reshape(LAYERS, HEADS, DH, HID).transpose(0, 2, 1, 3).reshape(LAYERS * DH, -1),
        "e_T": eT.reshape(LAYERS * DH, -1), "b_o": arr(L1_gnn_bo),
        "ln_g": arr(L1_gnn_ln_g), "ln_b": arr(L1_gnn_ln_b),
        "w_f1": halves(arr(L1_gnn_W1).T), "b_f1": arr(L1_gnn_b1).reshape(2, P).T,
        "w_f2": halves(arr(L1_gnn_W2).T), "b_f2": arr(L1_gnn_b2),
    }
    arrays = {f"in_{k}": np.ascontiguousarray(v) for k, v in arrays.items()}
    nc = bacc.Bacc("TRN2", target_bir_lowering=False, num_devices=1)
    a = {k[3:]: nc.dram_tensor(k, v.shape, mybir.dt.from_np(v.dtype), kind="ExternalInput").ap()
         for k, v in arrays.items()}
    out = nc.dram_tensor("out", (NPAD, HID), F32, kind="ExternalOutput").ap()
    gnn(nc, a, out)
    r = run_bass_kernel_spmd(nc, [arrays], core_ids=[0])
    return r.results[0]["out"][:NODES]
```
